# Optimizing a Trainium2 kernel written in Bass

```python
import numpy as np
import jax
import jax.numpy as jnp

def _softmax(x, axis=-1):
    return jax.nn.softmax(x, axis=axis)

def _gelu(x):
    return jax.nn.gelu(x, approximate=True)

def _silu(x):
    return jax.nn.silu(x)

def _sigmoid(x):
    return jax.nn.sigmoid(x)

def _layernorm(x, axis=-1, eps=1e-05):
    m = jnp.mean(x, axis=axis, keepdims=True)
    v = jnp.var(x, axis=axis, keepdims=True)
    return (x - m) / jnp.sqrt(v + eps)

def _scatter_add(tgt, idx, src, axis=0):
    return tgt.at[idx].add(src)

def _segment_sum(src, seg, n):
    return jax.ops.segment_sum(src, seg, n)
kernel_name = 'mk_seq_postln_d2_jaxref_r8_bf52e7'

def setup_inputs(seed: int=0):
    np.random.seed(seed)
    _w = jnp.asarray

    def _L0_attn_setup():
        import jax, jax.numpy as jnp
        import numpy as np
        DIM = 128
        N_HEADS = 16
        HEAD_DIM = DIM // N_HEADS
        D_LATENT = 32
        B, T = (1, 512)
        key = jax.random.key(seed)
        ks = jax.random.split(key, 6)
        s = 0.02
        return {'x': jax.random.normal(ks[0], (B, T, DIM), dtype=jnp.float32), 'W_DKV': jax.random.normal(ks[1], (DIM, D_LATENT), dtype=jnp.float32) * s, 'W_UK': jax.random.normal(ks[2], (D_LATENT, DIM), dtype=jnp.float32) * s, 'W_UV': jax.random.normal(ks[3], (D_LATENT, DIM), dtype=jnp.float32) * s, 'W_UQ': jax.random.normal(ks[4], (DIM, DIM), dtype=jnp.float32) * s, 'W_O': jax.random.normal(ks[5], (DIM, DIM), dtype=jnp.float32) * s}
    _L0_attn_in = _L0_attn_setup()

    def _L0_ffn_setup():
        import jax, jax.numpy as jnp
        import numpy as np
        FP8_MAX = 448.0
        key = jax.random.key(seed)
        k_x, k_w, k_b = jax.random.split(key, 3)
        B, S, IN, OUT = (4, 1024, 128, 128)
        x = jax.random.normal(k_x, (B, S, IN), dtype=jnp.float32)
        w_fp32 = jax.random.normal(k_w, (OUT, IN), dtype=jnp.float32)
        weight_fp8 = w_fp32.astype(jnp.float8_e4m3fn).astype(jnp.float32)
        bias = jax.random.normal(k_b, (OUT,), dtype=jnp.float32)
        input_scale = jnp.ones((1,), dtype=jnp.float32)
        weight_scale = jnp.ones((1,), dtype=jnp.float32)
        return {'x': x, 'weight_fp8': weight_fp8, 'bias': bias, 'input_scale': input_scale, 'weight_scale': weight_scale}
    _L0_ffn_in = _L0_ffn_setup()

    def _L1_attn_setup():
        import jax, jax.numpy as jnp
        import numpy as np
        DIM = 128
        DT_RANK = 64
        D_STATE = 16
        B, L = (4, 64)

        def _layer_norm(x, gamma, beta, eps=1e-06):
            mu = jnp.mean(x, axis=-1, keepdims=True)
            var = jnp.mean(jnp.square(x - mu), axis=-1, keepdims=True)
            return (x - mu) * jax.lax.rsqrt(var + eps) * gamma + beta

        def _ssm(u, W_x, b_x, W_dt, b_dt, A_log, Dp):
            r = W_dt.shape[0]
            n = A_log.shape[1]
            A = -jnp.exp(A_log)
            dbc = u @ W_x + b_x
            delta = jax.nn.softplus(dbc[..., :r] @ W_dt + b_dt)
            Bmat = dbc[..., r:r + n]
            Cmat = dbc[..., r + n:]
            dA = jnp.exp(jnp.einsum('bld,dn->bldn', delta, A))
            dBu = jnp.einsum('bld,bln,bld->bldn', delta, Bmat, u)

            def step(h, xs):
                dA_t, dBu_t, C_t = xs
                h = dA_t * h + dBu_t
                y = jnp.einsum('bdn,bn->bd', h, C_t)
                return (h, y)
            h0 = jnp.zeros((u.shape[0], u.shape[2], n), u.dtype)
            _, ys = jax.lax.scan(step, h0, (jnp.swapaxes(dA, 0, 1), jnp.swapaxes(dBu, 0, 1), jnp.swapaxes(Cmat, 0, 1)))
            y = jnp.swapaxes(ys, 0, 1)
            return y + u * Dp
        key = jax.random.key(seed)
        ks = jax.random.split(key, 16)
        s = 0.02
        d, r, n = (DIM, DT_RANK, D_STATE)
        inp = {'inputs': jax.random.normal(ks[0], (B, L, d), jnp.float32), 'gamma': jnp.ones((d,), jnp.float32), 'beta': jnp.zeros((d,), jnp.float32), 'W_proj': jax.random.normal(ks[1], (d, d), jnp.float32) * s, 'b_proj': jnp.zeros((d,), jnp.float32), 'W_fc': jax.random.normal(ks[2], (d, d), jnp.float32) * s, 'b_fc': jnp.zeros((d,), jnp.float32), 'W_bc': jax.random.normal(ks[3], (d, d), jnp.float32) * s, 'b_bc': jnp.zeros((d,), jnp.float32), 'W_x1': jax.random.normal(ks[4], (d, r + 2 * n), jnp.float32) * s, 'b_x1': jnp.zeros((r + 2 * n,), jnp.float32), 'W_dt1': jax.random.normal(ks[5], (r, d), jnp.float32) * s, 'b_dt1': jnp.full((d,), -4.0, jnp.float32), 'A_log1': jnp.log(jnp.broadcast_to(jnp.arange(1, n + 1, dtype=jnp.float32), (d, n))), 'D1': jnp.ones((d,), jnp.float32), 'W_x2': jax.random.normal(ks[6], (d, r + 2 * n), jnp.float32) * s, 'b_x2': jnp.zeros((r + 2 * n,), jnp.float32), 'W_dt2': jax.random.normal(ks[7], (r, d), jnp.float32) * s, 'b_dt2': jnp.full((d,), -4.0, jnp.float32), 'A_log2': jnp.log(jnp.broadcast_to(jnp.arange(1, n + 1, dtype=jnp.float32), (d, n))), 'D2': jnp.ones((d,), jnp.float32)}
        return inp
    _L1_attn_in = _L1_attn_setup()

    def _L1_ffn_setup():
        import jax, jax.numpy as jnp
        import numpy as np
        DIM = 128
        DEPTH = 6
        HEADS = 16
        DIM_HEAD = 64
        WINDOW = 32
        INNER = HEADS * DIM_HEAD
        DIM_INNER = int(DIM * 4 * 2 / 3)
        QK_SCALE = 8.0

        def shift_tokens(t):
            a, s = jnp.split(t, 2, -1)
            s = jnp.pad(s, ((0, 0), (1, 0), (0, 0)))[:, :-1]
            return jnp.concatenate([a, s], -1)

        def l2norm(t):
            return t / jnp.maximum(jnp.linalg.norm(t, axis=-1, keepdims=True), 1e-12)

        def rotate_half(x):
            x1, x2 = jnp.split(x, 2, -1)
            return jnp.concatenate([-x2, x1], -1)

        def rotary_tables(n):
            half = jnp.arange(0, DIM_HEAD, 2, dtype=jnp.float32)
            inv_freq = 1.0 / 10000.0 ** (half / DIM_HEAD)
            t = jnp.arange(n, dtype=jnp.float32)
            freqs = t[:, None] * inv_freq[None, :]
            freqs = jnp.concatenate([freqs, freqs], -1)
            base_scale = (half + 0.4 * DIM_HEAD) / (1.4 * DIM_HEAD)
            power = (t - n // 2) / (WINDOW // 2)
            scale = base_scale[None, :] ** power[:, None]
            scale = jnp.concatenate([scale, scale], -1)
            return (freqs, scale)

        def local_attention(q, k, v):
            b, h, n, d = q.shape
            w = WINDOW
            nw = n // w
            bq = q.reshape(b, h, nw, w, d)
            bk = k.reshape(b, h, nw, w, d)
            bv = v.reshape(b, h, nw, w, d)

            def look(t):
                p = jnp.pad(t, ((0, 0), (0, 0), (1, 0), (0, 0), (0, 0)))
                return jnp.concatenate([p[:, :, :nw], p[:, :, 1:]], axis=3)
            bk2, bv2 = (look(bk), look(bv))
            seq = jnp.arange(n).reshape(nw, w)
            seq_p = jnp.pad(seq, ((1, 0), (0, 0)), constant_values=-1)
            jt = jnp.concatenate([seq_p[:nw], seq_p[1:]], axis=1)
            it = seq[:, :, None]
            jb = jt[:, None, :]
            mask = (it < jb) | (it > jb + w) | (jb == -1)
            sim = jnp.einsum('bhwie,bhwje->bhwij', bq, bk2) * QK_SCALE
            sim = jnp.where(mask, -jnp.finfo(sim.dtype).max, sim)
            attn = jax.nn.softmax(sim, -1)
            out = jnp.einsum('bhwij,bhwje->bhwie', attn, bv2)
            return out.reshape(b, h, n, d)

        def attn_layer(x, Wqkv, qs, ksc, Wo):
            b, n, _ = x.shape
            qkv = x @ Wqkv
            q, k, v = jnp.split(qkv, 3, -1)
            sh = lambda t: t.reshape(b, n, HEADS, DIM_HEAD).transpose(0, 2, 1, 3)
            q, k, v = (sh(q), sh(k), sh(v))
            q = l2norm(q) * qs
            k = l2norm(k) * ksc
            freqs, scale = rotary_tables(n)
            cos, sin = (jnp.cos(freqs), jnp.sin(freqs))
            q = q * cos * scale + rotate_half(q) * sin * scale
            inv = 1.0 / scale
            k = k * cos * inv + rotate_half(k) * sin * inv
            out = local_attention(q, k, v)
            out = out.transpose(0, 2, 1, 3).reshape(b, n, INNER)
            return out @ Wo

        def ffn_layer(x, g, bln, W1, b1, W2, b2):
            mu = x.mean(-1, keepdims=True)
            var = ((x - mu) ** 2).mean(-1, keepdims=True)
            xn = (x - mu) / jnp.sqrt(var + 1e-05) * g + bln
            hg = xn @ W1 + b1
            a, gate = jnp.split(hg, 2, -1)
            return a * jax.nn.gelu(gate, approximate=False) @ W2 + b2
        key = jax.random.key(seed)
        ks = jax.random.split(key, 8)
        B, N = (2, 256)
        init = lambda k, shape: jax.random.normal(k, shape, jnp.float32) * 0.02
        return {'x': jax.random.normal(ks[0], (B, N, DIM), jnp.float32), 'Wqkv': init(ks[1], (DEPTH, DIM, 3 * INNER)), 'q_scale': jnp.ones((DEPTH, DIM_HEAD), jnp.float32), 'k_scale': jnp.ones((DEPTH, DIM_HEAD), jnp.float32), 'Wo': init(ks[2], (DEPTH, INNER, DIM)), 'ln_g': jnp.ones((DEPTH, DIM), jnp.float32), 'ln_b': jnp.zeros((DEPTH, DIM), jnp.float32), 'W1': init(ks[3], (DEPTH, DIM, 2 * DIM_INNER)), 'b1': jnp.zeros((DEPTH, 2 * DIM_INNER), jnp.float32), 'W2': init(ks[4], (DEPTH, DIM_INNER, DIM)), 'b2': jnp.zeros((DEPTH, DIM), jnp.float32)}
    _L1_ffn_in = _L1_ffn_setup()
    _d = {'L0_attn_x': _L0_attn_in['x'], 'L0_attn_W_DKV': _L0_attn_in['W_DKV'], 'L0_attn_W_UK': _L0_attn_in['W_UK'], 'L0_attn_W_UV': _L0_attn_in['W_UV'], 'L0_attn_W_UQ': _L0_attn_in['W_UQ'], 'L0_attn_W_O': _L0_attn_in['W_O'], 'L0_ffn_weight_fp8': _L0_ffn_in['weight_fp8'], 'L0_ffn_bias': _L0_ffn_in['bias'], 'L0_ffn_input_scale': _L0_ffn_in['input_scale'], 'L0_ffn_weight_scale': _L0_ffn_in['weight_scale'], 'L1_attn_gamma': _L1_attn_in['gamma'], 'L1_attn_beta': _L1_attn_in['beta'], 'L1_attn_W_proj': _L1_attn_in['W_proj'], 'L1_attn_b_proj': _L1_attn_in['b_proj'], 'L1_attn_W_fc': _L1_attn_in['W_fc'], 'L1_attn_b_fc': _L1_attn_in['b_fc'], 'L1_attn_W_bc': _L1_attn_in['W_bc'], 'L1_attn_b_bc': _L1_attn_in['b_bc'], 'L1_attn_W_x1': _L1_attn_in['W_x1'], 'L1_attn_b_x1': _L1_attn_in['b_x1'], 'L1_attn_W_dt1': _L1_attn_in['W_dt1'], 'L1_attn_b_dt1': _L1_attn_in['b_dt1'], 'L1_attn_A_log1': _L1_attn_in['A_log1'], 'L1_attn_D1': _L1_attn_in['D1'], 'L1_attn_W_x2': _L1_attn_in['W_x2'], 'L1_attn_b_x2': _L1_attn_in['b_x2'], 'L1_attn_W_dt2': _L1_attn_in['W_dt2'], 'L1_attn_b_dt2': _L1_attn_in['b_dt2'], 'L1_attn_A_log2': _L1_attn_in['A_log2'], 'L1_attn_D2': _L1_attn_in['D2'], 'L1_ffn_Wqkv': _L1_ffn_in['Wqkv'], 'L1_ffn_q_scale': _L1_ffn_in['q_scale'], 'L1_ffn_k_scale': _L1_ffn_in['k_scale'], 'L1_ffn_Wo': _L1_ffn_in['Wo'], 'L1_ffn_ln_g': _L1_ffn_in['ln_g'], 'L1_ffn_ln_b': _L1_ffn_in['ln_b'], 'L1_ffn_W1': _L1_ffn_in['W1'], 'L1_ffn_b1': _L1_ffn_in['b1'], 'L1_ffn_W2': _L1_ffn_in['W2'], 'L1_ffn_b2': _L1_ffn_in['b2']}
    _x0 = _d['L0_attn_x']
    _d['L0_attn_x'] = jax.random.normal(jax.random.fold_in(jax.random.key(seed), 1), (1, 2048, 128), dtype=_x0.dtype)
    del _x0
    return _d

def reference(L0_attn_x, L0_attn_W_DKV, L0_attn_W_UK, L0_attn_W_UV, L0_attn_W_UQ, L0_attn_W_O, L0_ffn_weight_fp8, L0_ffn_bias, L0_ffn_input_scale, L0_ffn_weight_scale, L1_attn_gamma, L1_attn_beta, L1_attn_W_proj, L1_attn_b_proj, L1_attn_W_fc, L1_attn_b_fc, L1_attn_W_bc, L1_attn_b_bc, L1_attn_W_x1, L1_attn_b_x1, L1_attn_W_dt1, L1_attn_b_dt1, L1_attn_A_log1, L1_attn_D1, L1_attn_W_x2, L1_attn_b_x2, L1_attn_W_dt2, L1_attn_b_dt2, L1_attn_A_log2, L1_attn_D2, L1_ffn_Wqkv, L1_ffn_q_scale, L1_ffn_k_scale, L1_ffn_Wo, L1_ffn_ln_g, L1_ffn_ln_b, L1_ffn_W1, L1_ffn_b1, L1_ffn_W2, L1_ffn_b2):

    def _L0_attn_ref(x, W_DKV, W_UK, W_UV, W_UQ, W_O):
        import jax, jax.numpy as jnp
        import numpy as np
        DIM = 128
        N_HEADS = 16
        HEAD_DIM = DIM // N_HEADS
        D_LATENT = 32
        B, T = (1, 512)
        b, t, d = x.shape
        h, hd = (N_HEADS, HEAD_DIM)
        c_kv = x @ W_DKV
        k = (c_kv @ W_UK).reshape(b, t, h, hd)
        v = (c_kv @ W_UV).reshape(b, t, h, hd)
        q = (x @ W_UQ).reshape(b, t, h, hd)
        scale = 1.0 / jnp.sqrt(jnp.asarray(hd, x.dtype))
        scores = jnp.einsum('bqhd,bkhd->bhqk', q, k) * scale
        causal = jnp.tril(jnp.ones((t, t), dtype=bool))
        scores = jnp.where(causal, scores, jnp.asarray(-jnp.inf, scores.dtype))
        probs = jax.nn.softmax(scores, axis=-1)
        ctx = jnp.einsum('bhqk,bkhd->bqhd', probs, v).reshape(b, t, d)
        return ctx @ W_O

    def _L0_ffn_ref(x, weight_fp8, bias, input_scale, weight_scale):
        import jax, jax.numpy as jnp
        import numpy as np
        FP8_MAX = 448.0
        x_q = jnp.clip(x / input_scale, -FP8_MAX, FP8_MAX)
        x_dq = x_q.astype(jnp.float8_e4m3fn).astype(x.dtype) * input_scale
        w_dq = weight_fp8 * weight_scale
        out = jnp.einsum('bsi,oi->bso', x_dq, w_dq) + bias
        return out

    def _L1_attn_ref(inputs, gamma, beta, W_proj, b_proj, W_fc, b_fc, W_bc, b_bc, W_x1, b_x1, W_dt1, b_dt1, A_log1, D1, W_x2, b_x2, W_dt2, b_dt2, A_log2, D2):
        import jax, jax.numpy as jnp
        import numpy as np
        DIM = 128
        DT_RANK = 64
        D_STATE = 16
        B, L = (4, 64)

        def _layer_norm(x, gamma, beta, eps=1e-06):
            mu = jnp.mean(x, axis=-1, keepdims=True)
            var = jnp.mean(jnp.square(x - mu), axis=-1, keepdims=True)
            return (x - mu) * jax.lax.rsqrt(var + eps) * gamma + beta

        def _ssm(u, W_x, b_x, W_dt, b_dt, A_log, Dp):
            r = W_dt.shape[0]
            n = A_log.shape[1]
            A = -jnp.exp(A_log)
            dbc = u @ W_x + b_x
            delta = jax.nn.softplus(dbc[..., :r] @ W_dt + b_dt)
            Bmat = dbc[..., r:r + n]
            Cmat = dbc[..., r + n:]
            dA = jnp.exp(jnp.einsum('bld,dn->bldn', delta, A))
            dBu = jnp.einsum('bld,bln,bld->bldn', delta, Bmat, u)

            def step(h, xs):
                dA_t, dBu_t, C_t = xs
                h = dA_t * h + dBu_t
                y = jnp.einsum('bdn,bn->bd', h, C_t)
                return (h, y)
            h0 = jnp.zeros((u.shape[0], u.shape[2], n), u.dtype)
            _, ys = jax.lax.scan(step, h0, (jnp.swapaxes(dA, 0, 1), jnp.swapaxes(dBu, 0, 1), jnp.swapaxes(Cmat, 0, 1)))
            y = jnp.swapaxes(ys, 0, 1)
            return y + u * Dp
        skip = inputs
        x = _layer_norm(inputs, gamma, beta)
        proj = x @ W_proj + b_proj
        z = jax.nn.silu(proj)
        u1 = jax.nn.softplus(proj @ W_fc + b_fc)
        y1 = _ssm(u1, W_x1, b_x1, W_dt1, b_dt1, A_log1, D1)
        u2 = jax.nn.softplus(proj @ W_bc + b_bc)
        y2 = _ssm(u2, W_x2, b_x2, W_dt2, b_dt2, A_log2, D2)
        return y1 * z + y2 * z + skip

    def _L1_ffn_ref(x, Wqkv, q_scale, k_scale, Wo, ln_g, ln_b, W1, b1, W2, b2):
        import jax, jax.numpy as jnp
        import numpy as np
        DIM = 128
        DEPTH = 6
        HEADS = 16
        DIM_HEAD = 64
        WINDOW = 32
        INNER = HEADS * DIM_HEAD
        DIM_INNER = int(DIM * 4 * 2 / 3)
        QK_SCALE = 8.0

        def shift_tokens(t):
            a, s = jnp.split(t, 2, -1)
            s = jnp.pad(s, ((0, 0), (1, 0), (0, 0)))[:, :-1]
            return jnp.concatenate([a, s], -1)

        def l2norm(t):
            return t / jnp.maximum(jnp.linalg.norm(t, axis=-1, keepdims=True), 1e-12)

        def rotate_half(x):
            x1, x2 = jnp.split(x, 2, -1)
            return jnp.concatenate([-x2, x1], -1)

        def rotary_tables(n):
            half = jnp.arange(0, DIM_HEAD, 2, dtype=jnp.float32)
            inv_freq = 1.0 / 10000.0 ** (half / DIM_HEAD)
            t = jnp.arange(n, dtype=jnp.float32)
            freqs = t[:, None] * inv_freq[None, :]
            freqs = jnp.concatenate([freqs, freqs], -1)
            base_scale = (half + 0.4 * DIM_HEAD) / (1.4 * DIM_HEAD)
            power = (t - n // 2) / (WINDOW // 2)
            scale = base_scale[None, :] ** power[:, None]
            scale = jnp.concatenate([scale, scale], -1)
            return (freqs, scale)

        def local_attention(q, k, v):
            b, h, n, d = q.shape
            w = WINDOW
            nw = n // w
            bq = q.reshape(b, h, nw, w, d)
            bk = k.reshape(b, h, nw, w, d)
            bv = v.reshape(b, h, nw, w, d)

            def look(t):
                p = jnp.pad(t, ((0, 0), (0, 0), (1, 0), (0, 0), (0, 0)))
                return jnp.concatenate([p[:, :, :nw], p[:, :, 1:]], axis=3)
            bk2, bv2 = (look(bk), look(bv))
            seq = jnp.arange(n).reshape(nw, w)
            seq_p = jnp.pad(seq, ((1, 0), (0, 0)), constant_values=-1)
            jt = jnp.concatenate([seq_p[:nw], seq_p[1:]], axis=1)
            it = seq[:, :, None]
            jb = jt[:, None, :]
            mask = (it < jb) | (it > jb + w) | (jb == -1)
            sim = jnp.einsum('bhwie,bhwje->bhwij', bq, bk2) * QK_SCALE
            sim = jnp.where(mask, -jnp.finfo(sim.dtype).max, sim)
            attn = jax.nn.softmax(sim, -1)
            out = jnp.einsum('bhwij,bhwje->bhwie', attn, bv2)
            return out.reshape(b, h, n, d)

        def attn_layer(x, Wqkv, qs, ksc, Wo):
            b, n, _ = x.shape
            qkv = x @ Wqkv
            q, k, v = jnp.split(qkv, 3, -1)
            sh = lambda t: t.reshape(b, n, HEADS, DIM_HEAD).transpose(0, 2, 1, 3)
            q, k, v = (sh(q), sh(k), sh(v))
            q = l2norm(q) * qs
            k = l2norm(k) * ksc
            freqs, scale = rotary_tables(n)
            cos, sin = (jnp.cos(freqs), jnp.sin(freqs))
            q = q * cos * scale + rotate_half(q) * sin * scale
            inv = 1.0 / scale
            k = k * cos * inv + rotate_half(k) * sin * inv
            out = local_attention(q, k, v)
            out = out.transpose(0, 2, 1, 3).reshape(b, n, INNER)
            return out @ Wo

        def ffn_layer(x, g, bln, W1, b1, W2, b2):
            mu = x.mean(-1, keepdims=True)
            var = ((x - mu) ** 2).mean(-1, keepdims=True)
            xn = (x - mu) / jnp.sqrt(var + 1e-05) * g + bln
            hg = xn @ W1 + b1
            a, gate = jnp.split(hg, 2, -1)
            return a * jax.nn.gelu(gate, approximate=False) @ W2 + b2
        for i in range(DEPTH):
            x = attn_layer(shift_tokens(x), Wqkv[i], q_scale[i], k_scale[i], Wo[i]) + x
            x = ffn_layer(shift_tokens(x), ln_g[i], ln_b[i], W1[i], b1[i], W2[i], b2[i]) + x
        return x
    x = L0_attn_x
    x = _layernorm(x + _L0_attn_ref(x, L0_attn_W_DKV, L0_attn_W_UK, L0_attn_W_UV, L0_attn_W_UQ, L0_attn_W_O), axis=-1)
    x = _layernorm(x + _L0_ffn_ref(x, L0_ffn_weight_fp8, L0_ffn_bias, L0_ffn_input_scale, L0_ffn_weight_scale), axis=-1)
    x = _layernorm(x + _L1_attn_ref(x, L1_attn_gamma, L1_attn_beta, L1_attn_W_proj, L1_attn_b_proj, L1_attn_W_fc, L1_attn_b_fc, L1_attn_W_bc, L1_attn_b_bc, L1_attn_W_x1, L1_attn_b_x1, L1_attn_W_dt1, L1_attn_b_dt1, L1_attn_A_log1, L1_attn_D1, L1_attn_W_x2, L1_attn_b_x2, L1_attn_W_dt2, L1_attn_b_dt2, L1_attn_A_log2, L1_attn_D2), axis=-1)
    x = _layernorm(x + _L1_ffn_ref(x, L1_ffn_Wqkv, L1_ffn_q_scale, L1_ffn_k_scale, L1_ffn_Wo, L1_ffn_ln_g, L1_ffn_ln_b, L1_ffn_W1, L1_ffn_b1, L1_ffn_W2, L1_ffn_b2), axis=-1)
    return x

_drawn_inputs = setup_inputs


def setup_inputs(seed=0):
    import zlib

    import numpy as np

    out = dict(_drawn_inputs(seed))
    spreads = {'L1_attn_gamma': (1.0, 0.6),
     'L1_attn_beta': (0.0, 0.8),
     'L1_attn_b_proj': (0.0, 0.1),
     'L1_attn_b_fc': (0.0, 0.8),
     'L1_attn_b_bc': (0.0, 0.8),
     'L1_attn_b_x1': (0.0, 0.8),
     'L1_attn_b_dt1': (-4.0, 0.6),
     'L1_attn_D1': (1.0, 0.6),
     'L1_attn_b_x2': (0.0, 0.8),
     'L1_attn_b_dt2': (-4.0, 0.6),
     'L1_attn_D2': (1.0, 0.6),
     'L1_ffn_q_scale': (1.0, 0.6),
     'L1_ffn_k_scale': (1.0, 0.6),
     'L1_ffn_ln_g': (1.0, 0.6),
     'L1_ffn_ln_b': (0.0, 0.8),
     'L1_ffn_b1': (0.0, 0.8),
     'L1_ffn_b2': (0.0, 0.1)}
    factors = {'L0_attn_W_DKV': 8.0,
     'L0_attn_W_UK': 8.0,
     'L0_attn_W_UV': 8.0,
     'L0_attn_W_UQ': 8.0,
     'L0_attn_W_O': 8.0,
     'L1_attn_W_fc': 8.0,
     'L1_attn_W_bc': 8.0,
     'L1_attn_W_x1': 8.0,
     'L1_attn_W_dt1': 8.0,
     'L1_attn_A_log1': 8.0,
     'L1_attn_W_x2': 8.0,
     'L1_attn_W_dt2': 8.0,
     'L1_attn_A_log2': 8.0,
     'L1_ffn_W1': 3.689,
     'L1_ffn_W2': 3.604}
    for name, (base, spread) in spreads.items():
        noise = np.random.default_rng([zlib.crc32(name.encode()), seed]).standard_normal(out[name].shape)
        drawn = base * np.exp(spread * noise) if base else spread * noise
        out[name] = jnp.asarray(drawn.astype(out[name].dtype))
    for name, factor in factors.items():
        out[name] = (out[name] * factor).astype(out[name].dtype)
    return out
```

```python
from collections import namedtuple
from contextlib import ExitStack

import concourse.bass as bass
from concourse import mybir

ALU = mybir.AluOpType
ACT = mybir.ActivationFunctionType
AX = mybir.AxisListType
F32 = mybir.dt.float32
BF16 = mybir.dt.bfloat16
U32 = mybir.dt.uint32

P = 128
T = 2048
TILES = T // P
CH = 512
CHUNKS = T // CH
BASE = 8


def need(eng, counter, count):
    eng.wait_ge(counter, count + BASE)


def Counters(nc, ctx, prefix, names):
    counters = namedtuple("Semaphores", names)(*[nc.alloc_semaphore(name=prefix + n) for n in names.split()])
    ctx.callback(nc.all_engine_barrier)
    ctx.callback(nc.clear_and_free_semaphores, list(counters))
    return counters


def start_counters(nc, counters):
    with nc.Block() as block:
        @block.sync
        def _(sp):
            for c in counters:
                sp.sem_inc(c, BASE)



LN_NAMES = "ln_mean ln_centered ln_squared ln_var ln_sd ln_rstd ln_done"


def ln_pe(pe, s, c, k, x, mean, var):
    pe.matmul(mean, c.avg[:, :], x, start=True, stop=True).then_inc(s.ln_mean, 1)
    need(pe, s.ln_squared, k + 1)
    pe.matmul(var, c.avg[:, :], c.ln_sq[:, :], start=True, stop=True).then_inc(s.ln_var, 1)


def ln_act(act, s, c, k, var, eps):
    need(act, s.ln_centered, k + 1)
    act.activation(c.ln_sq[:, :], c.ln_cen[:, :], ACT.Square).then_inc(s.ln_squared, 1)
    need(act, s.ln_var, k + 1)
    act.activation(c.ln_sd[:, :], var, ACT.Sqrt, bias=eps).then_inc(s.ln_sd, 1)


def ln_dve(dve, s, c, k, x, mean, out):
    need(dve, s.ln_mean, k + 1)
    dve.tensor_tensor(c.ln_cen[:, :], x, mean, ALU.subtract).then_inc(s.ln_centered, 1)
    need(dve, s.ln_sd, k + 1)
    dve.reciprocal(c.ln_rs[:, :], c.ln_sd[:, :]).then_inc(s.ln_rstd, 1)
    need(dve, s.ln_rstd, k + 1)
    dve.tensor_tensor(out, c.ln_cen[:, :], c.ln_rs[:, :], ALU.mult).then_inc(s.ln_done, 1)


class Common:

    def __init__(self, nc, ctx):
        def sb(name, shape, dt=F32):
            return ctx.enter_context(nc.sbuf_tensor(name, shape, dt))

        self.xa = sb("xa", [P, T + 1])
        self.xb = sb("xb", [P, T + 1])
        self.ident = sb("ident", [P, P])
        self.ident_bf = sb("ident_bf", [P, P], BF16)
        self.avg = sb("avg", [P, P])
        self.eps5 = sb("eps5", [P, 1])
        self.eps6 = sb("eps6", [P, 1])
        self.ln_cen = sb("ln_cen", [P, CH])
        self.ln_sq = sb("ln_sq", [P, CH])
        self.ln_sd = sb("ln_sd", [P, CH])
        self.ln_rs = sb("ln_rs", [P, CH])
        self.ps = ctx.enter_context(nc.psum_tensor("ps", [P, 8, CH], F32))


def load_phase(nc, c, x, ident):
    with ExitStack() as ctx:
        s = Counters(nc, ctx, "ld_", "x ident turned kept const")
        x_tok = ctx.enter_context(nc.sbuf_tensor("x_tok", [P, TILES, P], F32))
        block = ctx.enter_context(nc.Block())

        @block.sync
        def _(sp):
            sp.dma_start(c.ident[:, :], ident).then_inc(s.ident, 16)
            sp.dma_start(x_tok[:, :, :], x[0].rearrange("(t p) f -> p t f", p=P)).then_inc(s.x, 16)

        @block.gpsimd
        def _(pool):
            pool.memset(c.avg[:, :], 1.0 / P)
            pool.memset(c.eps5[:, :], 1e-5)
            pool.memset(c.eps6[:, :], 1e-6)
            pool.memset(c.xa[:, 0:1], 0.0)
            pool.memset(c.xb[:, 0:1], 0.0).then_inc(s.const, 1)

        @block.tensor
        def _(pe):
            pe.wait_ge(s.ident, 16)
            pe.wait_ge(s.x, 16)
            for b in range(CHUNKS):
                for t in range(4 * b, 4 * b + 4):
                    m = pe.transpose(c.ps[:, b, (t % 4) * P:(t % 4 + 1) * P], x_tok[:, t, :], c.ident[:, :])
                m.then_inc(s.turned, 1)

        @block.vector
        def _(dve):
            dve.wait_ge(s.ident, 16)
            dve.tensor_copy(c.ident_bf[:, :], c.ident[:, :])
            for b in range(CHUNKS):
                dve.wait_ge(s.turned, b + 1)
                dve.tensor_copy(c.xa[:, 1 + CH * b:1 + CH * (b + 1)], c.ps[:, b, :]).then_inc(s.kept, 1)



AHEADS = 16
AD = P // AHEADS
LATENT = 32
PAIRS = AHEADS // 2
MROWS = 8
USED = MROWS + 6 * AD
Q_PART = (0, 0, 1, 1, 0, 2)
K_PART = (0, 1, 0, 1, 2, 0)
VW = AD + 1
A_SCALE = AD ** -0.5
UNITS = [4 * (b + 1) for b in range(CHUNKS)]
STEP_UNITS = 2 * sum(UNITS)
STEPS = [(u, b) for u in range(2) for b in range(CHUNKS)]


def units_before(st):
    return sum(UNITS[b] for _, b in STEPS[:st])


def project_phase(nc, c, m, w_dkv, w_uk, w_uv, w_uq, ones_rows, q_stack, k_stack):
    with ExitStack() as ctx:
        def sb(name, shape, dt=F32):
            return ctx.enter_context(nc.sbuf_tensor("ap_" + name, shape, dt))

        WD = sb("WD", [P, LATENT])
        WK = sb("WK", [LATENT, P])
        WV = sb("WV", [LATENT, P])
        WQ = sb("WQ", [P, P])
        CT = sb("CT", [LATENT, T])
        ONES = sb("ONES", [P, 1])
        FILL = sb("FILL", [P, 2, T], BF16)
        PART = sb("PART", [P, 2, 3, T], BF16)
        REST = sb("REST", [P, 2, CH])
        s = Counters(nc, ctx, "ap_", "w ones zeroed filled latent ckept vdone vkept proj first rest second third stored")
        block = ctx.enter_context(nc.Block())

        @block.sync
        def _(sp):
            for dst, src in ((WD, w_dkv), (WK, w_uk), (WV, w_uv), (WQ, w_uq)):
                sp.dma_start(dst[:, :], src).then_inc(s.w, 16)
            sp.dma_start(ONES[:, :], ones_rows).then_inc(s.ones, 16)
            stacks = (q_stack, k_stack)
            for i in range(2):
                sp.wait_ge(s.filled, i + 1)
                sp.dma_start(stacks[i][:, 0:MROWS, :], FILL[:, i, :]).then_inc(s.stored, 16)
            for i, terms in enumerate((Q_PART, K_PART)):
                sp.wait_ge(s.third, 4 * (i + 1))
                for t, part in enumerate(terms):
                    sp.dma_start(stacks[i][:, MROWS + AD * t:MROWS + AD * (t + 1), :],
                                 PART[:, i, part, :]).then_inc(s.stored, 16)
            sp.wait_ge(s.stored, 16 * 14)

        @block.gpsimd
        def _(pool):
            pool.memset(FILL[:, 0, :], 0.0).then_inc(s.filled, 1)
            pool.wait_ge(s.ones, 16)
            pool.wait_ge(s.filled, 1)
            pool.tensor_copy(FILL[:, 1, :], ONES[:, 0:1].to_broadcast([P, T])).then_inc(s.filled, 1)

        @block.tensor
        def _(pe):
            pe.wait_ge(s.w, 64)
            for b in range(CHUNKS):
                pe.matmul(c.ps[0:LATENT, b, :], WD[:, :], c.xa[:, 1 + CH * b:1 + CH * (b + 1)],
                          start=True, stop=True).then_inc(s.latent, 1)
            for i in range(2):
                for b in range(CHUNKS):
                    k = 4 * i + b
                    if k >= 2:
                        pe.wait_ge(s.rest, k - 1)
                    if i == 1:
                        pe.wait_ge(s.ckept, b + 1)
                    w, x = (WQ, c.xa[:, 1 + CH * b:1 + CH * (b + 1)]) if i == 0 else (WK, CT[:, CH * b:CH * (b + 1)])
                    pe.matmul(c.ps[:, 4 + k % 2, :], w[:, :], x, start=True, stop=True).then_inc(s.proj, 1)
            for t in range(TILES):
                if t >= 8:
                    pe.wait_ge(s.vkept, t // 4 - 1)
                mm = pe.matmul(c.ps[:, 6 + (t // 4) % 2, (t % 4) * P:(t % 4 + 1) * P], CT[:, t * P:(t + 1) * P], WV[:, :],
                               start=True, stop=True)
                if t % 4 == 3:
                    mm.then_inc(s.vdone, 1)

        @block.scalar
        def _(act):
            for k in range(8):
                i, b = k // 4, k % 4
                act.wait_ge(s.proj, k + 1)
                act.activation(PART[:, i, 0, CH * b:CH * (b + 1)], c.ps[:, 4 + k % 2, :], ACT.Copy).then_inc(s.first, 1)
                act.wait_ge(s.rest, k + 1)
                act.activation(PART[:, i, 1, CH * b:CH * (b + 1)], REST[:, k % 2, :], ACT.Copy).then_inc(s.second, 1)

        @block.vector
        def _(dve):
            dve.memset(m.va[:, :, :, :], 1.0).then_inc(s.zeroed, 1)
            dve.wait_ge(s.zeroed, 1)
            for b in range(CHUNKS):
                dve.wait_ge(s.latent, b + 1)
                dve.tensor_copy(CT[:, CH * b:CH * (b + 1)], c.ps[0:LATENT, b, :]).then_inc(s.ckept, 1)

            def third(k):
                i, b = k // 4, k % 4
                dve.wait_ge(s.second, k + 1)
                dve.tensor_tensor(PART[:, i, 2, CH * b:CH * (b + 1)], REST[:, k % 2, :],
                                  PART[:, i, 1, CH * b:CH * (b + 1)], ALU.subtract).then_inc(s.third, 1)

            for k in range(8):
                i, b = k // 4, k % 4
                dve.wait_ge(s.first, k + 1)
                if k >= 2:
                    dve.wait_ge(s.third, k - 1)
                dve.tensor_tensor(REST[:, k % 2, :], c.ps[:, 4 + k % 2, :], PART[:, i, 0, CH * b:CH * (b + 1)],
                                  ALU.subtract).then_inc(s.rest, 1)
                if k >= 1:
                    third(k - 1)
            third(7)
            for b in range(CHUNKS):
                dve.wait_ge(s.vdone, b + 1)
                dve.tensor_copy(m.va[:, 4 * b:4 * b + 4, :, 0:AD],
                                c.ps[:, 6 + b % 2, :].rearrange("p (t h e) -> p t h e", t=4, e=AD)).then_inc(s.vkept, 1)


CROWS = 32 + VW
CAUSAL_COUNTERS = ("vs_ready p1_scored p1_maxed m_neg m_a m_b m_c m_d m_turned m_kept s_done exped attended "
                   "ctx_left ctx_turned ctx_sum ctx_done")


def causal_phase(nc, c, m, q_stack, k_stack, mask_qk, mask_kq):
    with ExitStack() as ctx:
        def sb(name, shape, dt=F32):
            return ctx.enter_context(nc.sbuf_tensor("ac_" + name, shape, dt))

        QS = sb("QS", [P, 2, T], BF16)
        KS = sb("KS", [P, 2, T], BF16)
        VS = sb("VS", [P, 2, TILES, 2 * VW])
        MQK = sb("MQK", [P, P], BF16)
        MKQ = sb("MKQ", [P, P], BF16)
        PM = sb("PM", [P, CHUNKS, 4, 2])
        NM = sb("NM", [P, 4, 2])
        NR = sb("NR", [P, 4, 2])
        M3 = sb("M3", [P, 4, P], BF16)
        PT = sb("PT", [P, 2, 2, CH])
        CX = sb("CX", [CROWS, CH])
        LI = sb("LI", [P, 4, 2])
        s = Counters(nc, ctx, "ac_", CAUSAL_COUNTERS)
        start_counters(nc, s)
        d = Counters(nc, ctx, "acd_", "stack0 stack1 masks zero")
        stack = (d.stack0, d.stack1)
        m_bank = c.ps[:, 7, :].bitcast(BF16)
        o_bank = c.ps[:, 7, CH // 2:CH // 2 + 4 * CROWS]
        m3 = M3[:, :, :].rearrange("p t (s r) -> p t s r", s=2)
        block = ctx.enter_context(nc.Block())

        @block.sync
        def _(sp):
            sp.dma_start(MQK[:, :], mask_qk).then_inc(d.masks, 16)
            sp.dma_start(MKQ[:, :], mask_kq).then_inc(d.masks, 16)
            with sp.Fori(0, PAIRS // 2) as it:
                for u in range(2):
                    need(sp, s.ctx_done, it * len(STEPS) + CHUNKS * (u - 1))
                    for dst, src in ((QS, q_stack), (KS, k_stack)):
                        for h in range(2):
                            sp.dma_start(dst[64 * h:64 * h + USED, u, :],
                                         src[bass.ds(it * 4 + 2 * u + h, 1), :, :].rearrange("h r t -> (h r) t"))\
                              .then_inc(stack[u], 16)

        @block.gpsimd
        def _(pool):
            pool.memset(CX[:, :], 0.0)
            pool.memset(M3[:, :, :], 0.0).then_inc(d.zero, 1)
            with pool.Fori(0, PAIRS // 2) as it:
                for u in range(2):
                    need(pool, s.ctx_done, it * len(STEPS) + CHUNKS * (u - 1))
                    pool.tensor_copy(VS[:, u, :, :], m.va[:, :, :, :].rearrange("p t h e -> p t (h e)")
                                     [:, :, bass.ds((it * 2 + u) * (2 * VW), 2 * VW)]).then_inc(s.vs_ready, 1)

        @block.tensor
        def _(pe):
            pe.wait_ge(d.masks, 32)
            pe.wait_ge(d.zero, 1)

            def p1(it, st, n):
                u, b = STEPS[st]
                i, j = n // (b + 1), n % (b + 1)
                last = j == b
                w = (i + 1) * P if last else CH
                q0 = CH * b + P * i
                if n == 0 and b == 0:
                    pe.wait_ge(stack[u], it * 64 + 64)
                need(pe, s.p1_maxed, it * STEP_UNITS + units_before(st) + n)
                for h in range(2):
                    mm = pe.matmul(c.ps[:, 4 + h, 0:w], QS[64 * h:64 * h + USED, u, q0:q0 + P],
                                   KS[64 * h:64 * h + USED, u, CH * j:CH * j + w], start=True, stop=not last)
                if last:
                    for h in range(2):
                        mm = pe.matmul(c.ps[:, 4 + h, w - P:w], c.ident_bf[:, :], MQK[:, :], start=False, stop=True)
                mm.then_inc(s.p1_scored, 1)

            def maxima(it, st):
                need(pe, s.m_d, it * len(STEPS) + st + 1)
                need(pe, s.m_kept, it * len(STEPS) + st)
                for i in range(4):
                    mm = pe.transpose(m_bank[:, i * P:(i + 1) * P], M3[:, i, :], c.ident_bf[:, :])
                mm.then_inc(s.m_turned, 1)

            def s2(it, st, j):
                u, b = STEPS[st]
                n = units_before(st) + j
                q0 = max(0, j - 4 * b) * P
                need(pe, s.exped, it * STEP_UNITS + n - 1)
                if j == 0:
                    need(pe, s.m_kept, it * len(STEPS) + st + 1)
                for h in range(2):
                    mm = pe.matmul(c.ps[:, 2 * (n % 2) + h, q0:CH], KS[64 * h:64 * h + USED, u, P * j:P * (j + 1)],
                                   QS[64 * h:64 * h + USED, u, CH * b + q0:CH * (b + 1)], start=True, stop=j < 4 * b)
                if j >= 4 * b:
                    for h in range(2):
                        mm = pe.matmul(c.ps[:, 2 * (n % 2) + h, q0:q0 + P], c.ident_bf[:, :], MKQ[:, :],
                                       start=False, stop=True)
                mm.then_inc(s.s_done, 1)

            def attend(it, st, j):
                u, b = STEPS[st]
                n = units_before(st) + j
                need(pe, s.exped, it * STEP_UNITS + n + 1)
                if j == 0:
                    need(pe, s.ctx_left, it * len(STEPS) + st)
                    if b == 0:
                        need(pe, s.vs_ready, it * 2 + u + 1)
                q0 = max(0, j - 4 * b) * P
                for h in range(2):
                    mm = pe.matmul(c.ps[32 * h:32 * h + VW, 6, q0:CH], VS[:, u, j, h * VW:(h + 1) * VW],
                                   PT[:, n % 2, h, q0:CH], start=j == 0, stop=j == UNITS[b] - 1,
                                   skip_group_check=True)
                mm.then_inc(s.attended, 1)

            def turn_context(it, st):
                k = it * len(STEPS) + st
                need(pe, s.ctx_left, k + 1)
                need(pe, s.ctx_done, k)
                for i in range(4):
                    mm = pe.matmul(o_bank[:, i * CROWS:(i + 1) * CROWS], CX[:, i * P:(i + 1) * P],
                                   c.ident[0:CROWS, 0:CROWS], start=i == 0, stop=True, skip_group_check=True)
                mm.then_inc(s.ctx_turned, 1)

            with pe.Fori(0, PAIRS // 2) as it:
                for n in range(UNITS[0]):
                    p1(it, 0, n)
                maxima(it, 0)
                for st, (u, b) in enumerate(STEPS):
                    after = UNITS[STEPS[st + 1][1]] if st + 1 < len(STEPS) else 0
                    for n in range(max(UNITS[b], after) + 1):
                        if n < UNITS[b]:
                            s2(it, st, n)
                        if n < after:
                            p1(it, st + 1, n)
                        if 1 <= n <= UNITS[b]:
                            attend(it, st, n - 1)
                    if st >= 1:
                        turn_context(it, st - 1)
                    if after:
                        maxima(it, st + 1)
                turn_context(it, len(STEPS) - 1)

        @block.scalar
        def _(act):
            act.wait_ge(d.zero, 1)

            def leave(it, st):
                k = it * len(STEPS) + st
                need(act, s.attended, it * STEP_UNITS + units_before(st + 1))
                need(act, s.ctx_turned, k)
                for h in range(2):
                    rows = slice(32 * h, 32 * h + VW)
                    mm = act.activation(CX[rows, :], c.ps[rows, 6, :], ACT.Copy)
                mm.then_inc(s.ctx_left, 1)

            with act.Fori(0, PAIRS // 2) as it:
                for st, (u, b) in enumerate(STEPS):
                    for j in range(UNITS[b]):
                        n = units_before(st) + j
                        q0 = max(0, j - 4 * b) * P
                        need(act, s.s_done, it * STEP_UNITS + n + 1)
                        need(act, s.attended, it * STEP_UNITS + n - 1)
                        act.activation(PT[:, n % 2, :, q0:CH], c.ps[:, 2 * (n % 2):2 * (n % 2) + 2, q0:CH], ACT.Exp,
                                       scale=A_SCALE).then_inc(s.exped, 1)
                        if j == 0 and st >= 1:
                            leave(it, st - 1)
                leave(it, len(STEPS) - 1)

        @block.vector
        def _(dve):
            dve.wait_ge(d.zero, 1)

            def p1_max(it, st, n):
                u, b = STEPS[st]
                i, j = n // (b + 1), n % (b + 1)
                w = (i + 1) * P if j == b else CH
                need(dve, s.p1_scored, it * STEP_UNITS + units_before(st) + n + 1)
                dve.tensor_reduce(PM[:, j, i, :], c.ps[:, 4:6, 0:w], AX.X, ALU.max).then_inc(s.p1_maxed, 1)

            def maxima(it, st):
                u, b = STEPS[st]
                k = it * len(STEPS) + st
                need(dve, s.p1_maxed, it * STEP_UNITS + units_before(st + 1))
                dve.tensor_reduce(NM[:, :, :], PM[:, 0:b + 1, :, :].rearrange("p j i s -> p i s j"), AX.X, ALU.max,
                                  negate=True).then_inc(s.m_neg, 1)
                need(dve, s.m_neg, k + 1)
                need(dve, s.m_turned, k)
                dve.tensor_copy(m3[:, :, :, 0], NM[:, :, :]).then_inc(s.m_a, 1)
                need(dve, s.m_a, k + 1)
                dve.tensor_tensor(NR[:, :, :], NM[:, :, :], m3[:, :, :, 0], ALU.subtract).then_inc(s.m_b, 1)
                need(dve, s.m_b, k + 1)
                dve.tensor_copy(m3[:, :, :, 1], NR[:, :, :]).then_inc(s.m_c, 1)
                need(dve, s.m_c, k + 1)
                dve.tensor_tensor(m3[:, :, :, 2], NR[:, :, :], m3[:, :, :, 1], ALU.subtract).then_inc(s.m_d, 1)

            def keep_maxima(it, st):
                u, b = STEPS[st]
                need(dve, s.m_turned, it * len(STEPS) + st + 1)
                for h in range(2):
                    mm = dve.tensor_copy(QS[64 * h:64 * h + 3, u, CH * b:CH * (b + 1)], m_bank[64 * h:64 * h + 3, 0:CH])
                mm.then_inc(s.m_kept, 1)

            def context(it, st):
                u, b = STEPS[st]
                k = it * len(STEPS) + st
                o = o_bank.rearrange("p (i r) -> p i r", r=CROWS)
                need(dve, s.ctx_turned, k + 1)
                dve.reciprocal(LI[:, :, :], o[:, :, AD::32]).then_inc(s.ctx_sum, 1)
                need(dve, s.ctx_sum, k + 1)
                for h in range(2):
                    mm = dve.tensor_tensor(m.ctx[:, 4 * b:4 * b + 4, bass.ds((it * 2 + u) * (2 * AD) + h * AD, AD)],
                                           o[:, :, 32 * h:32 * h + AD], LI[:, :, h:h + 1].to_broadcast([P, 4, AD]), ALU.mult)
                mm.then_inc(s.ctx_done, 1)

            with dve.Fori(0, PAIRS // 2) as it:
                for n in range(UNITS[0]):
                    p1_max(it, 0, n)
                maxima(it, 0)
                keep_maxima(it, 0)
                for st in range(len(STEPS)):
                    if st + 1 < len(STEPS):
                        for n in range(UNITS[STEPS[st + 1][1]]):
                            p1_max(it, st + 1, n)
                        maxima(it, st + 1)
                        keep_maxima(it, st + 1)
                    if st >= 1:
                        context(it, st - 1)
                context(it, len(STEPS) - 1)


POST_COUNTERS = ("ct_turned ct_kept y_done summed scale clipped low bits unit magic rounded w_turned w_kept o_done "
                 "o_kept o_summed " + LN_NAMES)


def quant_phase(nc, c, m, w_o, w8, bias, in_scale, w_scale):
    with ExitStack() as ctx:
        def sb(name, shape, dt=F32):
            return ctx.enter_context(nc.sbuf_tensor("qz_" + name, shape, dt))

        WO = sb("WO", [P, P])
        W8 = sb("W8", [P, P])
        W8T = sb("W8T", [P, P])
        BIAS = sb("BIAS", [P, 1])
        SI = sb("SI", [P, 1])
        SW = sb("SW", [P, 1])
        RSI = sb("RSI", [P, 1])
        SIW = sb("SIW", [P, 1])
        CT = sb("CT", [P, CH])
        Y = sb("Y", [P, CH])
        X1 = sb("X1", [P, CH])
        XQ = sb("XQ", [P, CH])
        UNIT = sb("UNIT", [P, CH])
        s = Counters(nc, ctx, "qz_", POST_COUNTERS)
        start_counters(nc, s)
        d = Counters(nc, ctx, "qzd_", "w")
        mean, var = c.ps[:, 2, :], c.ps[:, 3, :]
        block = ctx.enter_context(nc.Block())

        def xa(b):
            return c.xa[:, 1 + CH * b:1 + CH * (b + 1)]

        @block.sync
        def _(sp):
            for dst, src in ((WO, w_o), (W8, w8), (BIAS, bias.rearrange("(p a) -> p a", a=1)),
                             (SI, in_scale.rearrange("(a b) -> a b", a=1).broadcast_to([P, 1])),
                             (SW, w_scale.rearrange("(a b) -> a b", a=1).broadcast_to([P, 1]))):
                sp.dma_start(dst[:, :], src).then_inc(d.w, 16)

        @block.tensor
        def _(pe):
            pe.wait_ge(d.w, 80)
            pe.transpose(c.ps[:, 5, 0:P], W8[:, :], c.ident[:, :]).then_inc(s.w_turned, 1)
            for b in range(CHUNKS):
                need(pe, s.ct_kept, b)
                for i in range(4):
                    mm = pe.transpose(c.ps[:, 0, i * P:(i + 1) * P], m.ctx[:, 4 * b + i, :], c.ident[:, :])
                mm.then_inc(s.ct_turned, 1)
                need(pe, s.ct_kept, b + 1)
                need(pe, s.summed, b)
                pe.matmul(c.ps[:, 1, :], WO[:, :], CT[:, :], start=True, stop=True).then_inc(s.y_done, 1)
                need(pe, s.summed, b + 1)
                ln_pe(pe, s, c, 2 * b, Y[:, :], mean, var)
                need(pe, s.rounded, b + 1)
                need(pe, s.w_kept, 1)
                pe.matmul(c.ps[:, 4, :], W8T[:, :], XQ[:, :], start=True, stop=True).then_inc(s.o_done, 1)
                need(pe, s.o_summed, b + 1)
                ln_pe(pe, s, c, 2 * b + 1, Y[:, :], mean, var)

        @block.scalar
        def _(act):
            for b in range(CHUNKS):
                need(act, s.ct_turned, b + 1)
                need(act, s.y_done, b)
                act.activation(CT[:, :], c.ps[:, 0, :], ACT.Copy).then_inc(s.ct_kept, 1)
                ln_act(act, s, c, 2 * b, var, c.eps5[:, 0:1])
                ln_act(act, s, c, 2 * b + 1, var, c.eps5[:, 0:1])

        @block.vector
        def _(dve):
            dve.wait_ge(d.w, 80)
            dve.tensor_tensor(SIW[:, :], SI[:, :], SW[:, :], ALU.mult)
            dve.reciprocal(RSI[:, :], SI[:, :]).then_inc(s.scale, 1)
            need(dve, s.scale, 1)
            need(dve, s.w_turned, 1)
            dve.tensor_copy(W8T[:, :], c.ps[:, 5, 0:P]).then_inc(s.w_kept, 1)
            for b in range(CHUNKS):
                need(dve, s.y_done, b + 1)
                dve.tensor_tensor(Y[:, :], c.ps[:, 1, :], xa(b), ALU.add).then_inc(s.summed, 1)
                ln_dve(dve, s, c, 2 * b, Y[:, :], mean, X1[:, :])
                need(dve, s.ln_done, 2 * b + 1)
                need(dve, s.o_done, b)
                dve.tensor_scalar(XQ[:, :], X1[:, :], RSI[:, 0:1], 448.0, ALU.mult, ALU.min).then_inc(s.clipped, 1)
                need(dve, s.clipped, b + 1)
                dve.tensor_scalar(XQ[:, :], XQ[:, :], -448.0, None, ALU.max).then_inc(s.low, 1)
                need(dve, s.low, b + 1)
                dve.tensor_scalar(UNIT[:, :].bitcast(U32), XQ[:, :].bitcast(U32), 0x7F800000, None,
                                  ALU.bitwise_and).then_inc(s.bits, 1)
                need(dve, s.bits, b + 1)
                dve.tensor_scalar(UNIT[:, :], UNIT[:, :], 2.0 ** -6, 1.5 * 2.0 ** 20, ALU.max, ALU.mult).then_inc(s.unit, 1)
                need(dve, s.unit, b + 1)
                dve.tensor_tensor(XQ[:, :], XQ[:, :], UNIT[:, :], ALU.add).then_inc(s.magic, 1)
                need(dve, s.magic, b + 1)
                dve.tensor_tensor(XQ[:, :], XQ[:, :], UNIT[:, :], ALU.subtract).then_inc(s.rounded, 1)
                need(dve, s.o_done, b + 1)
                dve.tensor_scalar(Y[:, :], c.ps[:, 4, :], SIW[:, 0:1], BIAS[:, 0:1], ALU.mult, ALU.add).then_inc(s.o_kept, 1)
                need(dve, s.o_kept, b + 1)
                dve.tensor_tensor(Y[:, :], Y[:, :], X1[:, :], ALU.add).then_inc(s.o_summed, 1)
                ln_dve(dve, s, c, 2 * b + 1, Y[:, :], mean, xa(b))
                need(dve, s.ln_done, 2 * b + 2)


AttentionBuffers = namedtuple("AttentionBuffers", "va ctx")


def attention_and_quant(nc, c, t):
    q_stack = nc.dram_tensor("q_stack", (AHEADS, USED, T), BF16, kind="Internal").ap()
    k_stack = nc.dram_tensor("k_stack", (AHEADS, USED, T), BF16, kind="Internal").ap()
    with ExitStack() as ctx:
        m = AttentionBuffers(va=ctx.enter_context(nc.sbuf_tensor("va", [P, TILES, AHEADS, VW], F32)),
                            ctx=ctx.enter_context(nc.sbuf_tensor("ctx", [P, TILES, P], F32)))
        project_phase(nc, c, m, t["L0_attn_W_DKV"], t["L0_attn_W_UK"], t["L0_attn_W_UV"], t["L0_attn_W_UQ"],
                      t["c_ones_rows"], q_stack, k_stack)
        causal_phase(nc, c, m, q_stack, k_stack, t["c_mask_qk"], t["c_mask_kq"])
        quant_phase(nc, c, m, t["L0_attn_W_O"], t["L0_ffn_weight_fp8"], t["L0_ffn_bias"], t["L0_ffn_input_scale"],
                    t["L0_ffn_weight_scale"])



DT_RANK = 64
STATES = 16
BC = 2 * STATES
UNITS_SSM = 2 * STATES
SSM_COUNTERS = ("affined proj pkept sig_e sig_d sig_r gate vproj vkept vabs vexp vlog soft dtproj dtkept dlproj "
                "bcproj bckept bc_hi bc_rest bc_mid bc_done dx uskip b_done c_done da_done dbu_done scanned carried "
                "hc_done y_acc y_gated total copied " + LN_NAMES)


def ssm_phase(nc, c, x3, t):
    with ExitStack() as ctx:
        def sb(name, shape, dt=F32):
            return ctx.enter_context(nc.sbuf_tensor("sm_" + name, shape, dt))

        WP = sb("WP", [P, P])
        WU = sb("WU", [P, 2, P])
        WX = sb("WX", [P, 2, DT_RANK])
        WBC = sb("WBC", [P, 2, 3 * BC])
        WDT = sb("WDT", [DT_RANK, 2, P])
        VEC = sb("VEC", [P, 9])
        BX = sb("BX", [DT_RANK, 2])
        BBC = sb("BBC", [3 * BC, 2])
        AL = sb("AL", [P, 2, STATES])
        SEL = sb("SEL", [3 * BC, BC, P], BF16)
        XN = sb("XN", [P, CH])
        PJ = sb("PJ", [P, CH])
        SG = sb("SG", [P, CH])
        Z = sb("Z", [P, CH])
        VB = sb("VB", [P, 2, CH])
        VA = sb("VA", [P, 2, CH])
        VL = sb("VL", [P, 2, CH])
        U = sb("U", [P, 2, CH])
        DT = sb("DT", [DT_RANK, 2, CH])
        DL = sb("DL", [P, 2, CH])
        DX = sb("DX", [P, 2, CH])
        BCF = sb("BCF", [3 * BC, 2, CH])
        BCR = sb("BCR", [3 * BC, 2, CH])
        BCM = sb("BCM", [3 * BC, 2, CH], BF16)
        BCS = sb("BCS", [3 * BC, 2, CH], BF16)
        ACC = sb("ACC", [P, CH])
        Y = sb("Y", [P, CH])
        DA = sb("DA", [P, 2, CH])
        DBU = sb("DBU", [P, 2, CH])
        HS = sb("HS", [P, 2, CH])
        HL = sb("HL", [P, UNITS_SSM])
        HC = sb("HC", [P, 2, CH])
        s = Counters(nc, ctx, "sm_", SSM_COUNTERS)
        start_counters(nc, s)
        d = Counters(nc, ctx, "smd_", "w alog a")
        LOADS = 5 + 2 * 14
        B_BANK, C_BANK = (0, 1, 4), (2, 3, 7)
        mean, var = c.ps[:, 5, :], c.ps[:, 6, :]
        pre = (c.ps[:, 4, :], c.ps[:, 7, :])
        block = ctx.enter_context(nc.Block())
        col = lambda a: a.rearrange("(p a) -> p a", a=1)

        @block.sync
        def _(sp):
            loads = [(WP[:, :], t["W_proj"]), (VEC[:, 0:1], col(t["gamma"])), (VEC[:, 1:2], col(t["beta"])),
                     (VEC[:, 2:3], col(t["b_proj"])), (SEL[:, :, :], t["c_select"])]
            for k, (wu, bu) in enumerate((("W_fc", "b_fc"), ("W_bc", "b_bc"))):
                i = str(k + 1)
                loads += [(WU[:, k, :], t[wu]), (VEC[:, 3 + 3 * k:4 + 3 * k], col(t[bu])),
                          (VEC[:, 4 + 3 * k:5 + 3 * k], col(t["b_dt" + i])), (VEC[:, 5 + 3 * k:6 + 3 * k], col(t["D" + i])),
                          (WX[:, k, :], t["W_x" + i][:, 0:DT_RANK]), (WDT[:, k, :], t["W_dt" + i]),
                          (BX[:, k:k + 1], col(t["b_x" + i][0:DT_RANK])), (AL[:, k, :], t["A_log" + i])]
                for r in range(3):
                    loads += [(WBC[:, k, BC * r:BC * (r + 1)], t["W_x" + i][:, DT_RANK:DT_RANK + BC]),
                              (BBC[BC * r:BC * (r + 1), k:k + 1], col(t["b_x" + i][DT_RANK:DT_RANK + BC]))]
            for dst, src in loads:
                sp.dma_start(dst, src).then_inc(d.w, 16)
            assert len(loads) == LOADS

        @block.gpsimd
        def _(pool):
            pool.memset(HL[:, :], 0.0).then_inc(d.a, 1)
            with pool.Fori(0, CHUNKS) as b:
                for i in range(UNITS_SSM):
                    need(pool, s.hc_done, b * UNITS_SSM + i + 1)
                    if i == 0:
                        need(pool, s.uskip, b * 2 + 2)
                        need(pool, s.y_gated, b)
                    need(pool, s.y_acc, b * UNITS_SSM + i)
                    pool.tensor_tensor(Y[:, :], (ACC if i == 0 else Y)[:, :], HC[:, i % 2, :], ALU.add).then_inc(s.y_acc, 1)
                need(pool, s.ln_done, b * 2 + 2)
                pool.tensor_copy(x3[:, bass.ds(b * CH, CH)], c.xa[:, bass.ds(b * CH + 1, CH)]).then_inc(s.copied, 1)

        @block.tensor
        def _(pe):
            pe.wait_ge(d.w, 16 * LOADS)

            def spread(b, i):
                k, n, g = i // STATES, i % STATES, b * UNITS_SSM + i
                if i == 2:
                    need(pe, s.vkept, b * 2 + 2)
                need(pe, s.dbu_done, g - 2)
                pe.matmul(c.ps[:, B_BANK[i % 3], :], SEL[:, n, :], BCS[:, k, :], start=True, stop=True).then_inc(s.b_done, 1)
                need(pe, s.hc_done, g - 2)
                pe.matmul(c.ps[:, C_BANK[i % 3], :], SEL[:, STATES + n, :], BCS[:, k, :], start=True, stop=True).then_inc(s.c_done, 1)

            with pe.Fori(0, CHUNKS) as b:
                x = c.xa[:, bass.ds(b * CH + 1, CH)]
                ln_pe(pe, s, c, b * 2, x, mean, var)
                need(pe, s.affined, b + 1)
                pe.matmul(pre[0], WP[:, :], XN[:, :], start=True, stop=True).then_inc(s.proj, 1)
                need(pe, s.pkept, b + 1)
                for k in range(2):
                    pe.matmul(pre[k], WU[:, k, :], PJ[:, :], start=True, stop=True).then_inc(s.vproj, 1)
                need(pe, s.soft, b * 2 + 1)
                for k, bank in enumerate((mean, var)):
                    pe.matmul(pre[k][0:DT_RANK, :], WX[:, k, :], U[:, k, :], start=True, stop=True).then_inc(s.dtproj, 1)
                    pe.matmul(bank[0:3 * BC, :], WBC[:, k, :], U[:, k, :], start=True, stop=True).then_inc(s.bcproj, 1)
                for k in range(2):
                    need(pe, s.dtkept, b * 2 + k + 1)
                    pe.matmul(pre[k], WDT[:, k, :], DT[:, k, :], start=True, stop=True).then_inc(s.dlproj, 1)
                need(pe, s.bc_done, b + 1)
                for i in range(UNITS_SSM):
                    spread(b, i)
                need(pe, s.total, b + 1)
                ln_pe(pe, s, c, b * 2 + 1, ACC[:, :], mean, var)

        @block.scalar
        def _(act):
            act.wait_ge(d.w, 16 * LOADS)
            act.wait_ge(d.a, 1)
            act.activation(AL[:, :, :], AL[:, :, :], ACT.Exp).then_inc(d.alog, 1)
            act.wait_ge(d.alog, 1)
            act.activation(AL[:, :, :], AL[:, :, :], ACT.Copy, scale=-1.0).then_inc(d.alog, 1)
            act.wait_ge(d.alog, 2)

            with act.Fori(0, CHUNKS) as b:
                ln_act(act, s, c, b * 2, var, c.eps6[:, 0:1])
                need(act, s.proj, b + 1)
                act.activation(PJ[:, :], pre[0], ACT.Identity, bias=VEC[:, 2:3]).then_inc(s.pkept, 1)
                need(act, s.pkept, b + 1)
                act.activation(SG[:, :], PJ[:, :], ACT.Exp, scale=-1.0).then_inc(s.sig_e, 1)
                for i, (ready, bias) in enumerate(((s.vproj, 3), (s.dlproj, 4))):
                    g = b * 2 + i
                    need(act, s.soft, g)
                    for k in range(2):
                        need(act, ready, b * 2 + k + 1)
                        mm = act.activation(VB[:, k, :], pre[k], ACT.Identity, bias=VEC[:, bias + 3 * k:bias + 3 * k + 1])
                    mm.then_inc(s.vkept, 1)
                    need(act, s.vkept, g + 1)
                    act.activation(VA[:, :, :], VB[:, :, :], ACT.Abs).then_inc(s.vabs, 1)
                    need(act, s.vabs, g + 1)
                    act.activation(VL[:, :, :], VA[:, :, :], ACT.Exp, scale=-1.0).then_inc(s.vexp, 1)
                    need(act, s.vexp, g + 1)
                    act.activation(VL[:, :, :], VL[:, :, :], ACT.Ln, bias=1.0).then_inc(s.vlog, 1)
                    if i == 0:
                        for k in range(2):
                            need(act, s.dtproj, b * 2 + k + 1)
                            act.activation(DT[:, k, :], pre[k][0:DT_RANK, :], ACT.Identity, bias=BX[:, k:k + 1]).then_inc(s.dtkept, 1)
                        need(act, s.bc_done, b)
                        for k, bank in enumerate((mean, var)):
                            need(act, s.bcproj, b * 2 + k + 1)
                            mm = act.activation(BCF[:, k, :], bank[0:3 * BC, :], ACT.Identity, bias=BBC[:, k:k + 1])
                        mm.then_inc(s.bckept, 1)
                need(act, s.soft, b * 2 + 2)
                for i in range(UNITS_SSM):
                    k, n, g = i // STATES, i % STATES, b * UNITS_SSM + i
                    need(act, s.scanned, g - 1)
                    act.activation(DA[:, i % 2, :], DL[:, k, :], ACT.Exp, scale=AL[:, k, n:n + 1]).then_inc(s.da_done, 1)
                ln_act(act, s, c, b * 2 + 1, var, c.eps5[:, 0:1])

        @block.vector
        def _(dve):
            dve.wait_ge(d.w, 16 * LOADS)
            dve.wait_ge(d.a, 1)

            def times_b(b, i):
                g = b * UNITS_SSM + i
                need(dve, s.b_done, g + 1)
                need(dve, s.scanned, g - 1)
                dve.tensor_tensor(DBU[:, i % 2, :], c.ps[:, B_BANK[i % 3], :], DX[:, i // STATES, :], ALU.mult).then_inc(s.dbu_done, 1)

            def scan(b, i):
                g = b * UNITS_SSM + i
                need(dve, s.carried, g - 1)
                need(dve, s.hc_done, g - 1)
                need(dve, s.dbu_done, g + 1)
                need(dve, s.da_done, g + 1)
                dve.tensor_tensor_scan(HS[:, i % 2, :], DA[:, i % 2, :], DBU[:, i % 2, :], HL[:, i:i + 1],
                                       ALU.mult, ALU.add).then_inc(s.scanned, 1)

            def times_c(b, i):
                g = b * UNITS_SSM + i
                need(dve, s.scanned, g + 1)
                dve.tensor_copy(HL[:, i:i + 1], HS[:, i % 2, CH - 1:CH]).then_inc(s.carried, 1)
                need(dve, s.c_done, g + 1)
                need(dve, s.y_acc, g - 1)
                dve.tensor_tensor(HC[:, i % 2, :], c.ps[:, C_BANK[i % 3], :], HS[:, i % 2, :], ALU.mult).then_inc(s.hc_done, 1)

            with dve.Fori(0, CHUNKS) as b:
                x = c.xa[:, bass.ds(b * CH + 1, CH)]
                ln_dve(dve, s, c, b * 2, x, mean, XN[:, :])
                need(dve, s.ln_done, b * 2 + 1)
                dve.tensor_scalar(XN[:, :], XN[:, :], VEC[:, 0:1], VEC[:, 1:2], ALU.mult, ALU.add).then_inc(s.affined, 1)
                need(dve, s.vlog, b * 2 + 1)
                dve.scalar_tensor_tensor(U[:, :, :], VB[:, :, :], 0.0, VL[:, :, :], ALU.max, ALU.add).then_inc(s.soft, 1)
                need(dve, s.bckept, b + 1)
                dve.tensor_copy(BCS[:, :, :], BCF[:, :, :]).then_inc(s.bc_hi, 1)
                need(dve, s.bc_hi, b + 1)
                for i in (1, 2):
                    rows = slice(BC * i, BC * (i + 1))
                    mm = dve.tensor_tensor(BCR[rows, :, :], BCF[rows, :, :], BCS[rows, :, :], ALU.subtract)
                mm.then_inc(s.bc_rest, 1)
                need(dve, s.bc_rest, b + 1)
                dve.tensor_copy(BCS[BC:2 * BC, :, :], BCR[BC:2 * BC, :, :])
                dve.tensor_copy(BCM[2 * BC:3 * BC, :, :], BCR[2 * BC:3 * BC, :, :]).then_inc(s.bc_mid, 1)
                need(dve, s.bc_mid, b + 1)
                dve.tensor_tensor(BCS[2 * BC:3 * BC, :, :], BCR[2 * BC:3 * BC, :, :], BCM[2 * BC:3 * BC, :, :],
                                  ALU.subtract).then_inc(s.bc_done, 1)
                need(dve, s.sig_e, b + 1)
                dve.tensor_scalar(SG[:, :], SG[:, :], 1.0, None, ALU.add).then_inc(s.sig_d, 1)
                need(dve, s.sig_d, b + 1)
                dve.reciprocal(SG[:, :], SG[:, :]).then_inc(s.sig_r, 1)
                need(dve, s.sig_r, b + 1)
                dve.tensor_tensor(Z[:, :], SG[:, :], PJ[:, :], ALU.mult).then_inc(s.gate, 1)
                need(dve, s.vlog, b * 2 + 2)
                dve.scalar_tensor_tensor(DL[:, :, :], VB[:, :, :], 0.0, VL[:, :, :], ALU.max, ALU.add).then_inc(s.soft, 1)
                need(dve, s.soft, b * 2 + 2)
                dve.tensor_tensor(DX[:, :, :], DL[:, :, :], U[:, :, :], ALU.mult).then_inc(s.dx, 1)
                need(dve, s.dx, b + 1)
                dve.tensor_scalar(ACC[:, :], U[:, 0, :], VEC[:, 5:6], None, ALU.mult).then_inc(s.uskip, 1)
                need(dve, s.uskip, b * 2 + 1)
                dve.scalar_tensor_tensor(ACC[:, :], U[:, 1, :], VEC[:, 8:9], ACC[:, :], ALU.mult, ALU.add).then_inc(s.uskip, 1)
                for i in range(UNITS_SSM + 2):
                    if i < UNITS_SSM:
                        times_b(b, i)
                    if 1 <= i <= UNITS_SSM:
                        scan(b, i - 1)
                    if i >= 2:
                        times_c(b, i - 2)
                need(dve, s.y_acc, b * UNITS_SSM + UNITS_SSM)
                dve.tensor_tensor(ACC[:, :], Y[:, :], Z[:, :], ALU.mult).then_inc(s.y_gated, 1)
                need(dve, s.y_gated, b + 1)
                dve.scalar_tensor_tensor(ACC[:, :], x, 2.0, ACC[:, :], ALU.mult, ALU.add).then_inc(s.total, 1)
                need(dve, s.total, b + 1)
                ln_dve(dve, s, c, b * 2 + 1, ACC[:, :], mean, x)
                need(dve, s.ln_done, b * 2 + 2)



LAYERS = 6
HEADS = 16
DH = 64
INNER = HEADS * DH
WIN = 32
KEYS = P + WIN
GROUPS = 4
GH = HEADS // GROUPS
GD = GH * DH
HID = 341
HPART = [(0, 128), (128, 128), (256, HID - 256)]
AHEAD = 4

LOCAL_COUNTERS = ("xs_staged tab_ready qk_done v_done squared v_kept summed roped clamped norm_a "
                  "k_scaled kprev turned qk_kept scored maxed biased exped prev_turned p_turned pt_kept "
                  "attended recipd normed o_turned o_kept projected resid shifted affined gelud gate "
                  "val vprev_kept gated down ffn_done " + LN_NAMES)


def local_phase(nc, c, wqkv, q_scale, k_scale, wo, ln_g, ln_b, w1, b1, w2, b2, rope, mask, kfac):
    with ExitStack() as ctx:
        def sb(name, shape, dt=F32):
            return ctx.enter_context(nc.sbuf_tensor("lo_" + name, shape, dt))

        W = sb("W", [P, GROUPS, 3 * GD])
        WO = sb("WO", [P, INNER // P, P])
        W1 = sb("W1", [P, 2 * HID])
        W2 = sb("W2", [P, 3, P])
        B1 = sb("B1", [P, 2, 3])
        VEC = sb("VEC", [P, 3])
        QS = sb("QS", [P, 4 * DH])
        ROPE = sb("ROPE", [P, TILES, 4 * DH])
        TAB = sb("TAB", [P, 4 * DH])
        MASK = sb("MASK", [P, TILES + 1, KEYS], BF16)
        KFAC = sb("KFAC", [P, 1])
        XS = sb("XS", [P, P])
        SQ = sb("SQ", [P, 2, 2 * GD])
        SS = sb("SS", [P, 2, 2 * GH])
        SSM = sb("SSM", [P, 2, 2 * GH])
        MHALF = sb("MHALF", [P, 1])
        A = sb("A", [P, GROUPS, 2 * GH])
        TB = sb("TB", [P, 2, 2 * GD])
        RB = sb("RB", [P, 2, 2 * GD])
        QT = sb("QT", [P, 2, 2, P])
        KT = sb("KT", [P, GROUPS, 2, KEYS])
        V = sb("V", [P, GROUPS, GD])
        VP = sb("VP", [WIN, GROUPS, GD])
        NM = sb("NM", [P, 2, GH])
        NB = sb("NB", [P, 2, GH])
        PR = sb("PR", [P, 2, GH, KEYS])
        RS = sb("RS", [P, 2, GH])
        RI = sb("RI", [P, GH])
        PP = sb("PP", [WIN, 2, GH * WIN])
        PTS = sb("PTS", [P, 2, GH * P])
        ON = sb("ON", [P, GD])
        OTS = sb("OTS", [P, INNER // P, P])
        XS2 = sb("XS2", [P, CH])
        XN = sb("XN", [P, CH])
        GT = sb("GT", [P, 2, CH])
        H = sb("H", [P, 3, CH])

        s = Counters(nc, ctx, "lo_", LOCAL_COUNTERS)
        start_counters(nc, s)
        d = Counters(nc, ctx, "lod_", "const w wo ffn vec qs")
        N_FFN = 6 + 6

        QK_B, T_B, PT_B, O_B = 0, 1, 6, 7

        def s_bank(par):
            return c.ps[:, 2 + 2 * par:4 + 2 * par, 0:2 * KEYS].rearrange("p h (b k) -> p b h k", b=2)

        y_bank = c.ps[:, PT_B, 0:P]
        o_bank = c.ps[:, O_B, 0:GD]
        ot_bank = c.ps[:, O_B, 0:GD].rearrange("p (b t) -> p b t", b=2)
        v_bank = c.ps[:, O_B, GD:2 * GD]
        pt_bank = c.ps[:, PT_B, :]
        mean_bank, var_bank = c.ps[:, PT_B, :], c.ps[:, O_B, :]

        block = ctx.enter_context(nc.Block())

        @block.sync
        def _(sp):
            sp.dma_start(ROPE[:, :, :], rope).then_inc(d.const, 16)
            sp.dma_start(MASK[:, :, :], mask).then_inc(d.const, 16)
            sp.dma_start(KFAC[:, :], kfac).then_inc(d.const, 16)

            def layer(l, first):
                for part, src in enumerate((q_scale, k_scale)):
                    row = src[bass.ds(l, 1), :]
                    if part == 0 and not first:
                        need(sp, s.tab_ready, 16 * l)
                    sp.dma_start(QS[:, part * DH:(part + 1) * DH], row.broadcast_to([P, DH])).then_inc(d.qs, 16)
                    for h in range(2):
                        o = (2 + part) * DH + h * (DH // 2)
                        sp.dma_start(QS[:, o:o + DH // 2],
                                     src[bass.ds(l, 1), (1 - h) * (DH // 2):(2 - h) * (DH // 2)]
                                     .broadcast_to([P, DH // 2])).then_inc(d.qs, 16)
                for g in range(GROUPS):
                    if not first:
                        need(sp, s.v_done, 64 * l - 3 + g)
                    src = wqkv[bass.ds(l, 1), :, :].rearrange("a p (b n) -> p (a b) n", b=3)
                    sp.dma_start(W[:, g, :].rearrange("p (b n) -> p b n", b=3),
                                 src[:, :, GD * g:GD * (g + 1)]).then_inc(d.w, 16)
                if not first:
                    need(sp, s.projected, 16 * l)
                sp.dma_start(WO[:, :, :], wo[bass.ds(l, 1), :, :].rearrange("a (k p) n -> p (a k) n", p=P)).then_inc(d.wo, 16)
                if not first:
                    need(sp, s.ffn_done, 4 * l)
                sp.dma_start(W1[:, :], w1[bass.ds(l, 1), :, :].rearrange("a p n -> (a p) n")).then_inc(d.ffn, 16)
                sp.dma_start(W2[:, 0:2, :], w2[bass.ds(l, 1), 0:256, :].rearrange("a (k p) n -> p (a k) n", p=P)).then_inc(d.ffn, 16)
                sp.dma_start(W2[0:HID - 256, 2, :], w2[bass.ds(l, 1), 256:HID, :].rearrange("a p n -> (a p) n")).then_inc(d.ffn, 16)
                for i, src in enumerate((ln_g, ln_b, b2)):
                    sp.dma_start(VEC[:, i:i + 1], src[bass.ds(l, 1), :].rearrange("a p -> p a")).then_inc(d.ffn, 16)
                for half in range(2):
                    for j, (h0, w) in enumerate(HPART):
                        sp.dma_start(B1[0:w, half, j:j + 1],
                                     b1[bass.ds(l, 1), half * HID + h0:half * HID + h0 + w].rearrange("a p -> p a")).then_inc(d.ffn, 16)

            layer(0, True)
            with sp.Fori(1, LAYERS) as l:
                layer(l, False)

        @block.gpsimd
        def _(pool):
            pool.memset(MHALF[:, :], -0.5)
            pool.memset(VP[:, :, :], 0.0)
            pool.memset(KT[:, :, :, :], 0.0).then_inc(d.vec, 1)
            pool.wait_ge(d.const, 48)
            pool.wait_ge(d.vec, 1)

            def tile(l, ch, j, beyond=False):
                n = (l * CHUNKS + ch) * 4 + j
                t = ch * 4 + j
                if not beyond:
                    pool.wait_ge(d.w, l * (16 * GROUPS) + 16 * GROUPS)
                    pool.wait_ge(d.qs, l * 96 + 96)
                need(pool, s.v_done, n * 4)
                need(pool, s.ffn_done, l * 4 + ch - 3)
                need(pool, s.k_scaled, n * 4)
                pool.tensor_copy(XS[0:64, :], c.xa[0:64, bass.ds(t * P + 1, P)])
                pool.tensor_copy(XS[64:P, :], c.xa[64:P, bass.ds(t * P, P)]).then_inc(s.xs_staged, 1)
                need(pool, s.xs_staged, n + 1)
                need(pool, s.roped, n * 4)
                pool.tensor_tensor(TAB[:, :], ROPE[:, bass.ds(t, 1), :].rearrange("p a b -> p (a b)"),
                                   QS[:, :], ALU.mult).then_inc(s.tab_ready, 1)
                for g in range(GROUPS):
                    G, par = n * 4 + g, g % 2
                    need(pool, s.scored, G - 3)
                    pool.tensor_tensor(KT[:, g, :, 0:WIN], KT[:, g, :, P:KEYS],
                                       KFAC[:, :].unsqueeze(2).to_broadcast([P, 2, WIN]), ALU.mult).then_inc(s.kprev, 1)
                    need(pool, s.clamped, G + 1)
                    need(pool, s.exped, G - 3)
                    pool.tensor_tensor(A[:, g, :], SSM[:, par, :], MHALF[:, 0:1].to_broadcast([P, 2 * GH]),
                                       ALU.pow).then_inc(s.norm_a, 1)
                    need(pool, s.norm_a, G + 1)
                    need(pool, s.roped, G + 1)
                    a_k = A[:, g, GH:2 * GH].unsqueeze(2).to_broadcast([P, GH, DH])
                    for i, buf in enumerate((TB, RB)):
                        k = buf[:, par, GD:2 * GD].rearrange("p (h e) -> p h e", h=GH)
                        m = pool.tensor_tensor(k, k, a_k, ALU.mult)
                    m.then_inc(s.k_scaled, 1)

            with pool.Fori(0, LAYERS) as l:
                with pool.Fori(0, CHUNKS) as ch:
                    with pool.Fori(0, 4) as j:
                        tile(l, ch, j)
            tile(LAYERS, 0, 0, beyond=True)

        @block.tensor
        def _(pe):
            pe.wait_ge(d.const, 48)
            pe.wait_ge(d.vec, 1)

            def proj_v(G, g):
                need(pe, s.v_kept, G)
                need(pe, s.o_kept, G - AHEAD + 1)
                pe.matmul(v_bank, XS[:, :], W[:, g, 2 * GD:3 * GD], start=True, stop=True).then_inc(s.v_done, 1)

            def proj_qk(G, n, g):
                need(pe, s.xs_staged, n + 1)
                need(pe, s.roped, G)
                pe.matmul(c.ps[:, QK_B, :], XS[:, :], W[:, g, 0:2 * GD], start=True, stop=True).then_inc(s.qk_done, 1)

            def turn(G, par):
                need(pe, s.k_scaled, G + 1)
                need(pe, s.qk_kept, G)
                for b in range(4):
                    o = c.ps[:, T_B, b * P:(b + 1) * P]
                    pe.matmul(o, TB[:, par, b * P:(b + 1) * P], c.ident[:, :], is_transpose=True, start=True, stop=False)
                    m = pe.matmul(o, RB[:, par, b * P:(b + 1) * P], c.ident[:, :], is_transpose=True, start=False, stop=True)
                m.then_inc(s.turned, 1)

            def score(G, t, g, par):
                need(pe, s.qk_kept, G + 1)
                need(pe, s.exped, G - 1)
                for h in range(2):
                    for b in range(2):
                        pe.matmul(s_bank(par)[:, b, h, :], c.ident_bf[:, :],
                                  MASK[:, bass.ds(t, 1), :].rearrange("p a k -> p (a k)"),
                                  start=(b == 0), stop=False, skip_group_check=True)
                for b in range(2):
                    for h in range(2):
                        m = pe.matmul(s_bank(par)[:, b, h, :], QT[64 * h:64 * h + 64, par, b, :],
                                      KT[64 * h:64 * h + 64, g, b, :], start=False, stop=(b == 1),
                                      skip_group_check=True)
                m.then_inc(s.scored, 1)

            def pturn(G, n, par):
                need(pe, s.exped, G + 1)
                need(pe, s.pt_kept, G)
                need(pe, s.resid, n)
                for h in range(GH):
                    m = pe.transpose(pt_bank[:, h * P:(h + 1) * P], PR[:, par, h, WIN:KEYS], c.ident[:, :])
                m.then_inc(s.p_turned, 1)

            def attend(G, g, par):
                need(pe, s.pt_kept, G + 1)
                need(pe, s.prev_turned, G + 1)
                need(pe, s.v_kept, G + AHEAD)
                need(pe, s.vprev_kept, G - 3)
                for h in range(GH):
                    pe.matmul(o_bank[:, h * DH:(h + 1) * DH], PTS[:, par, h * P:(h + 1) * P],
                              V[:, g, h * DH:(h + 1) * DH], start=(h == 0), stop=False, skip_group_check=True)
                for h in range(GH):
                    m = pe.matmul(o_bank[0:WIN, h * DH:(h + 1) * DH], PP[:, par, h * WIN:(h + 1) * WIN],
                                  VP[:, g, h * DH:(h + 1) * DH], start=False, stop=(h == GH - 1),
                                  skip_group_check=True)
                m.then_inc(s.attended, 1)

            def oturn(G):
                need(pe, s.normed, G + 1)
                for b in range(2):
                    m = pe.transpose(ot_bank[:, b, :], ON[:, b * P:(b + 1) * P], c.ident[:, :])
                m.then_inc(s.o_turned, 1)

            def project(n, l):
                need(pe, s.o_kept, 4 * n + 4)
                pe.wait_ge(d.wo, 16 * l + 16)
                need(pe, s.pt_kept, 4 * n + 4)
                for k in range(INNER // P):
                    m = pe.matmul(y_bank, WO[:, k, :], OTS[:, k, :], start=(k == 0), stop=(k == INNER // P - 1))
                m.then_inc(s.projected, 1)

            def step(n, t, g, l, first=False):
                G = n * 4 + g
                if not first:
                    pturn(G, n, g % 2)
                proj_qk(G + AHEAD, n + 1, g)
                if not first:
                    attend(G, g, g % 2)
                if not first or g >= 1:
                    turn(G + 3, (g + 3) % 2)
                if not first:
                    oturn(G)
                if not first or g >= 2:
                    score(G + 2, t + (g + 2) // 4, (g + 2) % 4, g % 2)
                proj_v(G + AHEAD, g)
                if not first and g == GROUPS - 1:
                    project(n, l)

            def ffn(k, l):
                need(pe, s.shifted, k + 1)
                need(pe, s.pt_kept, 16 * k + 16)
                need(pe, s.v_kept, 16 * k + 16 + AHEAD)
                need(pe, s.o_kept, 16 * k + 16)
                ln_pe(pe, s, c, k, XS2[:, :], mean_bank, var_bank)
                need(pe, s.affined, k + 1)
                pe.wait_ge(d.ffn, l * (16 * N_FFN) + 16 * N_FFN)
                for j, (h0, w) in enumerate(HPART):
                    need(pe, s.gelud, 3 * k + j)
                    pe.matmul(mean_bank[0:w, :], W1[:, HID + h0:HID + h0 + w], XN[:, :], start=True, stop=True).then_inc(s.gate, 1)
                    need(pe, s.gated, 3 * k + j)
                    pe.matmul(var_bank[0:w, :], W1[:, h0:h0 + w], XN[:, :], start=True, stop=True).then_inc(s.val, 1)
                need(pe, s.gated, 3 * k + 3)
                for j, (h0, w) in enumerate(HPART):
                    m = pe.matmul(mean_bank, W2[0:w, j, :], H[0:w, j, :], start=(j == 0), stop=(j == 2))
                m.then_inc(s.down, 1)

            for g in range(GROUPS):
                step(-1, -1, g, 0, first=True)
            with pe.Fori(0, LAYERS) as l:
                with pe.Fori(0, CHUNKS) as ch:
                    with pe.Fori(0, 4) as j:
                        need(pe, s.ffn_done, l * 4 + ch)
                        for g in range(GROUPS):
                            step((l * CHUNKS + ch) * 4 + j, ch * 4 + j, g, l)
                    ffn(l * CHUNKS + ch, l)

        @block.scalar
        def _(act):
            def square(G, par):
                need(act, s.qk_done, G + 1)
                need(act, s.summed, G - 1)
                act.activation(SQ[:, par, :], c.ps[:, QK_B, :], ACT.Square).then_inc(s.squared, 1)

            def keep(G, g, par):
                need(act, s.turned, G + 1)
                need(act, s.scored, G - 1)
                need(act, s.kprev, G + 1)
                act.activation(QT[:, par, :, :], c.ps[:, T_B, 0:GD].rearrange("p (b t) -> p b t", b=2), ACT.Copy)
                act.activation(KT[:, g, :, WIN:KEYS], c.ps[:, T_B, GD:2 * GD].rearrange("p (b t) -> p b t", b=2),
                               ACT.Copy).then_inc(s.qk_kept, 1)

            def exps(G, g, par):
                need(act, s.biased, G + 1)
                need(act, s.p_turned, G - 1)
                need(act, s.prev_turned, G - 1)
                need(act, s.recipd, G - 1)
                for h in range(GH):
                    m = act.activation(PR[:, par, h, :], s_bank(par)[:, h // 2, h % 2, :], ACT.Exp,
                                       bias=NB[:, par, h:h + 1], scale=A[:, g, h:h + 1],
                                       accum_out=RS[:, par, h:h + 1])
                m.then_inc(s.exped, 1)

            def pt_keep(G, par):
                need(act, s.p_turned, G + 1)
                need(act, s.attended, G - 1)
                act.activation(PTS[:, par, :], pt_bank, ACT.Copy).then_inc(s.pt_kept, 1)

            def step(n, g, first=False):
                G = n * 4 + g
                if not first:
                    pt_keep(G, g % 2)
                square(G + AHEAD, g % 2)
                if not first or g == 3:
                    exps(G + 1, (g + 1) % 4, (g + 1) % 2)
                if not first or g >= 1:
                    keep(G + 3, (g + 3) % 4, (g + 3) % 2)

            def ffn(k, l):
                ln_act(act, s, c, k, var_bank, c.eps5[:, 0:1])
                act.wait_ge(d.ffn, l * (16 * N_FFN) + 16 * N_FFN)
                for j, (h0, w) in enumerate(HPART):
                    need(act, s.gate, 3 * k + j + 1)
                    need(act, s.gated, 3 * k + j - 1)
                    act.activation(GT[0:w, j % 2, :], mean_bank[0:w, :], ACT.Gelu,
                                   bias=B1[0:w, 1, j:j + 1]).then_inc(s.gelud, 1)

            for g in range(GROUPS):
                step(-1, g, first=True)
            with act.Fori(0, LAYERS) as l:
                with act.Fori(0, CHUNKS) as ch:
                    with act.Fori(0, 4) as j:
                        for g in range(GROUPS):
                            step((l * CHUNKS + ch) * 4 + j, g)
                    ffn(l * CHUNKS + ch, l)

        @block.vector
        def _(dve):
            def rope_qk(G, n, par):
                need(dve, s.squared, G + 1)
                need(dve, s.tab_ready, n + 1)
                need(dve, s.turned, G - 1)
                tab = TAB[:, :].rearrange("p (c q e) -> p c q e", c=2, q=2)
                qk = c.ps[:, QK_B, :].rearrange("p (q h e) -> p q h e", q=2, h=GH)
                dve.tensor_tensor(TB[:, par, :].rearrange("p (q h e) -> p q h e", q=2, h=GH), qk,
                                  tab[:, 0, :, :].unsqueeze(2).to_broadcast([P, 2, GH, DH]), ALU.mult)
                for q in range(2):
                    src = c.ps[:, QK_B, q * GD:(q + 1) * GD].rearrange("p (h a e) -> p h a e", h=GH, a=2)[:, :, ::-1, :]
                    dst = RB[:, par, q * GD:(q + 1) * GD].rearrange("p (h a e) -> p h a e", h=GH, a=2)
                    sin = tab[:, 1, q, :].rearrange("p (a e) -> p a e", a=2).unsqueeze(1).to_broadcast([P, GH, 2, DH // 2])
                    m = dve.tensor_tensor(dst, src, sin, ALU.mult)
                m.then_inc(s.roped, 1)

            def sums(G, par):
                dve.tensor_reduce(SS[:, par, :], SQ[:, par, :].rearrange("p (h e) -> p h e", e=DH), AX.X,
                                  ALU.add).then_inc(s.summed, 1)
                need(dve, s.norm_a, G - 1)
                need(dve, s.summed, G + 1)
                dve.tensor_scalar(SSM[:, par, :], SS[:, par, :], 1e-24, None, ALU.max).then_inc(s.clamped, 1)

            def v_keep(G, g, first):
                need(dve, s.v_done, G + 1)
                if not first:
                    need(dve, s.attended, G - 3)
                    dve.tensor_copy(VP[:, g, :], V[P - WIN:P, g, :]).then_inc(s.vprev_kept, 1)
                    need(dve, s.vprev_kept, G - 3)
                dve.tensor_copy(V[:, g, :], v_bank).then_inc(s.v_kept, 1)

            def prev_turn(G, par):
                need(dve, s.exped, G + 1)
                need(dve, s.attended, G - 1)
                dve.transpose(PP[:, par, :].rearrange("p (h k) -> p h k", h=GH), PR[0:WIN, par, :, 0:WIN]).then_inc(s.prev_turned, 1)

            def recip(G, par):
                dve.reciprocal(RI[:, :], RS[:, par, :]).then_inc(s.recipd, 1)

            def normalize(G):
                need(dve, s.attended, G + 1)
                need(dve, s.recipd, G + 1)
                dve.tensor_tensor(ON[:, :].rearrange("p (h e) -> p h e", h=GH),
                                  o_bank.rearrange("p (h e) -> p h e", h=GH),
                                  RI[:, :].unsqueeze(2).to_broadcast([P, GH, DH]), ALU.mult).then_inc(s.normed, 1)

            def o_keep(G, n, g):
                need(dve, s.o_turned, G + 1)
                need(dve, s.projected, n)
                dve.tensor_copy(OTS[:, 2 * g:2 * g + 2, :], ot_bank).then_inc(s.o_kept, 1)

            def maxes(G, g, par):
                need(dve, s.scored, G + 1)
                dve.tensor_reduce(NM[:, par, :].rearrange("p (b h) -> p b h", b=2), s_bank(par), AX.X, ALU.max,
                                  negate=True).then_inc(s.maxed, 1)
                need(dve, s.maxed, G + 1)
                need(dve, s.norm_a, G + 1)
                need(dve, s.exped, G - 1)
                dve.tensor_tensor(NB[:, par, :], NM[:, par, :], A[:, g, 0:GH], ALU.mult).then_inc(s.biased, 1)

            def residual(n, t):
                need(dve, s.projected, n + 1)
                dve.tensor_tensor(c.xb[:, bass.ds(t * P + 1, P)], y_bank, c.xa[:, bass.ds(t * P + 1, P)],
                                  ALU.add).then_inc(s.resid, 1)

            def step(n, t, g, first=False):
                G = n * 4 + g
                if not first:
                    prev_turn(G, g % 2)
                    recip(G, g % 2)
                rope_qk(G + AHEAD, n + 1, g % 2)
                if not first:
                    normalize(G)
                sums(G + AHEAD, g % 2)
                if not first:
                    o_keep(G, n, g)
                if not first or g >= 2:
                    maxes(G + 2, (g + 2) % 4, g % 2)
                v_keep(G + AHEAD, g, first)
                if not first and g == GROUPS - 1:
                    residual(n, t)

            def ffn(k, ch, l):
                need(dve, s.resid, 4 * k + 4)
                dve.tensor_copy(XS2[0:64, :], c.xb[0:64, bass.ds(ch * CH + 1, CH)])
                dve.tensor_copy(XS2[64:P, :], c.xb[64:P, bass.ds(ch * CH, CH)]).then_inc(s.shifted, 1)
                need(dve, s.shifted, k + 1)
                ln_dve(dve, s, c, k, XS2[:, :], mean_bank, XN[:, :])
                need(dve, s.ln_done, k + 1)
                dve.wait_ge(d.ffn, l * (16 * N_FFN) + 16 * N_FFN)
                dve.tensor_scalar(XN[:, :], XN[:, :], VEC[:, 0:1], VEC[:, 1:2], ALU.mult, ALU.add).then_inc(s.affined, 1)
                for j, (h0, w) in enumerate(HPART):
                    need(dve, s.val, 3 * k + j + 1)
                    need(dve, s.gelud, 3 * k + j + 1)
                    dve.scalar_tensor_tensor(H[0:w, j, :], var_bank[0:w, :], B1[0:w, 0, j:j + 1], GT[0:w, j % 2, :],
                                             ALU.add, ALU.mult).then_inc(s.gated, 1)
                need(dve, s.down, k + 1)
                need(dve, s.xs_staged, 4 * k + 5)
                dve.scalar_tensor_tensor(c.xa[:, bass.ds(ch * CH + 1, CH)], mean_bank, VEC[:, 2:3],
                                         c.xb[:, bass.ds(ch * CH + 1, CH)], ALU.add, ALU.add).then_inc(s.ffn_done, 1)

            for g in range(GROUPS):
                step(-1, -1, g, first=True)
            with dve.Fori(0, LAYERS) as l:
                with dve.Fori(0, CHUNKS) as ch:
                    with dve.Fori(0, 4) as j:
                        for g in range(GROUPS):
                            step((l * CHUNKS + ch) * 4 + j, ch * 4 + j, g)
                    ffn(l * CHUNKS + ch, ch, l)


def store_phase(nc, c, x3, out):
    with ExitStack() as ctx:
        s = Counters(nc, ctx, "st_", LN_NAMES + " summed turned kept stored")
        y_tok = ctx.enter_context(nc.sbuf_tensor("y_tok", [P, TILES, P], F32))
        start_counters(nc, [s.ln_mean, s.ln_centered, s.ln_squared, s.ln_var, s.ln_sd, s.ln_rstd, s.ln_done])
        block = ctx.enter_context(nc.Block())

        def x(b):
            return c.xb[:, 1 + CH * b:1 + CH * (b + 1)]

        def y(b):
            return c.xa[:, 1 + CH * b:1 + CH * (b + 1)]

        @block.tensor
        def _(pe):
            for b in range(CHUNKS):
                pe.wait_ge(s.summed, b + 1)
                ln_pe(pe, s, c, b, x(b), c.ps[:, 0, :], c.ps[:, 1, :])
                need(pe, s.ln_done, b + 1)
                for t in range(4):
                    m = pe.transpose(c.ps[:, 4 + b, t * P:(t + 1) * P],
                                     c.xa[:, 1 + CH * b + P * t:1 + CH * b + P * (t + 1)], c.ident[:, :])
                m.then_inc(s.turned, 1)

        @block.scalar
        def _(act):
            for b in range(CHUNKS):
                ln_act(act, s, c, b, c.ps[:, 1, :], c.eps5[:, 0:1])

        @block.vector
        def _(dve):
            for b in range(CHUNKS):
                dve.tensor_tensor(x(b), x3[:, CH * b:CH * (b + 1)], y(b), ALU.add).then_inc(s.summed, 1)
            dve.wait_ge(s.summed, CHUNKS)
            for b in range(CHUNKS):
                ln_dve(dve, s, c, b, x(b), c.ps[:, 0, :], y(b))
                dve.wait_ge(s.turned, b + 1)
                dve.tensor_copy(y_tok[:, 4 * b:4 * b + 4, :],
                                c.ps[:, 4 + b, :].rearrange("p (t f) -> p t f", t=4)).then_inc(s.kept, 1)

        @block.sync
        def _(sp):
            for b in range(CHUNKS):
                sp.wait_ge(s.kept, b + 1)
                sp.dma_start(out[0, CH * b:CH * (b + 1), :].rearrange("(t p) f -> p t f", p=P),
                             y_tok[:, 4 * b:4 * b + 4, :]).then_inc(s.stored, 16)
            sp.wait_ge(s.stored, 16 * CHUNKS)


def program(nc, t, out):
    with ExitStack() as ctx:
        c = Common(nc, ctx)
        load_phase(nc, c, t["L0_attn_x"], t["c_ident"])
        attention_and_quant(nc, c, t)
        x3 = ctx.enter_context(nc.sbuf_tensor("x3", [P, T], F32))
        ssm_phase(nc, c, x3, {n.removeprefix("L1_attn_"): a for n, a in t.items()})
        local_phase(nc, c, *[t["L1_ffn_" + n] for n in ("Wqkv", "q_scale", "k_scale", "Wo", "ln_g", "ln_b", "W1", "b1", "W2", "b2")],
                    t["c_rope"], t["c_mask"], t["c_kfac"])
        store_phase(nc, c, x3, out)



def constants():
    import numpy as np
    bf16 = mybir.dt.np(BF16)
    f32 = np.float32
    half = np.arange(0, DH, 2, dtype=f32)
    inv_freq = (f32(1.0) / f32(10000.0) ** (half / f32(DH))).astype(f32)
    freqs = np.arange(T, dtype=f32)[:, None] * inv_freq[None, :]
    cos, sin = np.cos(freqs).astype(f32), np.sin(freqs).astype(f32)
    base = ((half + 0.4 * DH) / (1.4 * DH)).astype(np.float64)
    power = (np.arange(T) % P - P // 2) / (WIN // 2)
    scale = base[None, :] ** power[:, None]
    both = lambda a: np.concatenate([a, a], -1)
    sign = np.concatenate([-np.ones(DH // 2), np.ones(DH // 2)])[None, :]
    parts = [both(cos * scale) * 8.0, both(cos / scale), both(sin * scale) * sign * 8.0, both(sin / scale) * sign]
    rope = np.stack(parts, 1).astype(f32).reshape(TILES, P, 4 * DH).transpose(1, 0, 2)
    q = np.arange(P)[:, None]
    k = np.arange(KEYS)[None, :] - WIN
    seen = (k <= q) & (k >= q - WIN)
    mask = np.repeat(np.where(seen, 0.0, -1e30)[:, None, :], TILES + 1, 1)
    mask[:, [0, TILES], 0:WIN] = -1e30
    return {
        "c_ident": np.eye(P, dtype=f32),
        "c_rope": np.ascontiguousarray(rope),
        "c_mask": mask.astype(bf16),
        "c_select": np.ascontiguousarray(np.broadcast_to(
            (np.arange(3 * BC)[:, None] % BC == np.arange(BC)[None, :])[:, :, None], (3 * BC, BC, P))).astype(bf16),
        "c_ones_rows": (np.arange(P) % MROWS < 3).astype(f32)[:, None],
        "c_mask_qk": np.where(np.arange(P)[None, :] > q, -1e30, 0.0).astype(bf16),
        "c_mask_kq": np.where(q > np.arange(P)[None, :], -1e30, 0.0).astype(bf16),
        "c_kfac": np.tile(both(base ** (P // (WIN // 2))), 2).astype(f32)[:, None],
    }


def kernel(**inputs):
    import numpy as _np
    import concourse.bacc as _bacc
    from concourse import mybir as _mybir
    from concourse.bass_utils import run_bass_kernel_spmd as _run

    nc = _bacc.Bacc("TRN2", target_bir_lowering=False, num_devices=1)
    arrays = {"in_" + n: _np.ascontiguousarray(a) for n, a in inputs.items()}
    arrays.update(constants())
    tensors = {n.removeprefix("in_"): nc.dram_tensor(n, a.shape, _mybir.dt.from_np(a.dtype), kind="ExternalInput").ap()
               for n, a in arrays.items()}
    out = nc.dram_tensor("out_0_dram", (1, T, P), F32, kind="ExternalOutput").ap()
    program(nc, tensors, out)
    r = _run(nc, [arrays], core_ids=[0])
    return r.results[0]["out_0_dram"]
```

```python
from collections import namedtuple
from contextlib import ExitStack

import concourse.bass as bass
from concourse import mybir

ALU = mybir.AluOpType
ACT = mybir.ActivationFunctionType
AX = mybir.AxisListType
F32 = mybir.dt.float32
BF16 = mybir.dt.bfloat16
U32 = mybir.dt.uint32

P = 128
T = 2048
TILES = T // P
CH = 512
CHUNKS = T // CH
BASE = 8


def need(eng, counter, count):
    eng.wait_ge(counter, count + BASE)


def Counters(nc, ctx, prefix, names):
    counters = namedtuple("Semaphores", names)(*[nc.alloc_semaphore(name=prefix + n) for n in names.split()])
    ctx.callback(nc.all_engine_barrier)
    ctx.callback(nc.clear_and_free_semaphores, list(counters))
    return counters


def start_counters(nc, counters):
    with nc.Block() as block:
        @block.sync
        def _(sp):
            for c in counters:
                sp.sem_inc(c, BASE)



LN_NAMES = "ln_mean ln_centered ln_squared ln_var ln_sd ln_rstd ln_done"


def ln_pe(pe, s, c, k, x, mean, var):
    pe.matmul(mean, c.avg[:, :], x, start=True, stop=True).then_inc(s.ln_mean, 1)
    need(pe, s.ln_squared, k + 1)
    pe.matmul(var, c.avg[:, :], c.ln_sq[:, :], start=True, stop=True).then_inc(s.ln_var, 1)


def ln_act(act, s, c, k, var, eps):
    need(act, s.ln_centered, k + 1)
    act.activation(c.ln_sq[:, :], c.ln_cen[:, :], ACT.Square).then_inc(s.ln_squared, 1)
    need(act, s.ln_var, k + 1)
    act.activation(c.ln_sd[:, :], var, ACT.Sqrt, bias=eps).then_inc(s.ln_sd, 1)


def ln_dve(dve, s, c, k, x, mean, out):
    need(dve, s.ln_mean, k + 1)
    dve.tensor_tensor(c.ln_cen[:, :], x, mean, ALU.subtract).then_inc(s.ln_centered, 1)
    need(dve, s.ln_sd, k + 1)
    dve.reciprocal(c.ln_rs[:, :], c.ln_sd[:, :]).then_inc(s.ln_rstd, 1)
    need(dve, s.ln_rstd, k + 1)
    dve.tensor_tensor(out, c.ln_cen[:, :], c.ln_rs[:, :], ALU.mult).then_inc(s.ln_done, 1)


class Common:

    def __init__(self, nc, ctx):
        def sb(name, shape, dt=F32):
            return ctx.enter_context(nc.sbuf_tensor(name, shape, dt))

        self.xa = sb("xa", [P, T + 1])
        self.xb = sb("xb", [P, T + 1])
        self.ident = sb("ident", [P, P])
        self.ident_bf = sb("ident_bf", [P, P], BF16)
        self.avg = sb("avg", [P, P])
        self.eps5 = sb("eps5", [P, 1])
        self.eps6 = sb("eps6", [P, 1])
        self.ln_cen = sb("ln_cen", [P, CH])
        self.ln_sq = sb("ln_sq", [P, CH])
        self.ln_sd = sb("ln_sd", [P, CH])
        self.ln_rs = sb("ln_rs", [P, CH])
        self.ps = ctx.enter_context(nc.psum_tensor("ps", [P, 8, CH], F32))


def load_phase(nc, c, x, ident):
    with ExitStack() as ctx:
        s = Counters(nc, ctx, "ld_", "x ident turned kept const")
        x_tok = ctx.enter_context(nc.sbuf_tensor("x_tok", [P, TILES, P], F32))
        block = ctx.enter_context(nc.Block())

        @block.sync
        def _(sp):
            sp.dma_start(c.ident[:, :], ident).then_inc(s.ident, 16)
            sp.dma_start(x_tok[:, :, :], x[0].rearrange("(t p) f -> p t f", p=P)).then_inc(s.x, 16)

        @block.gpsimd
        def _(pool):
            pool.memset(c.avg[:, :], 1.0 / P)
            pool.memset(c.eps5[:, :], 1e-5)
            pool.memset(c.eps6[:, :], 1e-6)
            pool.memset(c.xa[:, 0:1], 0.0)
            pool.memset(c.xb[:, 0:1], 0.0).then_inc(s.const, 1)

        @block.tensor
        def _(pe):
            pe.wait_ge(s.ident, 16)
            pe.wait_ge(s.x, 16)
            for b in range(CHUNKS):
                for t in range(4 * b, 4 * b + 4):
                    m = pe.transpose(c.ps[:, b, (t % 4) * P:(t % 4 + 1) * P], x_tok[:, t, :], c.ident[:, :])
                m.then_inc(s.turned, 1)

        @block.vector
        def _(dve):
            dve.wait_ge(s.ident, 16)
            dve.tensor_copy(c.ident_bf[:, :], c.ident[:, :])
            for b in range(CHUNKS):
                dve.wait_ge(s.turned, b + 1)
                dve.tensor_copy(c.xa[:, 1 + CH * b:1 + CH * (b + 1)], c.ps[:, b, :]).then_inc(s.kept, 1)



AHEADS = 16
AD = P // AHEADS
LATENT = 32
PAIRS = AHEADS // 2
MROWS = 8
USED = MROWS + 6 * AD
Q_PART = (0, 0, 1, 1, 0, 2)
K_PART = (0, 1, 0, 1, 2, 0)
VW = AD + 1
A_SCALE = AD ** -0.5
UNITS = [4 * (b + 1) for b in range(CHUNKS)]
STEP_UNITS = 2 * sum(UNITS)
STEPS = [(0, b) for b in range(CHUNKS)] + [(1, b) for b in reversed(range(CHUNKS))]


def units_before(st):
    return sum(UNITS[b] for _, b in STEPS[:st])


def project_phase(nc, c, m, w_dkv, w_uk, w_uv, w_uq, ones_rows, q_stack, k_stack):
    with ExitStack() as ctx:
        def sb(name, shape, dt=F32):
            return ctx.enter_context(nc.sbuf_tensor("ap_" + name, shape, dt))

        WD = sb("WD", [P, LATENT])
        WK = sb("WK", [LATENT, P])
        WV = sb("WV", [LATENT, P])
        WQ = sb("WQ", [P, P])
        CT = sb("CT", [LATENT, T])
        ONES = sb("ONES", [P, 1])
        FILL = sb("FILL", [P, 2, T], BF16)
        PART = sb("PART", [P, 2, 3, T], BF16)
        REST = sb("REST", [P, 2, CH])
        s = Counters(nc, ctx, "ap_", "w ones zeroed filled latent ckept vdone vkept proj first rest second third stored")
        block = ctx.enter_context(nc.Block())

        @block.sync
        def _(sp):
            for dst, src in ((WD, w_dkv), (WK, w_uk), (WV, w_uv), (WQ, w_uq)):
                sp.dma_start(dst[:, :], src).then_inc(s.w, 16)
            sp.dma_start(ONES[:, :], ones_rows).then_inc(s.ones, 16)
            stacks = (q_stack, k_stack)
            for i in range(2):
                sp.wait_ge(s.filled, i + 1)
                sp.dma_start(stacks[i][:, 0:MROWS, :], FILL[:, i, :]).then_inc(s.stored, 16)
            for i, terms in enumerate((Q_PART, K_PART)):
                sp.wait_ge(s.third, 4 * (i + 1))
                for t, part in enumerate(terms):
                    sp.dma_start(stacks[i][:, MROWS + AD * t:MROWS + AD * (t + 1), :],
                                 PART[:, i, part, :]).then_inc(s.stored, 16)
            sp.wait_ge(s.stored, 16 * 14)

        @block.gpsimd
        def _(pool):
            pool.memset(FILL[:, 0, :], 0.0).then_inc(s.filled, 1)
            pool.wait_ge(s.ones, 16)
            pool.wait_ge(s.filled, 1)
            pool.tensor_copy(FILL[:, 1, :], ONES[:, 0:1].to_broadcast([P, T])).then_inc(s.filled, 1)

        @block.tensor
        def _(pe):
            pe.wait_ge(s.w, 64)
            for b in range(CHUNKS):
                pe.matmul(c.ps[0:LATENT, b, :], WD[:, :], c.xa[:, 1 + CH * b:1 + CH * (b + 1)],
                          start=True, stop=True).then_inc(s.latent, 1)
            for i in range(2):
                for b in range(CHUNKS):
                    k = 4 * i + b
                    if k >= 2:
                        pe.wait_ge(s.rest, k - 1)
                    if i == 1:
                        pe.wait_ge(s.ckept, b + 1)
                    w, x = (WQ, c.xa[:, 1 + CH * b:1 + CH * (b + 1)]) if i == 0 else (WK, CT[:, CH * b:CH * (b + 1)])
                    pe.matmul(c.ps[:, 4 + k % 2, :], w[:, :], x, start=True, stop=True).then_inc(s.proj, 1)
            for t in range(TILES):
                if t >= 8:
                    pe.wait_ge(s.vkept, t // 4 - 1)
                mm = pe.matmul(c.ps[:, 6 + (t // 4) % 2, (t % 4) * P:(t % 4 + 1) * P], CT[:, t * P:(t + 1) * P], WV[:, :],
                               start=True, stop=True)
                if t % 4 == 3:
                    mm.then_inc(s.vdone, 1)

        @block.scalar
        def _(act):
            for k in range(8):
                i, b = k // 4, k % 4
                act.wait_ge(s.proj, k + 1)
                act.activation(PART[:, i, 0, CH * b:CH * (b + 1)], c.ps[:, 4 + k % 2, :], ACT.Copy).then_inc(s.first, 1)
                act.wait_ge(s.rest, k + 1)
                act.activation(PART[:, i, 1, CH * b:CH * (b + 1)], REST[:, k % 2, :], ACT.Copy).then_inc(s.second, 1)

        @block.vector
        def _(dve):
            dve.memset(m.va[:, :, :, :], 1.0).then_inc(s.zeroed, 1)
            dve.wait_ge(s.zeroed, 1)
            for b in range(CHUNKS):
                dve.wait_ge(s.latent, b + 1)
                dve.tensor_copy(CT[:, CH * b:CH * (b + 1)], c.ps[0:LATENT, b, :]).then_inc(s.ckept, 1)

            def third(k):
                i, b = k // 4, k % 4
                dve.wait_ge(s.second, k + 1)
                dve.tensor_tensor(PART[:, i, 2, CH * b:CH * (b + 1)], REST[:, k % 2, :],
                                  PART[:, i, 1, CH * b:CH * (b + 1)], ALU.subtract).then_inc(s.third, 1)

            for k in range(8):
                i, b = k // 4, k % 4
                dve.wait_ge(s.first, k + 1)
                if k >= 2:
                    dve.wait_ge(s.third, k - 1)
                dve.tensor_tensor(REST[:, k % 2, :], c.ps[:, 4 + k % 2, :], PART[:, i, 0, CH * b:CH * (b + 1)],
                                  ALU.subtract).then_inc(s.rest, 1)
                if k >= 1:
                    third(k - 1)
            third(7)
            for b in range(CHUNKS):
                dve.wait_ge(s.vdone, b + 1)
                dve.tensor_copy(m.va[:, 4 * b:4 * b + 4, :, 0:AD],
                                c.ps[:, 6 + b % 2, :].rearrange("p (t h e) -> p t h e", t=4, e=AD)).then_inc(s.vkept, 1)


CROWS = 32 + VW
CAUSAL_COUNTERS = ("vs_ready p1_scored p1_maxed m_neg m_a m_b m_c m_d m_turned m_kept s_done exped attended "
                   "ctx_left ctx_turned ctx_sum ctx_done")


def causal_phase(nc, c, m, q_stack, k_stack, mask_qk, mask_kq):
    with ExitStack() as ctx:
        def sb(name, shape, dt=F32):
            return ctx.enter_context(nc.sbuf_tensor("ac_" + name, shape, dt))

        QS = sb("QS", [P, 2, T], BF16)
        KS = sb("KS", [P, 2, T], BF16)
        VS = sb("VS", [P, 2, TILES, 2 * VW])
        MQK = sb("MQK", [P, P], BF16)
        MKQ = sb("MKQ", [P, P], BF16)
        PM = sb("PM", [P, CHUNKS, 4, 2])
        NM = sb("NM", [P, 4, 2])
        NR = sb("NR", [P, 4, 2])
        M3 = sb("M3", [P, 4, P], BF16)
        PT = sb("PT", [P, 2, 2, CH])
        CX = sb("CX", [CROWS, CH])
        LI = sb("LI", [P, 4, 2])
        s = Counters(nc, ctx, "ac_", CAUSAL_COUNTERS)
        start_counters(nc, s)
        d = Counters(nc, ctx, "acd_", "stack0 stack1 masks zero")
        stack = (d.stack0, d.stack1)
        m_bank = c.ps[:, 7, :].bitcast(BF16)
        o_bank = c.ps[:, 7, CH // 2:CH // 2 + 4 * CROWS]
        m3 = M3[:, :, :].rearrange("p t (s r) -> p t s r", s=2)
        block = ctx.enter_context(nc.Block())

        @block.sync
        def _(sp):
            sp.dma_start(MQK[:, :], mask_qk).then_inc(d.masks, 16)
            sp.dma_start(MKQ[:, :], mask_kq).then_inc(d.masks, 16)
            with sp.Fori(0, PAIRS // 2) as it:
                for u in range(2):
                    need(sp, s.ctx_done, it * len(STEPS) + CHUNKS * (u - 1))
                    for dst, src in ((QS, q_stack), (KS, k_stack)):
                        for h in range(2):
                            sp.dma_start(dst[64 * h:64 * h + USED, u, :],
                                         src[bass.ds(it * 4 + 2 * u + h, 1), :, :].rearrange("h r t -> (h r) t"))\
                              .then_inc(stack[u], 16)

        @block.gpsimd
        def _(pool):
            pool.memset(CX[:, :], 0.0)
            pool.memset(M3[:, :, :], 0.0).then_inc(d.zero, 1)
            with pool.Fori(0, PAIRS // 2) as it:
                for u in range(2):
                    need(pool, s.ctx_done, it * len(STEPS) + CHUNKS * (u - 1))
                    pool.tensor_copy(VS[:, u, :, :], m.va[:, :, :, :].rearrange("p t h e -> p t (h e)")
                                     [:, :, bass.ds((it * 2 + u) * (2 * VW), 2 * VW)]).then_inc(s.vs_ready, 1)

        @block.tensor
        def _(pe):
            pe.wait_ge(d.masks, 32)
            pe.wait_ge(d.zero, 1)

            def p1(it, st, n):
                u, b = STEPS[st]
                i, j = n // (b + 1), n % (b + 1)
                last = j == b
                w = (i + 1) * P if last else CH
                q0 = CH * b + P * i
                if n == 0 and st % CHUNKS == 0:
                    pe.wait_ge(stack[u], it * 64 + 64)
                done = 2 * (it * STEP_UNITS + units_before(st) + n)
                for h in range(2):
                    need(pe, s.p1_maxed, done + h - 1)
                    mm = pe.matmul(c.ps[:, 4 + h, 0:w], QS[64 * h:64 * h + USED, u, q0:q0 + P],
                                   KS[64 * h:64 * h + USED, u, CH * j:CH * j + w], start=True, stop=not last)
                    if last:
                        mm = pe.matmul(c.ps[:, 4 + h, w - P:w], c.ident_bf[:, :], MQK[:, :], start=False, stop=True)
                    mm.then_inc(s.p1_scored, 1)

            def maxima(it, st):
                need(pe, s.m_d, it * len(STEPS) + st + 1)
                need(pe, s.m_kept, it * len(STEPS) + st)
                for i in range(4):
                    mm = pe.transpose(m_bank[:, i * P:(i + 1) * P], M3[:, i, :], c.ident_bf[:, :])
                mm.then_inc(s.m_turned, 1)

            def s2(it, st, j):
                u, b = STEPS[st]
                n = units_before(st) + j
                q0 = max(0, j - 4 * b) * P
                need(pe, s.exped, it * STEP_UNITS + n - 1)
                if j == 0:
                    need(pe, s.m_kept, it * len(STEPS) + st + 1)
                for h in range(2):
                    mm = pe.matmul(c.ps[:, 2 * (n % 2) + h, q0:CH], KS[64 * h:64 * h + USED, u, P * j:P * (j + 1)],
                                   QS[64 * h:64 * h + USED, u, CH * b + q0:CH * (b + 1)], start=True, stop=j < 4 * b)
                if j >= 4 * b:
                    for h in range(2):
                        mm = pe.matmul(c.ps[:, 2 * (n % 2) + h, q0:q0 + P], c.ident_bf[:, :], MKQ[:, :],
                                       start=False, stop=True)
                mm.then_inc(s.s_done, 1)

            def attend(it, st, j):
                u, b = STEPS[st]
                n = units_before(st) + j
                need(pe, s.exped, it * STEP_UNITS + n + 1)
                if j == 0:
                    need(pe, s.ctx_left, it * len(STEPS) + st)
                    if st % CHUNKS == 0:
                        need(pe, s.vs_ready, it * 2 + u + 1)
                q0 = max(0, j - 4 * b) * P
                for h in range(2):
                    mm = pe.matmul(c.ps[32 * h:32 * h + VW, 6, q0:CH], VS[:, u, j, h * VW:(h + 1) * VW],
                                   PT[:, n % 2, h, q0:CH], start=j == 0, stop=j == UNITS[b] - 1,
                                   skip_group_check=True)
                mm.then_inc(s.attended, 1)

            def turn_context(it, st):
                k = it * len(STEPS) + st
                need(pe, s.ctx_left, k + 1)
                need(pe, s.ctx_done, k)
                for i in range(4):
                    mm = pe.matmul(o_bank[:, i * CROWS:(i + 1) * CROWS], CX[:, i * P:(i + 1) * P],
                                   c.ident[0:CROWS, 0:CROWS], start=i == 0, stop=True, skip_group_check=True)
                mm.then_inc(s.ctx_turned, 1)

            with pe.Fori(0, PAIRS // 2) as it:
                for n in range(UNITS[0]):
                    p1(it, 0, n)
                maxima(it, 0)
                for st, (u, b) in enumerate(STEPS):
                    after = UNITS[STEPS[st + 1][1]] if st + 1 < len(STEPS) else 0
                    among = max(2, UNITS[b] - 3)
                    for n in range(UNITS[b] + 1):
                        if n < UNITS[b]:
                            s2(it, st, n)
                        for i in range(after):
                            if i * among // after == n:
                                p1(it, st + 1, i)
                        if 1 <= n <= UNITS[b]:
                            attend(it, st, n - 1)
                        if n == among:
                            if st >= 1:
                                turn_context(it, st - 1)
                            if after:
                                maxima(it, st + 1)
                turn_context(it, len(STEPS) - 1)

        @block.scalar
        def _(act):
            act.wait_ge(d.zero, 1)

            def leave(it, st):
                k = it * len(STEPS) + st
                need(act, s.attended, it * STEP_UNITS + units_before(st + 1))
                need(act, s.ctx_turned, k)
                for h in range(2):
                    rows = slice(32 * h, 32 * h + VW)
                    mm = act.activation(CX[rows, :], c.ps[rows, 6, :], ACT.Copy)
                mm.then_inc(s.ctx_left, 1)

            with act.Fori(0, PAIRS // 2) as it:
                for st, (u, b) in enumerate(STEPS):
                    for j in range(UNITS[b]):
                        n = units_before(st) + j
                        q0 = max(0, j - 4 * b) * P
                        need(act, s.s_done, it * STEP_UNITS + n + 1)
                        need(act, s.attended, it * STEP_UNITS + n - 1)
                        act.activation(PT[:, n % 2, :, q0:CH], c.ps[:, 2 * (n % 2):2 * (n % 2) + 2, q0:CH], ACT.Exp,
                                       scale=A_SCALE).then_inc(s.exped, 1)
                        if j == 0 and st >= 1:
                            leave(it, st - 1)
                leave(it, len(STEPS) - 1)

        @block.vector
        def _(dve):
            dve.wait_ge(d.zero, 1)

            def p1_max(it, st, n):
                u, b = STEPS[st]
                i, j = n // (b + 1), n % (b + 1)
                w = (i + 1) * P if j == b else CH
                done = 2 * (it * STEP_UNITS + units_before(st) + n)
                for h in range(2):
                    need(dve, s.p1_scored, done + h + 1)
                    dve.tensor_reduce(PM[:, j, i, h:h + 1], c.ps[:, 4 + h, 0:w], AX.X, ALU.max).then_inc(s.p1_maxed, 1)

            def maxima(it, st):
                u, b = STEPS[st]
                k = it * len(STEPS) + st
                need(dve, s.p1_maxed, 2 * (it * STEP_UNITS + units_before(st + 1)))
                dve.tensor_reduce(NM[:, :, :], PM[:, 0:b + 1, :, :].rearrange("p j i s -> p i s j"), AX.X, ALU.max,
                                  negate=True).then_inc(s.m_neg, 1)
                need(dve, s.m_neg, k + 1)
                need(dve, s.m_turned, k)
                dve.tensor_copy(m3[:, :, :, 0], NM[:, :, :]).then_inc(s.m_a, 1)
                need(dve, s.m_a, k + 1)
                dve.tensor_tensor(NR[:, :, :], NM[:, :, :], m3[:, :, :, 0], ALU.subtract).then_inc(s.m_b, 1)
                need(dve, s.m_b, k + 1)
                dve.tensor_copy(m3[:, :, :, 1], NR[:, :, :]).then_inc(s.m_c, 1)
                need(dve, s.m_c, k + 1)
                dve.tensor_tensor(m3[:, :, :, 2], NR[:, :, :], m3[:, :, :, 1], ALU.subtract).then_inc(s.m_d, 1)

            def keep_maxima(it, st):
                u, b = STEPS[st]
                need(dve, s.m_turned, it * len(STEPS) + st + 1)
                for h in range(2):
                    mm = dve.tensor_copy(QS[64 * h:64 * h + 3, u, CH * b:CH * (b + 1)], m_bank[64 * h:64 * h + 3, 0:CH])
                mm.then_inc(s.m_kept, 1)

            def context(it, st):
                u, b = STEPS[st]
                k = it * len(STEPS) + st
                o = o_bank.rearrange("p (i r) -> p i r", r=CROWS)
                need(dve, s.ctx_turned, k + 1)
                dve.reciprocal(LI[:, :, :], o[:, :, AD::32]).then_inc(s.ctx_sum, 1)
                need(dve, s.ctx_sum, k + 1)
                for h in range(2):
                    mm = dve.tensor_tensor(m.ctx[:, 4 * b:4 * b + 4, bass.ds((it * 2 + u) * (2 * AD) + h * AD, AD)],
                                           o[:, :, 32 * h:32 * h + AD], LI[:, :, h:h + 1].to_broadcast([P, 4, AD]), ALU.mult)
                mm.then_inc(s.ctx_done, 1)

            with dve.Fori(0, PAIRS // 2) as it:
                for n in range(UNITS[0]):
                    p1_max(it, 0, n)
                maxima(it, 0)
                keep_maxima(it, 0)
                for st in range(len(STEPS)):
                    if st + 1 < len(STEPS):
                        for n in range(UNITS[STEPS[st + 1][1]]):
                            p1_max(it, st + 1, n)
                        maxima(it, st + 1)
                        keep_maxima(it, st + 1)
                    if st >= 1:
                        context(it, st - 1)
                context(it, len(STEPS) - 1)


POST_COUNTERS = ("ct_turned ct_kept y_done summed scale clipped low bits unit magic rounded w_turned w_kept o_done "
                 "o_kept o_summed " + LN_NAMES)


def quant_phase(nc, c, m, w_o, w8, bias, in_scale, w_scale):
    with ExitStack() as ctx:
        def sb(name, shape, dt=F32):
            return ctx.enter_context(nc.sbuf_tensor("qz_" + name, shape, dt))

        WO = sb("WO", [P, P])
        W8 = sb("W8", [P, P])
        W8T = sb("W8T", [P, P])
        BIAS = sb("BIAS", [P, 1])
        SI = sb("SI", [P, 1])
        SW = sb("SW", [P, 1])
        RSI = sb("RSI", [P, 1])
        SIW = sb("SIW", [P, 1])
        CT = sb("CT", [P, CH])
        Y = sb("Y", [P, CH])
        X1 = sb("X1", [P, CH])
        XQ = sb("XQ", [P, CH])
        UNIT = sb("UNIT", [P, CH])
        s = Counters(nc, ctx, "qz_", POST_COUNTERS)
        start_counters(nc, s)
        d = Counters(nc, ctx, "qzd_", "w")
        mean, var = c.ps[:, 2, :], c.ps[:, 3, :]
        block = ctx.enter_context(nc.Block())

        def xa(b):
            return c.xa[:, 1 + CH * b:1 + CH * (b + 1)]

        @block.sync
        def _(sp):
            for dst, src in ((WO, w_o), (W8, w8), (BIAS, bias.rearrange("(p a) -> p a", a=1)),
                             (SI, in_scale.rearrange("(a b) -> a b", a=1).broadcast_to([P, 1])),
                             (SW, w_scale.rearrange("(a b) -> a b", a=1).broadcast_to([P, 1]))):
                sp.dma_start(dst[:, :], src).then_inc(d.w, 16)

        @block.tensor
        def _(pe):
            pe.wait_ge(d.w, 80)
            pe.transpose(c.ps[:, 5, 0:P], W8[:, :], c.ident[:, :]).then_inc(s.w_turned, 1)
            for b in range(CHUNKS):
                need(pe, s.ct_kept, b)
                for i in range(4):
                    mm = pe.transpose(c.ps[:, 0, i * P:(i + 1) * P], m.ctx[:, 4 * b + i, :], c.ident[:, :])
                mm.then_inc(s.ct_turned, 1)
                need(pe, s.ct_kept, b + 1)
                need(pe, s.summed, b)
                pe.matmul(c.ps[:, 1, :], WO[:, :], CT[:, :], start=True, stop=True).then_inc(s.y_done, 1)
                need(pe, s.summed, b + 1)
                ln_pe(pe, s, c, 2 * b, Y[:, :], mean, var)
                need(pe, s.rounded, b + 1)
                need(pe, s.w_kept, 1)
                pe.matmul(c.ps[:, 4, :], W8T[:, :], XQ[:, :], start=True, stop=True).then_inc(s.o_done, 1)
                need(pe, s.o_summed, b + 1)
                ln_pe(pe, s, c, 2 * b + 1, Y[:, :], mean, var)

        @block.scalar
        def _(act):
            for b in range(CHUNKS):
                need(act, s.ct_turned, b + 1)
                need(act, s.y_done, b)
                act.activation(CT[:, :], c.ps[:, 0, :], ACT.Copy).then_inc(s.ct_kept, 1)
                ln_act(act, s, c, 2 * b, var, c.eps5[:, 0:1])
                ln_act(act, s, c, 2 * b + 1, var, c.eps5[:, 0:1])

        @block.vector
        def _(dve):
            dve.wait_ge(d.w, 80)
            dve.tensor_tensor(SIW[:, :], SI[:, :], SW[:, :], ALU.mult)
            dve.reciprocal(RSI[:, :], SI[:, :]).then_inc(s.scale, 1)
            need(dve, s.scale, 1)
            need(dve, s.w_turned, 1)
            dve.tensor_copy(W8T[:, :], c.ps[:, 5, 0:P]).then_inc(s.w_kept, 1)
            for b in range(CHUNKS):
                need(dve, s.y_done, b + 1)
                dve.tensor_tensor(Y[:, :], c.ps[:, 1, :], xa(b), ALU.add).then_inc(s.summed, 1)
                ln_dve(dve, s, c, 2 * b, Y[:, :], mean, X1[:, :])
                need(dve, s.ln_done, 2 * b + 1)
                need(dve, s.o_done, b)
                dve.tensor_scalar(XQ[:, :], X1[:, :], RSI[:, 0:1], 448.0, ALU.mult, ALU.min).then_inc(s.clipped, 1)
                need(dve, s.clipped, b + 1)
                dve.tensor_scalar(XQ[:, :], XQ[:, :], -448.0, None, ALU.max).then_inc(s.low, 1)
                need(dve, s.low, b + 1)
                dve.tensor_scalar(UNIT[:, :].bitcast(U32), XQ[:, :].bitcast(U32), 0x7F800000, None,
                                  ALU.bitwise_and).then_inc(s.bits, 1)
                need(dve, s.bits, b + 1)
                dve.tensor_scalar(UNIT[:, :], UNIT[:, :], 2.0 ** -6, 1.5 * 2.0 ** 20, ALU.max, ALU.mult).then_inc(s.unit, 1)
                need(dve, s.unit, b + 1)
                dve.tensor_tensor(XQ[:, :], XQ[:, :], UNIT[:, :], ALU.add).then_inc(s.magic, 1)
                need(dve, s.magic, b + 1)
                dve.tensor_tensor(XQ[:, :], XQ[:, :], UNIT[:, :], ALU.subtract).then_inc(s.rounded, 1)
                need(dve, s.o_done, b + 1)
                dve.tensor_scalar(Y[:, :], c.ps[:, 4, :], SIW[:, 0:1], BIAS[:, 0:1], ALU.mult, ALU.add).then_inc(s.o_kept, 1)
                need(dve, s.o_kept, b + 1)
                dve.tensor_tensor(Y[:, :], Y[:, :], X1[:, :], ALU.add).then_inc(s.o_summed, 1)
                ln_dve(dve, s, c, 2 * b + 1, Y[:, :], mean, xa(b))
                need(dve, s.ln_done, 2 * b + 2)


AttentionBuffers = namedtuple("AttentionBuffers", "va ctx")


def attention_and_quant(nc, c, t):
    q_stack = nc.dram_tensor("q_stack", (AHEADS, USED, T), BF16, kind="Internal").ap()
    k_stack = nc.dram_tensor("k_stack", (AHEADS, USED, T), BF16, kind="Internal").ap()
    with ExitStack() as ctx:
        m = AttentionBuffers(va=ctx.enter_context(nc.sbuf_tensor("va", [P, TILES, AHEADS, VW], F32)),
                            ctx=ctx.enter_context(nc.sbuf_tensor("ctx", [P, TILES, P], F32)))
        project_phase(nc, c, m, t["L0_attn_W_DKV"], t["L0_attn_W_UK"], t["L0_attn_W_UV"], t["L0_attn_W_UQ"],
                      t["c_ones_rows"], q_stack, k_stack)
        causal_phase(nc, c, m, q_stack, k_stack, t["c_mask_qk"], t["c_mask_kq"])
        quant_phase(nc, c, m, t["L0_attn_W_O"], t["L0_ffn_weight_fp8"], t["L0_ffn_bias"], t["L0_ffn_input_scale"],
                    t["L0_ffn_weight_scale"])



DT_RANK = 64
STATES = 16
BC = 2 * STATES
UNITS_SSM = 2 * STATES
SSM_COUNTERS = ("affined proj pkept sig_e sig_d sig_r gate vproj vkept vabs vexp vlog soft dtproj dtkept dlproj "
                "bcproj bckept bc_hi bc_rest bc_mid bc_done dx uskip b_done c_done da_done dbu_done scanned carried "
                "hc_done y_acc y_gated total copied " + LN_NAMES)


def ssm_phase(nc, c, x3, t):
    with ExitStack() as ctx:
        def sb(name, shape, dt=F32):
            return ctx.enter_context(nc.sbuf_tensor("sm_" + name, shape, dt))

        WP = sb("WP", [P, P])
        WU = sb("WU", [P, 2, P])
        WX = sb("WX", [P, 2, DT_RANK])
        WBC = sb("WBC", [P, 2, 3 * BC])
        WDT = sb("WDT", [DT_RANK, 2, P])
        VEC = sb("VEC", [P, 9])
        BX = sb("BX", [DT_RANK, 2])
        BBC = sb("BBC", [3 * BC, 2])
        AL = sb("AL", [P, 2, STATES])
        SEL = sb("SEL", [3 * BC, BC, P], BF16)
        XN = sb("XN", [P, CH])
        PJ = sb("PJ", [P, CH])
        SG = sb("SG", [P, CH])
        Z = sb("Z", [P, CH])
        VB = sb("VB", [P, 2, CH])
        VA = sb("VA", [P, 2, CH])
        VL = sb("VL", [P, 2, CH])
        U = sb("U", [P, 2, CH])
        DT = sb("DT", [DT_RANK, 2, CH])
        DL = sb("DL", [P, 2, CH])
        DX = sb("DX", [P, 2, CH])
        BCF = sb("BCF", [3 * BC, 2, CH])
        BCR = sb("BCR", [3 * BC, 2, CH])
        BCM = sb("BCM", [3 * BC, 2, CH], BF16)
        BCS = sb("BCS", [3 * BC, 2, CH], BF16)
        ACC = sb("ACC", [P, CH])
        Y = sb("Y", [P, CH])
        DA = sb("DA", [P, 2, CH])
        DBU = sb("DBU", [P, 2, CH])
        HS = sb("HS", [P, 2, CH])
        HL = sb("HL", [P, UNITS_SSM])
        HC = sb("HC", [P, 2, CH])
        s = Counters(nc, ctx, "sm_", SSM_COUNTERS)
        start_counters(nc, s)
        d = Counters(nc, ctx, "smd_", "w alog a")
        LOADS = 5 + 2 * 14
        B_BANK, C_BANK = (0, 1, 4), (2, 3, 7)
        mean, var = c.ps[:, 5, :], c.ps[:, 6, :]
        pre = (c.ps[:, 4, :], c.ps[:, 7, :])
        block = ctx.enter_context(nc.Block())
        col = lambda a: a.rearrange("(p a) -> p a", a=1)

        @block.sync
        def _(sp):
            loads = [(WP[:, :], t["W_proj"]), (VEC[:, 0:1], col(t["gamma"])), (VEC[:, 1:2], col(t["beta"])),
                     (VEC[:, 2:3], col(t["b_proj"])), (SEL[:, :, :], t["c_select"])]
            for k, (wu, bu) in enumerate((("W_fc", "b_fc"), ("W_bc", "b_bc"))):
                i = str(k + 1)
                loads += [(WU[:, k, :], t[wu]), (VEC[:, 3 + 3 * k:4 + 3 * k], col(t[bu])),
                          (VEC[:, 4 + 3 * k:5 + 3 * k], col(t["b_dt" + i])), (VEC[:, 5 + 3 * k:6 + 3 * k], col(t["D" + i])),
                          (WX[:, k, :], t["W_x" + i][:, 0:DT_RANK]), (WDT[:, k, :], t["W_dt" + i]),
                          (BX[:, k:k + 1], col(t["b_x" + i][0:DT_RANK])), (AL[:, k, :], t["A_log" + i])]
                for r in range(3):
                    loads += [(WBC[:, k, BC * r:BC * (r + 1)], t["W_x" + i][:, DT_RANK:DT_RANK + BC]),
                              (BBC[BC * r:BC * (r + 1), k:k + 1], col(t["b_x" + i][DT_RANK:DT_RANK + BC]))]
            for dst, src in loads:
                sp.dma_start(dst, src).then_inc(d.w, 16)
            assert len(loads) == LOADS

        @block.gpsimd
        def _(pool):
            pool.memset(HL[:, :], 0.0).then_inc(d.a, 1)
            with pool.Fori(0, CHUNKS) as b:
                for i in range(UNITS_SSM):
                    need(pool, s.hc_done, b * UNITS_SSM + i + 1)
                    if i == 0:
                        need(pool, s.uskip, b * 2 + 2)
                        need(pool, s.y_gated, b)
                    need(pool, s.y_acc, b * UNITS_SSM + i)
                    pool.tensor_tensor(Y[:, :], (ACC if i == 0 else Y)[:, :], HC[:, i % 2, :], ALU.add).then_inc(s.y_acc, 1)
                need(pool, s.ln_done, b * 2 + 2)
                pool.tensor_copy(x3[:, bass.ds(b * CH, CH)], c.xa[:, bass.ds(b * CH + 1, CH)]).then_inc(s.copied, 1)

        @block.tensor
        def _(pe):
            pe.wait_ge(d.w, 16 * LOADS)

            def spread(b, i):
                k, n, g = i // STATES, i % STATES, b * UNITS_SSM + i
                if i == 2:
                    need(pe, s.vkept, b * 2 + 2)
                need(pe, s.dbu_done, g - 2)
                pe.matmul(c.ps[:, B_BANK[i % 3], :], SEL[:, n, :], BCS[:, k, :], start=True, stop=True).then_inc(s.b_done, 1)
                need(pe, s.hc_done, g - 2)
                pe.matmul(c.ps[:, C_BANK[i % 3], :], SEL[:, STATES + n, :], BCS[:, k, :], start=True, stop=True).then_inc(s.c_done, 1)

            with pe.Fori(0, CHUNKS) as b:
                x = c.xa[:, bass.ds(b * CH + 1, CH)]
                ln_pe(pe, s, c, b * 2, x, mean, var)
                need(pe, s.affined, b + 1)
                pe.matmul(pre[0], WP[:, :], XN[:, :], start=True, stop=True).then_inc(s.proj, 1)
                need(pe, s.pkept, b + 1)
                for k in range(2):
                    pe.matmul(pre[k], WU[:, k, :], PJ[:, :], start=True, stop=True).then_inc(s.vproj, 1)
                need(pe, s.soft, b * 2 + 1)
                for k, bank in enumerate((mean, var)):
                    pe.matmul(pre[k][0:DT_RANK, :], WX[:, k, :], U[:, k, :], start=True, stop=True).then_inc(s.dtproj, 1)
                    pe.matmul(bank[0:3 * BC, :], WBC[:, k, :], U[:, k, :], start=True, stop=True).then_inc(s.bcproj, 1)
                for k in range(2):
                    need(pe, s.dtkept, b * 2 + k + 1)
                    pe.matmul(pre[k], WDT[:, k, :], DT[:, k, :], start=True, stop=True).then_inc(s.dlproj, 1)
                need(pe, s.bc_done, b + 1)
                for i in range(UNITS_SSM):
                    spread(b, i)
                need(pe, s.total, b + 1)
                ln_pe(pe, s, c, b * 2 + 1, ACC[:, :], mean, var)

        @block.scalar
        def _(act):
            act.wait_ge(d.w, 16 * LOADS)
            act.wait_ge(d.a, 1)
            act.activation(AL[:, :, :], AL[:, :, :], ACT.Exp).then_inc(d.alog, 1)
            act.wait_ge(d.alog, 1)
            act.activation(AL[:, :, :], AL[:, :, :], ACT.Copy, scale=-1.0).then_inc(d.alog, 1)
            act.wait_ge(d.alog, 2)

            with act.Fori(0, CHUNKS) as b:
                ln_act(act, s, c, b * 2, var, c.eps6[:, 0:1])
                need(act, s.proj, b + 1)
                act.activation(PJ[:, :], pre[0], ACT.Identity, bias=VEC[:, 2:3]).then_inc(s.pkept, 1)
                need(act, s.pkept, b + 1)
                act.activation(SG[:, :], PJ[:, :], ACT.Exp, scale=-1.0).then_inc(s.sig_e, 1)
                for i, (ready, bias) in enumerate(((s.vproj, 3), (s.dlproj, 4))):
                    g = b * 2 + i
                    need(act, s.soft, g)
                    for k in range(2):
                        need(act, ready, b * 2 + k + 1)
                        mm = act.activation(VB[:, k, :], pre[k], ACT.Identity, bias=VEC[:, bias + 3 * k:bias + 3 * k + 1])
                    mm.then_inc(s.vkept, 1)
                    need(act, s.vkept, g + 1)
                    act.activation(VA[:, :, :], VB[:, :, :], ACT.Abs).then_inc(s.vabs, 1)
                    need(act, s.vabs, g + 1)
                    act.activation(VL[:, :, :], VA[:, :, :], ACT.Exp, scale=-1.0).then_inc(s.vexp, 1)
                    need(act, s.vexp, g + 1)
                    act.activation(VL[:, :, :], VL[:, :, :], ACT.Ln, bias=1.0).then_inc(s.vlog, 1)
                    if i == 0:
                        for k in range(2):
                            need(act, s.dtproj, b * 2 + k + 1)
                            act.activation(DT[:, k, :], pre[k][0:DT_RANK, :], ACT.Identity, bias=BX[:, k:k + 1]).then_inc(s.dtkept, 1)
                        need(act, s.bc_done, b)
                        for k, bank in enumerate((mean, var)):
                            need(act, s.bcproj, b * 2 + k + 1)
                            mm = act.activation(BCF[:, k, :], bank[0:3 * BC, :], ACT.Identity, bias=BBC[:, k:k + 1])
                        mm.then_inc(s.bckept, 1)
                need(act, s.soft, b * 2 + 2)
                for i in range(UNITS_SSM):
                    k, n, g = i // STATES, i % STATES, b * UNITS_SSM + i
                    need(act, s.scanned, g - 1)
                    act.activation(DA[:, i % 2, :], DL[:, k, :], ACT.Exp, scale=AL[:, k, n:n + 1]).then_inc(s.da_done, 1)
                ln_act(act, s, c, b * 2 + 1, var, c.eps5[:, 0:1])

        @block.vector
        def _(dve):
            dve.wait_ge(d.w, 16 * LOADS)
            dve.wait_ge(d.a, 1)

            def times_b(b, i):
                g = b * UNITS_SSM + i
                need(dve, s.b_done, g + 1)
                need(dve, s.scanned, g - 1)
                dve.tensor_tensor(DBU[:, i % 2, :], c.ps[:, B_BANK[i % 3], :], DX[:, i // STATES, :], ALU.mult).then_inc(s.dbu_done, 1)

            def scan(b, i):
                g = b * UNITS_SSM + i
                need(dve, s.carried, g - 1)
                need(dve, s.hc_done, g - 1)
                need(dve, s.dbu_done, g + 1)
                need(dve, s.da_done, g + 1)
                dve.tensor_tensor_scan(HS[:, i % 2, :], DA[:, i % 2, :], DBU[:, i % 2, :], HL[:, i:i + 1],
                                       ALU.mult, ALU.add).then_inc(s.scanned, 1)

            def times_c(b, i):
                g = b * UNITS_SSM + i
                need(dve, s.scanned, g + 1)
                dve.tensor_copy(HL[:, i:i + 1], HS[:, i % 2, CH - 1:CH]).then_inc(s.carried, 1)
                need(dve, s.c_done, g + 1)
                need(dve, s.y_acc, g - 1)
                dve.tensor_tensor(HC[:, i % 2, :], c.ps[:, C_BANK[i % 3], :], HS[:, i % 2, :], ALU.mult).then_inc(s.hc_done, 1)

            with dve.Fori(0, CHUNKS) as b:
                x = c.xa[:, bass.ds(b * CH + 1, CH)]
                ln_dve(dve, s, c, b * 2, x, mean, XN[:, :])
                need(dve, s.ln_done, b * 2 + 1)
                dve.tensor_scalar(XN[:, :], XN[:, :], VEC[:, 0:1], VEC[:, 1:2], ALU.mult, ALU.add).then_inc(s.affined, 1)
                need(dve, s.vlog, b * 2 + 1)
                dve.scalar_tensor_tensor(U[:, :, :], VB[:, :, :], 0.0, VL[:, :, :], ALU.max, ALU.add).then_inc(s.soft, 1)
                need(dve, s.bckept, b + 1)
                dve.tensor_copy(BCS[:, :, :], BCF[:, :, :]).then_inc(s.bc_hi, 1)
                need(dve, s.bc_hi, b + 1)
                for i in (1, 2):
                    rows = slice(BC * i, BC * (i + 1))
                    mm = dve.tensor_tensor(BCR[rows, :, :], BCF[rows, :, :], BCS[rows, :, :], ALU.subtract)
                mm.then_inc(s.bc_rest, 1)
                need(dve, s.bc_rest, b + 1)
                dve.tensor_copy(BCS[BC:2 * BC, :, :], BCR[BC:2 * BC, :, :])
                dve.tensor_copy(BCM[2 * BC:3 * BC, :, :], BCR[2 * BC:3 * BC, :, :]).then_inc(s.bc_mid, 1)
                need(dve, s.bc_mid, b + 1)
                dve.tensor_tensor(BCS[2 * BC:3 * BC, :, :], BCR[2 * BC:3 * BC, :, :], BCM[2 * BC:3 * BC, :, :],
                                  ALU.subtract).then_inc(s.bc_done, 1)
                need(dve, s.sig_e, b + 1)
                dve.tensor_scalar(SG[:, :], SG[:, :], 1.0, None, ALU.add).then_inc(s.sig_d, 1)
                need(dve, s.sig_d, b + 1)
                dve.reciprocal(SG[:, :], SG[:, :]).then_inc(s.sig_r, 1)
                need(dve, s.sig_r, b + 1)
                dve.tensor_tensor(Z[:, :], SG[:, :], PJ[:, :], ALU.mult).then_inc(s.gate, 1)
                need(dve, s.vlog, b * 2 + 2)
                dve.scalar_tensor_tensor(DL[:, :, :], VB[:, :, :], 0.0, VL[:, :, :], ALU.max, ALU.add).then_inc(s.soft, 1)
                need(dve, s.soft, b * 2 + 2)
                dve.tensor_tensor(DX[:, :, :], DL[:, :, :], U[:, :, :], ALU.mult).then_inc(s.dx, 1)
                need(dve, s.dx, b + 1)
                dve.tensor_scalar(ACC[:, :], U[:, 0, :], VEC[:, 5:6], None, ALU.mult).then_inc(s.uskip, 1)
                need(dve, s.uskip, b * 2 + 1)
                dve.scalar_tensor_tensor(ACC[:, :], U[:, 1, :], VEC[:, 8:9], ACC[:, :], ALU.mult, ALU.add).then_inc(s.uskip, 1)
                for i in range(UNITS_SSM + 2):
                    if i < UNITS_SSM:
                        times_b(b, i)
                    if 1 <= i <= UNITS_SSM:
                        scan(b, i - 1)
                    if i >= 2:
                        times_c(b, i - 2)
                need(dve, s.y_acc, b * UNITS_SSM + UNITS_SSM)
                dve.tensor_tensor(ACC[:, :], Y[:, :], Z[:, :], ALU.mult).then_inc(s.y_gated, 1)
                need(dve, s.y_gated, b + 1)
                dve.scalar_tensor_tensor(ACC[:, :], x, 2.0, ACC[:, :], ALU.mult, ALU.add).then_inc(s.total, 1)
                need(dve, s.total, b + 1)
                ln_dve(dve, s, c, b * 2 + 1, ACC[:, :], mean, x)
                need(dve, s.ln_done, b * 2 + 2)



LAYERS = 6
HEADS = 16
DH = 64
INNER = HEADS * DH
WIN = 32
KEYS = P + WIN
GROUPS = 4
GH = HEADS // GROUPS
GD = GH * DH
HID = 341
HPART = [(0, 128), (128, 128), (256, HID - 256)]
AHEAD = 4

SHIFT, MEAN, VAR, SPREAD, GATE, VAL, DOWN = 0, 2, 3, 4, (5, 6, 7), (9, 10, 11), 12
PIECES = 13

LOCAL_COUNTERS = ("xs_staged tab_ready qk_done v_done squared v_kept summed roped clamped norm_a "
                  "k_scaled rotated kprev turned qk_kept scored maxed biased exped prev_turned p_turned pt_kept "
                  "attended recipd normed o_turned o_kept projected resid shifted affined gelud gate "
                  "val vprev_kept gated down ffn_done gate_kept ln_mean ln_centered ln_squared ln_var "
                  "ln_eps ln_rstd scaled ln_diag ln_spread ln_done")


def local_phase(nc, c, wqkv, q_scale, k_scale, wo, ln_g, ln_b, w1, b1, w2, b2, rope, mask, kfac):
    with ExitStack() as ctx:
        def sb(name, shape, dt=F32):
            return ctx.enter_context(nc.sbuf_tensor("lo_" + name, shape, dt))

        W = sb("W", [P, GROUPS, 3 * GD])
        WO = sb("WO", [P, INNER // P, P])
        W1 = sb("W1", [P, 2 * HID])
        W2 = sb("W2", [P, 3, P])
        B1 = sb("B1", [P, 2, 3])
        VEC = sb("VEC", [P, 3])
        QS = sb("QS", [P, 4 * DH])
        ROPE = sb("ROPE", [P, TILES, 4 * DH])
        TAB = sb("TAB", [P, 4 * DH])
        MASK = sb("MASK", [P, TILES + 1, KEYS], BF16)
        KFAC = sb("KFAC", [P, 1])
        XS = sb("XS", [P, 2, P])
        SQ = sb("SQ", [P, 2, 2 * GD])
        SS = sb("SS", [P, 2, 2 * GH])
        SSM = sb("SSM", [P, 2, 2 * GH])
        MHALF = sb("MHALF", [P, 1])
        A = sb("A", [P, GROUPS, 2 * GH])
        TB = sb("TB", [P, 2, 2 * GD])
        RB = sb("RB", [P, 2, 2 * GD])
        QT = sb("QT", [P, 2, 2, P])
        KT = sb("KT", [P, GROUPS, 2, KEYS])
        V = sb("V", [P, GROUPS, GD])
        VP = sb("VP", [WIN, GROUPS, GD])
        NM = sb("NM", [P, 2, GH])
        NB = sb("NB", [P, 2, GH])
        PR = sb("PR", [P, 2, GH, KEYS])
        RS = sb("RS", [P, 2, GH])
        RI = sb("RI", [P, GH])
        PP = sb("PP", [WIN, 2, GH * WIN])
        PTS = sb("PTS", [P, 2, GH * P])
        ON = sb("ON", [P, GD])
        OTS = sb("OTS", [P, INNER // P, P])
        XS2 = sb("XS2", [P, CH])
        XN = sb("XN", [P, CH])
        VE = sb("VE", [P, 4])
        RV = sb("RV", [P, 4])
        DIAG = sb("DIAG", [P, 4, P])
        ONES = sb("ONES", [P, P])
        GT = sb("GT", [P, 3, CH])
        H = sb("H", [P, 3, CH])

        s = Counters(nc, ctx, "lo_", LOCAL_COUNTERS)
        start_counters(nc, s)
        d = Counters(nc, ctx, "lod_", "const w wo ffn vec qs")
        N_FFN = 6 + 6

        QK_B, T_B, PT_B, O_B = 0, 1, 6, 7

        def s_bank(par):
            return c.ps[:, 2 + 2 * par:4 + 2 * par, 0:2 * KEYS].rearrange("p h (b k) -> p b h k", b=2)

        y_bank = c.ps[:, T_B, 0:P]
        o_bank = c.ps[:, O_B, 0:GD]
        ot_bank = c.ps[:, O_B, 0:GD].rearrange("p (b t) -> p b t", b=2)
        v_bank = c.ps[:, T_B, P:P + GD]
        pt_bank = c.ps[:, PT_B, :]
        f_bank = c.ps[:, PT_B, :]

        def chunks(eng, chunk):
            load = 16 * N_FFN
            chunk(0, 0, None)
            with eng.Fori(1, CHUNKS) as ch:
                chunk(0, ch, (ch - 1, ch - 1, load))
            with eng.Fori(1, LAYERS) as l:
                chunk(l, 0, (l * CHUNKS - 1, CHUNKS - 1, l * load))
                with eng.Fori(1, CHUNKS) as ch:
                    chunk(l, ch, (l * CHUNKS + ch - 1, ch - 1, l * load + load))

        LAST = (LAYERS * CHUNKS - 1, CHUNKS - 1, LAYERS * 16 * N_FFN)

        block = ctx.enter_context(nc.Block())

        @block.sync
        def _(sp):
            sp.dma_start(ROPE[:, :, :], rope).then_inc(d.const, 16)
            sp.dma_start(MASK[:, :, :], mask).then_inc(d.const, 16)
            sp.dma_start(KFAC[:, :], kfac).then_inc(d.const, 16)

            def layer(l, first):
                for part, src in enumerate((q_scale, k_scale)):
                    row = src[bass.ds(l, 1), :]
                    if part == 0 and not first:
                        need(sp, s.tab_ready, 16 * l)
                    sp.dma_start(QS[:, part * DH:(part + 1) * DH], row.broadcast_to([P, DH])).then_inc(d.qs, 16)
                    for h in range(2):
                        o = (2 + part) * DH + h * (DH // 2)
                        sp.dma_start(QS[:, o:o + DH // 2],
                                     src[bass.ds(l, 1), (1 - h) * (DH // 2):(2 - h) * (DH // 2)]
                                     .broadcast_to([P, DH // 2])).then_inc(d.qs, 16)
                for g in range(GROUPS):
                    if not first:
                        need(sp, s.v_done, 64 * l - 3 + g)
                    src = wqkv[bass.ds(l, 1), :, :].rearrange("a p (b n) -> p (a b) n", b=3)
                    sp.dma_start(W[:, g, :].rearrange("p (b n) -> p b n", b=3),
                                 src[:, :, GD * g:GD * (g + 1)]).then_inc(d.w, 16)
                if not first:
                    need(sp, s.projected, 16 * l)
                sp.dma_start(WO[:, :, :], wo[bass.ds(l, 1), :, :].rearrange("a (k p) n -> p (a k) n", p=P)).then_inc(d.wo, 16)
                if not first:
                    need(sp, s.ffn_done, 4 * l)
                sp.dma_start(W1[:, :], w1[bass.ds(l, 1), :, :].rearrange("a p n -> (a p) n")).then_inc(d.ffn, 16)
                sp.dma_start(W2[:, 0:2, :], w2[bass.ds(l, 1), 0:256, :].rearrange("a (k p) n -> p (a k) n", p=P)).then_inc(d.ffn, 16)
                sp.dma_start(W2[0:HID - 256, 2, :], w2[bass.ds(l, 1), 256:HID, :].rearrange("a p n -> (a p) n")).then_inc(d.ffn, 16)
                for i, src in enumerate((ln_g, ln_b, b2)):
                    sp.dma_start(VEC[:, i:i + 1], src[bass.ds(l, 1), :].rearrange("a p -> p a")).then_inc(d.ffn, 16)
                for half in range(2):
                    for j, (h0, w) in enumerate(HPART):
                        sp.dma_start(B1[0:w, half, j:j + 1],
                                     b1[bass.ds(l, 1), half * HID + h0:half * HID + h0 + w].rearrange("a p -> p a")).then_inc(d.ffn, 16)

            layer(0, True)
            with sp.Fori(1, LAYERS) as l:
                layer(l, False)

        @block.gpsimd
        def _(pool):
            pool.memset(MHALF[:, :], -0.5)
            pool.memset(ONES[:, :], 1.0)
            pool.memset(VP[:, :, :], 0.0)
            pool.memset(KT[:, :, :, :], 0.0).then_inc(d.vec, 1)
            pool.wait_ge(d.const, 48)
            pool.wait_ge(d.vec, 1)

            def piece(p, ffn):
                k, fch, load = ffn
                if p == SHIFT:
                    need(pool, s.resid, k * 4 + 4)
                    need(pool, s.ln_centered, k)
                    for rows, first in ((slice(0, 64), 1), (slice(64, P), 0)):
                        m = pool.tensor_tensor(XS2[rows, :], c.xb[rows, bass.ds(fch * CH + first, CH)],
                                               ONES[rows, 0:1].to_broadcast([64, CH]), ALU.mult)
                    m.then_inc(s.shifted, 1)
                    need(pool, s.shifted, k + 1)
                if p == VAR:
                    need(pool, s.ln_eps, k + 1)
                    pool.tensor_tensor(RV[:, :], VE[:, :], MHALF[:, 0:1].to_broadcast([P, 4]), ALU.pow).then_inc(s.ln_rstd, 1)
                    need(pool, s.ln_rstd, k + 1)
                    need(pool, s.ln_spread, k)
                    pool.tensor_tensor(DIAG[:, :, :], c.ident[:, :].unsqueeze(1).to_broadcast([P, 4, P]),
                                       RV[:, :].unsqueeze(2).to_broadcast([P, 4, P]), ALU.mult).then_inc(s.ln_diag, 1)
                if p == SPREAD:
                    pool.wait_ge(d.ffn, load)
                    need(pool, s.ln_done, k + 1)
                    pool.tensor_tensor(XN[:, :], XN[:, :], VEC[:, 0:1].to_broadcast([P, CH]), ALU.mult).then_inc(s.scaled, 1)
                    need(pool, s.scaled, k + 1)
                    pool.tensor_tensor(XN[:, :], XN[:, :], VEC[:, 1:2].to_broadcast([P, CH]), ALU.add).then_inc(s.affined, 1)

            def stage(n, t, slot, chunk_count, scaled):
                need(pool, s.v_done, n * 4 - 4)
                need(pool, s.ffn_done, chunk_count - 3)
                need(pool, s.k_scaled, scaled)
                for rows, first in ((slice(0, 64), 1), (slice(64, P), 0)):
                    m = pool.tensor_tensor(XS[rows, slot, :], c.xa[rows, bass.ds(t * P + first, P)],
                                           ONES[rows, 0:1].to_broadcast([64, P]), ALU.mult)
                m.then_inc(s.xs_staged, 1)
                need(pool, s.xs_staged, n + 1)

            def tile(l, ch, j, ffn=None, beyond=False):
                n = (l * CHUNKS + ch) * 4 + j
                t = ch * 4 + j
                if not beyond:
                    pool.wait_ge(d.w, l * (16 * GROUPS) + 16 * GROUPS)
                    pool.wait_ge(d.qs, l * 96 + 96)
                if j == 0 or beyond:
                    stage(n, t, 0, l * CHUNKS + ch, n * 4)
                need(pool, s.roped, n * 4)
                pool.tensor_tensor(TAB[:, :], ROPE[:, bass.ds(t, 1), :].rearrange("p a b -> p (a b)"),
                                   QS[:, :], ALU.mult).then_inc(s.tab_ready, 1)
                for g in range(GROUPS):
                    G, par = n * 4 + g, g % 2
                    need(pool, s.scored, G - 3)
                    pool.tensor_tensor(KT[:, g, :, 0:WIN], KT[:, g, :, P:KEYS],
                                       KFAC[:, :].unsqueeze(2).to_broadcast([P, 2, WIN]), ALU.mult).then_inc(s.kprev, 1)
                    need(pool, s.roped, G + 1)
                    pool.tensor_tensor(TB[:, par, :], TB[:, par, :], RB[:, par, :], ALU.add).then_inc(s.rotated, 1)
                    need(pool, s.clamped, G + 1)
                    need(pool, s.exped, G - 3)
                    pool.tensor_tensor(A[:, g, :], SSM[:, par, :], MHALF[:, 0:1].to_broadcast([P, 2 * GH]),
                                       ALU.pow).then_inc(s.norm_a, 1)
                    need(pool, s.norm_a, G + 1)
                    need(pool, s.rotated, G + 1)
                    a_k = A[:, g, GH:2 * GH].unsqueeze(2).to_broadcast([P, GH, DH])
                    k = TB[:, par, GD:2 * GD].rearrange("p (h e) -> p h e", h=GH)
                    pool.tensor_tensor(k, k, a_k, ALU.mult).then_inc(s.k_scaled, 1)
                    if ffn is not None:
                        p = 4 * (j - 1) + g
                        if p == SHIFT:
                            need(pool, s.k_scaled, G + 1)
                        piece(p, ffn)
                    if g == 2 and j < 3 and not beyond:
                        stage(n + 1, t + 1, (j + 1) % 2, l * CHUNKS + ch, G + 1)

            def chunk(l, ch, ffn):
                for j in range(4):
                    tile(l, ch, j, ffn)

            chunks(pool, chunk)
            tile(LAYERS, 0, 0, beyond=True)
            need(pool, s.k_scaled, (LAYERS * TILES + 1) * GROUPS)
            for p in range(PIECES):
                piece(p, LAST)

        @block.tensor
        def _(pe):
            pe.wait_ge(d.const, 48)
            pe.wait_ge(d.vec, 1)

            def proj_v(G, slot, g):
                need(pe, s.v_kept, G)
                need(pe, s.qk_kept, G)
                pe.matmul(v_bank, XS[:, slot, :], W[:, g, 2 * GD:3 * GD], start=True, stop=True).then_inc(s.v_done, 1)

            def proj_qk(G, n, slot, g):
                need(pe, s.xs_staged, n + 1)
                need(pe, s.roped, G)
                pe.matmul(c.ps[:, QK_B, :], XS[:, slot, :], W[:, g, 0:2 * GD], start=True, stop=True).then_inc(s.qk_done, 1)

            def turn(G, n, par):
                need(pe, s.k_scaled, G + 1)
                need(pe, s.resid, n)
                need(pe, s.v_kept, G + 1)
                need(pe, s.qk_kept, G)
                for b in range(4):
                    m = pe.transpose(c.ps[:, T_B, b * P:(b + 1) * P], TB[:, par, b * P:(b + 1) * P], c.ident[:, :])
                m.then_inc(s.turned, 1)

            def masks(G, t, par):
                need(pe, s.exped, G - 1)
                for h in range(2):
                    for b in range(2):
                        pe.matmul(s_bank(par)[:, b, h, :], c.ident_bf[:, :],
                                  MASK[:, bass.ds(t, 1), :].rearrange("p a k -> p (a k)"),
                                  start=(b == 0), stop=False, skip_group_check=True)

            def score(G, g, par):
                need(pe, s.qk_kept, G + 1)
                for b in range(2):
                    for h in range(2):
                        m = pe.matmul(s_bank(par)[:, b, h, :], QT[64 * h:64 * h + 64, par, b, :],
                                      KT[64 * h:64 * h + 64, g, b, :], start=False, stop=(b == 1),
                                      skip_group_check=True)
                m.then_inc(s.scored, 1)

            def pturn(G, par, p, ffn):
                need(pe, s.exped, G + 1)
                need(pe, s.pt_kept, G)
                if ffn is not None:
                    piece_left(p - 1, ffn)
                for h in range(GH):
                    m = pe.transpose(pt_bank[:, h * P:(h + 1) * P], PR[:, par, h, WIN:KEYS], c.ident[:, :])
                m.then_inc(s.p_turned, 1)

            def attend(G, g, par):
                need(pe, s.pt_kept, G + 1)
                need(pe, s.prev_turned, G + 1)
                need(pe, s.v_kept, G + 1)
                need(pe, s.o_kept, G)
                need(pe, s.vprev_kept, G - 3)
                for h in range(GH):
                    pe.matmul(o_bank[:, h * DH:(h + 1) * DH], PTS[:, par, h * P:(h + 1) * P],
                              V[:, g, h * DH:(h + 1) * DH], start=(h == 0), stop=False, skip_group_check=True)
                for h in range(GH):
                    m = pe.matmul(o_bank[0:WIN, h * DH:(h + 1) * DH], PP[:, par, h * WIN:(h + 1) * WIN],
                                  VP[:, g, h * DH:(h + 1) * DH], start=False, stop=(h == GH - 1),
                                  skip_group_check=True)
                m.then_inc(s.attended, 1)

            def oturn(G):
                need(pe, s.normed, G + 1)
                for b in range(2):
                    m = pe.transpose(ot_bank[:, b, :], ON[:, b * P:(b + 1) * P], c.ident[:, :])
                m.then_inc(s.o_turned, 1)

            def project(n, l):
                need(pe, s.o_kept, 4 * n + 4)
                pe.wait_ge(d.wo, 16 * l + 16)
                for k in range(INNER // P):
                    m = pe.matmul(y_bank, WO[:, k, :], OTS[:, k, :], start=(k == 0), stop=(k == INNER // P - 1))
                m.then_inc(s.projected, 1)

            def piece_left(p, ffn):
                k = ffn[0]
                if p == MEAN:
                    need(pe, s.ln_centered, k + 1)
                if p == VAR:
                    need(pe, s.ln_eps, k + 1)
                if p == SPREAD:
                    need(pe, s.ln_done, k + 1)
                if p in GATE:
                    need(pe, s.gate_kept, k * 3 + (GATE.index(p) + 1))
                if p in VAL:
                    need(pe, s.gated, k * 3 + (VAL.index(p) + 1))
                if p == DOWN:
                    need(pe, s.ffn_done, k + 1)

            def piece(p, ffn):
                k, fch, load = ffn
                piece_left(p - 1, ffn)
                if p == MEAN:
                    need(pe, s.shifted, k + 1)
                    pe.matmul(f_bank, c.avg[:, :], XS2[:, :], start=True, stop=True).then_inc(s.ln_mean, 1)
                if p == VAR:
                    need(pe, s.ln_squared, k + 1)
                    for i in range(4):
                        m = pe.matmul(f_bank[:, i:i + 1], c.ln_sq[:, i * P:(i + 1) * P], c.avg[:, 0:1],
                                      start=i == 0, stop=True, skip_group_check=True)
                    m.then_inc(s.ln_var, 1)
                if p == SPREAD:
                    need(pe, s.ln_diag, k + 1)
                    pe.matmul(f_bank, ONES[:, :], DIAG[:, :, :].rearrange("p a b -> p (a b)"),
                              start=True, stop=True).then_inc(s.ln_spread, 1)
                if p in GATE:
                    h0, w = HPART[GATE.index(p)]
                    if p == GATE[0]:
                        pe.wait_ge(d.ffn, load)
                        need(pe, s.affined, k + 1)
                    pe.matmul(f_bank[0:w, :], W1[:, HID + h0:HID + h0 + w], XN[:, :], start=True, stop=True).then_inc(s.gate, 1)
                if p in VAL:
                    h0, w = HPART[VAL.index(p)]
                    pe.matmul(f_bank[0:w, :], W1[:, h0:h0 + w], XN[:, :], start=True, stop=True).then_inc(s.val, 1)
                if p == DOWN:
                    for j, (h0, w) in enumerate(HPART):
                        m = pe.matmul(f_bank, W2[0:w, j, :], H[0:w, j, :], start=(j == 0), stop=(j == 2))
                    m.then_inc(s.down, 1)

            def step(n, t, g, l, slot, p=None, ffn=None, first=False):
                G = n * 4 + g
                if not first:
                    pturn(G, g % 2, p, ffn)
                proj_qk(G + AHEAD, n + 1, slot, g)
                if not first:
                    attend(G, g, g % 2)
                if not first or g >= 1:
                    turn(G + 3, n, (g + 3) % 2)
                if ffn is not None and p < PIECES:
                    piece(p, ffn)
                if not first or g >= 2:
                    masks(G + 2, t + (g + 2) // 4, g % 2)
                if not first:
                    oturn(G)
                if not first or g >= 2:
                    score(G + 2, (g + 2) % 4, g % 2)
                proj_v(G + AHEAD, slot, g)
                if not first and g == GROUPS - 1:
                    project(n, l)

            def chunk(l, ch, ffn):
                for j in range(4):
                    for g in range(GROUPS):
                        step((l * CHUNKS + ch) * 4 + j, ch * 4 + j, g, l, (j + 1) % 2, 4 * j + g, ffn)

            for g in range(GROUPS):
                step(-1, -1, g, 0, 0, first=True)
            chunks(pe, chunk)
            for p in range(PIECES):
                piece(p, LAST)

        @block.scalar
        def _(act):
            def square(G, par):
                need(act, s.qk_done, G + 1)
                need(act, s.summed, G - 1)
                act.activation(SQ[:, par, :], c.ps[:, QK_B, :], ACT.Square).then_inc(s.squared, 1)

            def keep(G, g, par):
                need(act, s.turned, G + 1)
                need(act, s.scored, G - 1)
                need(act, s.kprev, G + 1)
                act.activation(QT[:, par, :, :], c.ps[:, T_B, 0:GD].rearrange("p (b t) -> p b t", b=2), ACT.Copy)
                act.activation(KT[:, g, :, WIN:KEYS], c.ps[:, T_B, GD:2 * GD].rearrange("p (b t) -> p b t", b=2),
                               ACT.Copy).then_inc(s.qk_kept, 1)

            def exps(G, g, par):
                need(act, s.biased, G + 1)
                need(act, s.p_turned, G - 1)
                need(act, s.prev_turned, G - 1)
                need(act, s.recipd, G - 1)
                for h in range(GH):
                    m = act.activation(PR[:, par, h, :], s_bank(par)[:, h // 2, h % 2, :], ACT.Exp,
                                       bias=NB[:, par, h:h + 1], scale=A[:, g, h:h + 1],
                                       accum_out=RS[:, par, h:h + 1])
                m.then_inc(s.exped, 1)

            def pt_keep(G, par):
                need(act, s.p_turned, G + 1)
                need(act, s.attended, G - 1)
                act.activation(PTS[:, par, :], pt_bank, ACT.Copy).then_inc(s.pt_kept, 1)

            def piece(p, ffn):
                k, fch, load = ffn
                if p == MEAN:
                    need(act, s.ln_centered, k + 1)
                    need(act, s.ln_var, k)
                    act.activation(c.ln_sq[:, :], c.ln_cen[:, :], ACT.Square).then_inc(s.ln_squared, 1)
                if p in GATE:
                    j = GATE.index(p)
                    w = HPART[j][1]
                    if j == 0:
                        act.wait_ge(d.ffn, load)
                        need(act, s.gated, k * 3)
                    need(act, s.gate, k * 3 + (j + 1))
                    act.activation(GT[0:w, j, :], f_bank[0:w, :], ACT.Identity, bias=B1[0:w, 1, j:j + 1]).then_inc(s.gate_kept, 1)
                if p == GATE[-1]:
                    need(act, s.gate_kept, k * 3 + 3)
                    act.activation(GT[:, 0:2, :], GT[:, 0:2, :], ACT.Gelu)
                    act.activation(GT[0:w, 2, :], GT[0:w, 2, :], ACT.Gelu).then_inc(s.gelud, 1)

            def step(n, g, p=None, ffn=None, first=False):
                G = n * 4 + g
                if not first:
                    pt_keep(G, g % 2)
                square(G + AHEAD, g % 2)
                if not first or g == 3:
                    exps(G + 1, (g + 1) % 4, (g + 1) % 2)
                if not first or g >= 1:
                    keep(G + 3, (g + 3) % 4, (g + 3) % 2)
                if ffn is not None and p < PIECES:
                    piece(p, ffn)

            def chunk(l, ch, ffn):
                for j in range(4):
                    for g in range(GROUPS):
                        step((l * CHUNKS + ch) * 4 + j, g, 4 * j + g, ffn)

            for g in range(GROUPS):
                step(-1, g, first=True)
            chunks(act, chunk)
            for p in range(PIECES):
                piece(p, LAST)

        @block.vector
        def _(dve):
            def rope_qk(G, n, par):
                need(dve, s.squared, G + 1)
                need(dve, s.tab_ready, n + 1)
                need(dve, s.turned, G - 1)
                tab = TAB[:, :].rearrange("p (c q e) -> p c q e", c=2, q=2)
                qk = c.ps[:, QK_B, :].rearrange("p (q h e) -> p q h e", q=2, h=GH)
                dve.tensor_tensor(TB[:, par, :].rearrange("p (q h e) -> p q h e", q=2, h=GH), qk,
                                  tab[:, 0, :, :].unsqueeze(2).to_broadcast([P, 2, GH, DH]), ALU.mult)
                for q in range(2):
                    src = c.ps[:, QK_B, q * GD:(q + 1) * GD].rearrange("p (h a e) -> p h a e", h=GH, a=2)[:, :, ::-1, :]
                    dst = RB[:, par, q * GD:(q + 1) * GD].rearrange("p (h a e) -> p h a e", h=GH, a=2)
                    sin = tab[:, 1, q, :].rearrange("p (a e) -> p a e", a=2).unsqueeze(1).to_broadcast([P, GH, 2, DH // 2])
                    m = dve.tensor_tensor(dst, src, sin, ALU.mult)
                m.then_inc(s.roped, 1)

            def sums(G, par):
                dve.tensor_reduce(SS[:, par, :], SQ[:, par, :].rearrange("p (h e) -> p h e", e=DH), AX.X,
                                  ALU.add).then_inc(s.summed, 1)
                need(dve, s.norm_a, G - 1)
                need(dve, s.summed, G + 1)
                dve.tensor_scalar(SSM[:, par, :], SS[:, par, :], 1e-24, None, ALU.max).then_inc(s.clamped, 1)

            def v_keep(G, n, g, first):
                need(dve, s.v_done, G + 1)
                if not first and g == GROUPS - 1:
                    need(dve, s.projected, n + 1)
                if not first:
                    need(dve, s.attended, G - 3)
                    dve.tensor_copy(VP[:, g, :], V[P - WIN:P, g, :]).then_inc(s.vprev_kept, 1)
                    need(dve, s.vprev_kept, G - 3)
                dve.tensor_copy(V[:, g, :], v_bank).then_inc(s.v_kept, 1)

            def prev_turn(G, par):
                need(dve, s.exped, G + 1)
                need(dve, s.attended, G - 1)
                dve.transpose(PP[:, par, :].rearrange("p (h k) -> p h k", h=GH), PR[0:WIN, par, :, 0:WIN]).then_inc(s.prev_turned, 1)

            def recip(G, par):
                dve.reciprocal(RI[:, :], RS[:, par, :]).then_inc(s.recipd, 1)

            def normalize(G):
                need(dve, s.attended, G + 1)
                need(dve, s.recipd, G + 1)
                dve.tensor_tensor(ON[:, :].rearrange("p (h e) -> p h e", h=GH),
                                  o_bank.rearrange("p (h e) -> p h e", h=GH),
                                  RI[:, :].unsqueeze(2).to_broadcast([P, GH, DH]), ALU.mult).then_inc(s.normed, 1)

            def o_keep(G, n, g):
                need(dve, s.o_turned, G + 1)
                need(dve, s.projected, n)
                dve.tensor_copy(OTS[:, 2 * g:2 * g + 2, :], ot_bank).then_inc(s.o_kept, 1)

            def maxes(G, g, par):
                need(dve, s.scored, G + 1)
                dve.tensor_reduce(NM[:, par, :].rearrange("p (b h) -> p b h", b=2), s_bank(par), AX.X, ALU.max,
                                  negate=True).then_inc(s.maxed, 1)
                need(dve, s.maxed, G + 1)
                need(dve, s.norm_a, G + 1)
                need(dve, s.exped, G - 1)
                dve.tensor_tensor(NB[:, par, :], NM[:, par, :], A[:, g, 0:GH], ALU.mult).then_inc(s.biased, 1)

            def residual(n, t):
                need(dve, s.projected, n + 1)
                dve.tensor_tensor(c.xb[:, bass.ds(t * P + 1, P)], y_bank, c.xa[:, bass.ds(t * P + 1, P)],
                                  ALU.add).then_inc(s.resid, 1)

            def piece(p, ffn):
                k, fch, load = ffn
                if p == MEAN:
                    need(dve, s.ln_mean, k + 1)
                    need(dve, s.ln_squared, k)
                    dve.tensor_tensor(c.ln_cen[:, :], XS2[:, :], f_bank, ALU.subtract).then_inc(s.ln_centered, 1)
                if p == VAR:
                    need(dve, s.ln_var, k + 1)
                    need(dve, s.ln_rstd, k)
                    dve.tensor_scalar(VE[:, :], f_bank[:, 0:4], 1e-5, None, ALU.add).then_inc(s.ln_eps, 1)
                if p == SPREAD:
                    need(dve, s.ln_spread, k + 1)
                    need(dve, s.val, k * 3)
                    dve.tensor_tensor(XN[:, :], c.ln_cen[:, :], f_bank, ALU.mult).then_inc(s.ln_done, 1)
                if p in VAL:
                    j = VAL.index(p)
                    w = HPART[j][1]
                    if j == 0:
                        dve.wait_ge(d.ffn, load)
                        need(dve, s.gelud, k + 1)
                        need(dve, s.down, k)
                    need(dve, s.val, k * 3 + (j + 1))
                    dve.scalar_tensor_tensor(H[0:w, j, :], f_bank[0:w, :], B1[0:w, 0, j:j + 1], GT[0:w, j, :],
                                             ALU.add, ALU.mult).then_inc(s.gated, 1)
                if p == DOWN:
                    need(dve, s.down, k + 1)
                    need(dve, s.xs_staged, k * 4 + 5)
                    dve.scalar_tensor_tensor(c.xa[:, bass.ds(fch * CH + 1, CH)], f_bank, VEC[:, 2:3],
                                             c.xb[:, bass.ds(fch * CH + 1, CH)], ALU.add, ALU.add).then_inc(s.ffn_done, 1)

            def step(n, t, g, p=None, ffn=None, first=False):
                G = n * 4 + g
                if not first:
                    normalize(G)
                rope_qk(G + AHEAD, n + 1, g % 2)
                sums(G + AHEAD, g % 2)
                if not first:
                    o_keep(G, n, g)
                if not first or g == GROUPS - 1:
                    prev_turn(G + 1, (g + 1) % 2)
                    recip(G + 1, (g + 1) % 2)
                if ffn is not None and p < PIECES:
                    piece(p, ffn)
                if not first or g >= 2:
                    maxes(G + 2, (g + 2) % 4, g % 2)
                v_keep(G + AHEAD, n, g, first)
                if not first and g == GROUPS - 1:
                    residual(n, t)

            def chunk(l, ch, ffn):
                for j in range(4):
                    for g in range(GROUPS):
                        step((l * CHUNKS + ch) * 4 + j, ch * 4 + j, g, 4 * j + g, ffn)

            for g in range(GROUPS):
                step(-1, -1, g, first=True)
            chunks(dve, chunk)
            for p in range(PIECES):
                piece(p, LAST)


def store_phase(nc, c, x3, out):
    with ExitStack() as ctx:
        s = Counters(nc, ctx, "st_", LN_NAMES + " summed turned kept stored")
        y_tok = ctx.enter_context(nc.sbuf_tensor("y_tok", [P, TILES, P], F32))
        start_counters(nc, [s.ln_mean, s.ln_centered, s.ln_squared, s.ln_var, s.ln_sd, s.ln_rstd, s.ln_done])
        block = ctx.enter_context(nc.Block())

        def x(b):
            return c.xb[:, 1 + CH * b:1 + CH * (b + 1)]

        def y(b):
            return c.xa[:, 1 + CH * b:1 + CH * (b + 1)]

        @block.tensor
        def _(pe):
            for b in range(CHUNKS):
                pe.wait_ge(s.summed, b + 1)
                ln_pe(pe, s, c, b, x(b), c.ps[:, 0, :], c.ps[:, 1, :])
                need(pe, s.ln_done, b + 1)
                for t in range(4):
                    m = pe.transpose(c.ps[:, 4 + b, t * P:(t + 1) * P],
                                     c.xa[:, 1 + CH * b + P * t:1 + CH * b + P * (t + 1)], c.ident[:, :])
                m.then_inc(s.turned, 1)

        @block.scalar
        def _(act):
            for b in range(CHUNKS):
                ln_act(act, s, c, b, c.ps[:, 1, :], c.eps5[:, 0:1])

        @block.vector
        def _(dve):
            for b in range(CHUNKS):
                dve.tensor_tensor(x(b), x3[:, CH * b:CH * (b + 1)], y(b), ALU.add).then_inc(s.summed, 1)
            dve.wait_ge(s.summed, CHUNKS)
            for b in range(CHUNKS):
                ln_dve(dve, s, c, b, x(b), c.ps[:, 0, :], y(b))
                dve.wait_ge(s.turned, b + 1)
                dve.tensor_copy(y_tok[:, 4 * b:4 * b + 4, :],
                                c.ps[:, 4 + b, :].rearrange("p (t f) -> p t f", t=4)).then_inc(s.kept, 1)

        @block.sync
        def _(sp):
            for b in range(CHUNKS):
                sp.wait_ge(s.kept, b + 1)
                sp.dma_start(out[0, CH * b:CH * (b + 1), :].rearrange("(t p) f -> p t f", p=P),
                             y_tok[:, 4 * b:4 * b + 4, :]).then_inc(s.stored, 16)
            sp.wait_ge(s.stored, 16 * CHUNKS)


def program(nc, t, out):
    with ExitStack() as ctx:
        c = Common(nc, ctx)
        load_phase(nc, c, t["L0_attn_x"], t["c_ident"])
        attention_and_quant(nc, c, t)
        x3 = ctx.enter_context(nc.sbuf_tensor("x3", [P, T], F32))
        ssm_phase(nc, c, x3, {n.removeprefix("L1_attn_"): a for n, a in t.items()})
        local_phase(nc, c, *[t["L1_ffn_" + n] for n in ("Wqkv", "q_scale", "k_scale", "Wo", "ln_g", "ln_b", "W1", "b1", "W2", "b2")],
                    t["c_rope"], t["c_mask"], t["c_kfac"])
        store_phase(nc, c, x3, out)



def constants():
    import numpy as np
    bf16 = mybir.dt.np(BF16)
    f32 = np.float32
    half = np.arange(0, DH, 2, dtype=f32)
    inv_freq = (f32(1.0) / f32(10000.0) ** (half / f32(DH))).astype(f32)
    freqs = np.arange(T, dtype=f32)[:, None] * inv_freq[None, :]
    cos, sin = np.cos(freqs).astype(f32), np.sin(freqs).astype(f32)
    base = ((half + 0.4 * DH) / (1.4 * DH)).astype(np.float64)
    power = (np.arange(T) % P - P // 2) / (WIN // 2)
    scale = base[None, :] ** power[:, None]
    both = lambda a: np.concatenate([a, a], -1)
    sign = np.concatenate([-np.ones(DH // 2), np.ones(DH // 2)])[None, :]
    parts = [both(cos * scale) * 8.0, both(cos / scale), both(sin * scale) * sign * 8.0, both(sin / scale) * sign]
    rope = np.stack(parts, 1).astype(f32).reshape(TILES, P, 4 * DH).transpose(1, 0, 2)
    q = np.arange(P)[:, None]
    k = np.arange(KEYS)[None, :] - WIN
    seen = (k <= q) & (k >= q - WIN)
    mask = np.repeat(np.where(seen, 0.0, -1e30)[:, None, :], TILES + 1, 1)
    mask[:, [0, TILES], 0:WIN] = -1e30
    return {
        "c_ident": np.eye(P, dtype=f32),
        "c_rope": np.ascontiguousarray(rope),
        "c_mask": mask.astype(bf16),
        "c_select": np.ascontiguousarray(np.broadcast_to(
            (np.arange(3 * BC)[:, None] % BC == np.arange(BC)[None, :])[:, :, None], (3 * BC, BC, P))).astype(bf16),
        "c_ones_rows": (np.arange(P) % MROWS < 3).astype(f32)[:, None],
        "c_mask_qk": np.where(np.arange(P)[None, :] > q, -1e30, 0.0).astype(bf16),
        "c_mask_kq": np.where(q > np.arange(P)[None, :], -1e30, 0.0).astype(bf16),
        "c_kfac": np.tile(both(base ** (P // (WIN // 2))), 2).astype(f32)[:, None],
    }


def kernel(**inputs):
    import numpy as _np
    import concourse.bacc as _bacc
    from concourse import mybir as _mybir
    from concourse.bass_utils import run_bass_kernel_spmd as _run

    nc = _bacc.Bacc("TRN2", target_bir_lowering=False, num_devices=1)
    arrays = {"in_" + n: _np.ascontiguousarray(a) for n, a in inputs.items()}
    arrays.update(constants())
    tensors = {n.removeprefix("in_"): nc.dram_tensor(n, a.shape, _mybir.dt.from_np(a.dtype), kind="ExternalInput").ap()
               for n, a in arrays.items()}
    out = nc.dram_tensor("out_0_dram", (1, T, P), F32, kind="ExternalOutput").ap()
    program(nc, tensors, out)
    r = _run(nc, [arrays], core_ids=[0])
    return r.results[0]["out_0_dram"]
```

```python
from collections import namedtuple
from contextlib import ExitStack

import concourse.bass as bass
from concourse import mybir

ALU = mybir.AluOpType
ACT = mybir.ActivationFunctionType
AX = mybir.AxisListType
F32 = mybir.dt.float32
BF16 = mybir.dt.bfloat16
U32 = mybir.dt.uint32

P = 128
T = 2048
TILES = T // P
CH = 512
CHUNKS = T // CH
BASE = 8


def need(eng, counter, count):
    eng.wait_ge(counter, count + BASE)


def Counters(nc, ctx, prefix, names):
    counters = namedtuple("Semaphores", names)(*[nc.alloc_semaphore(name=prefix + n) for n in names.split()])
    ctx.callback(nc.all_engine_barrier)
    ctx.callback(nc.clear_and_free_semaphores, list(counters))
    return counters


def start_counters(nc, counters):
    with nc.Block() as block:
        @block.sync
        def _(sp):
            for c in counters:
                sp.sem_inc(c, BASE)



LN_NAMES = "ln_mean ln_centered ln_squared ln_var ln_sd ln_rstd ln_done"


def ln_mean(pe, s, c, k, x, mean):
    pe.matmul(mean, c.avg[:, :], x, start=True, stop=True).then_inc(s.ln_mean, 1)


def ln_var(pe, s, c, k, var):
    need(pe, s.ln_squared, k + 1)
    pe.matmul(var, c.avg[:, :], c.ln_sq[:, :], start=True, stop=True).then_inc(s.ln_var, 1)


def ln_square(act, s, c, k):
    need(act, s.ln_centered, k + 1)
    act.activation(c.ln_sq[:, :], c.ln_cen[:, :], ACT.Square).then_inc(s.ln_squared, 1)


def ln_root(act, s, c, k, var, eps):
    need(act, s.ln_var, k + 1)
    act.activation(c.ln_sd[:, :], var, ACT.Sqrt, bias=eps).then_inc(s.ln_sd, 1)


def ln_center(dve, s, c, k, x, mean):
    need(dve, s.ln_mean, k + 1)
    dve.tensor_tensor(c.ln_cen[:, :], x, mean, ALU.subtract).then_inc(s.ln_centered, 1)


def ln_scale(dve, s, c, k, out):
    need(dve, s.ln_sd, k + 1)
    dve.reciprocal(c.ln_rs[:, :], c.ln_sd[:, :]).then_inc(s.ln_rstd, 1)
    need(dve, s.ln_rstd, k + 1)
    dve.tensor_tensor(out, c.ln_cen[:, :], c.ln_rs[:, :], ALU.mult).then_inc(s.ln_done, 1)


def ln_pe(pe, s, c, k, x, mean, var):
    ln_mean(pe, s, c, k, x, mean)
    ln_var(pe, s, c, k, var)


def ln_act(act, s, c, k, var, eps):
    ln_square(act, s, c, k)
    ln_root(act, s, c, k, var, eps)


def ln_dve(dve, s, c, k, x, mean, out):
    ln_center(dve, s, c, k, x, mean)
    ln_scale(dve, s, c, k, out)


LnBuffers = namedtuple("LnBuffers", "avg ln_cen ln_sq ln_sd ln_rs")


def ln_buffers(nc, ctx, c, prefix):
    cen, sq, sd, rs = (ctx.enter_context(nc.sbuf_tensor(prefix + n, [P, CHUNKS, CH], F32)) for n in ("cen", "sq", "sd", "rs"))
    return [LnBuffers(c.avg, cen[:, b, :], sq[:, b, :], sd[:, b, :], rs[:, b, :]) for b in range(CHUNKS)]


Early = namedtuple("Early", "tensors loads loaded")


def load_early(sp, early):
    for dst, src in early.loads:
        sp.dma_start(dst, src).then_inc(early.loaded, 16)


class Common:

    def __init__(self, nc, ctx):
        def sb(name, shape, dt=F32):
            return ctx.enter_context(nc.sbuf_tensor(name, shape, dt))

        self.xa = sb("xa", [P, T + 1])
        self.xb = sb("xb", [P, T + 1])
        self.ident = sb("ident", [P, P])
        self.ident_bf = sb("ident_bf", [P, P], BF16)
        self.avg = sb("avg", [P, P])
        self.eps5 = sb("eps5", [P, 1])
        self.eps6 = sb("eps6", [P, 1])
        self.ln_cen = sb("ln_cen", [P, CH])
        self.ln_sq = sb("ln_sq", [P, CH])
        self.ln_sd = sb("ln_sd", [P, CH])
        self.ln_rs = sb("ln_rs", [P, CH])
        self.ps = ctx.enter_context(nc.psum_tensor("ps", [P, 8, CH], F32))


def load_phase(nc, c, x, ident):
    with ExitStack() as ctx:
        s = Counters(nc, ctx, "ld_", "x ident turned kept const")
        x_tok = ctx.enter_context(nc.sbuf_tensor("x_tok", [P, TILES, P], F32))
        block = ctx.enter_context(nc.Block())

        @block.sync
        def _(sp):
            sp.dma_start(c.ident[:, :], ident).then_inc(s.ident, 16)
            sp.dma_start(x_tok[:, :, :], x[0].rearrange("(t p) f -> p t f", p=P)).then_inc(s.x, 16)

        @block.gpsimd
        def _(pool):
            pool.memset(c.avg[:, :], 1.0 / P)
            pool.memset(c.eps5[:, :], 1e-5)
            pool.memset(c.eps6[:, :], 1e-6)
            pool.memset(c.xa[:, 0:1], 0.0)
            pool.memset(c.xb[:, 0:1], 0.0).then_inc(s.const, 1)

        @block.tensor
        def _(pe):
            pe.wait_ge(s.ident, 16)
            pe.wait_ge(s.x, 16)
            for b in range(CHUNKS):
                for t in range(4 * b, 4 * b + 4):
                    m = pe.transpose(c.ps[:, b, (t % 4) * P:(t % 4 + 1) * P], x_tok[:, t, :], c.ident[:, :])
                m.then_inc(s.turned, 1)

        @block.vector
        def _(dve):
            dve.wait_ge(s.ident, 16)
            dve.tensor_copy(c.ident_bf[:, :], c.ident[:, :])
            for b in range(CHUNKS):
                dve.wait_ge(s.turned, b + 1)
                dve.tensor_copy(c.xa[:, 1 + CH * b:1 + CH * (b + 1)], c.ps[:, b, :]).then_inc(s.kept, 1)



AHEADS = 16
AD = P // AHEADS
LATENT = 32
PAIRS = AHEADS // 2
MROWS = 8
USED = MROWS + 6 * AD
Q_PART = (0, 0, 1, 1, 0, 2)
K_PART = (0, 1, 0, 1, 2, 0)
VW = AD + 1
A_SCALE = AD ** -0.5
UNITS = [4 * (b + 1) for b in range(CHUNKS)]
STEP_UNITS = 2 * sum(UNITS)
STEPS = [(0, b) for b in range(CHUNKS)] + [(1, b) for b in reversed(range(CHUNKS))]


def units_before(st):
    return sum(UNITS[b] for _, b in STEPS[:st])


def project_phase(nc, c, m, w_dkv, w_uk, w_uv, w_uq, ones_rows, q_stack, k_stack):
    with ExitStack() as ctx:
        def sb(name, shape, dt=F32):
            return ctx.enter_context(nc.sbuf_tensor("ap_" + name, shape, dt))

        WD = sb("WD", [P, LATENT])
        WK = sb("WK", [LATENT, P])
        WV = sb("WV", [LATENT, P])
        WQ = sb("WQ", [P, P])
        CT = sb("CT", [LATENT, T])
        ONES = sb("ONES", [P, 1])
        FILL = sb("FILL", [P, 2, T], BF16)
        PART = sb("PART", [P, 2, 3, T], BF16)
        REST = sb("REST", [P, 2, CH])
        s = Counters(nc, ctx, "ap_", "w ones zeroed filled latent ckept vdone vkept proj first rest second third stored")
        block = ctx.enter_context(nc.Block())

        @block.sync
        def _(sp):
            for dst, src in ((WD, w_dkv), (WK, w_uk), (WV, w_uv), (WQ, w_uq)):
                sp.dma_start(dst[:, :], src).then_inc(s.w, 16)
            sp.dma_start(ONES[:, :], ones_rows).then_inc(s.ones, 16)
            stacks = (q_stack, k_stack)
            for i in range(2):
                sp.wait_ge(s.filled, i + 1)
                sp.dma_start(stacks[i][:, 0:MROWS, :], FILL[:, i, :]).then_inc(s.stored, 16)
            for i, terms in enumerate((Q_PART, K_PART)):
                sp.wait_ge(s.third, 4 * (i + 1))
                for t, part in enumerate(terms):
                    sp.dma_start(stacks[i][:, MROWS + AD * t:MROWS + AD * (t + 1), :],
                                 PART[:, i, part, :]).then_inc(s.stored, 16)
            sp.wait_ge(s.stored, 16 * 14)

        @block.gpsimd
        def _(pool):
            pool.memset(FILL[:, 0, :], 0.0).then_inc(s.filled, 1)
            pool.wait_ge(s.ones, 16)
            pool.wait_ge(s.filled, 1)
            pool.tensor_copy(FILL[:, 1, :], ONES[:, 0:1].to_broadcast([P, T])).then_inc(s.filled, 1)

        @block.tensor
        def _(pe):
            pe.wait_ge(s.w, 64)
            for b in range(CHUNKS):
                pe.matmul(c.ps[0:LATENT, b, :], WD[:, :], c.xa[:, 1 + CH * b:1 + CH * (b + 1)],
                          start=True, stop=True).then_inc(s.latent, 1)
            for i in range(2):
                for b in range(CHUNKS):
                    k = 4 * i + b
                    if k >= 2:
                        pe.wait_ge(s.rest, k - 1)
                    if i == 1:
                        pe.wait_ge(s.ckept, b + 1)
                    w, x = (WQ, c.xa[:, 1 + CH * b:1 + CH * (b + 1)]) if i == 0 else (WK, CT[:, CH * b:CH * (b + 1)])
                    pe.matmul(c.ps[:, 4 + k % 2, :], w[:, :], x, start=True, stop=True).then_inc(s.proj, 1)
            for t in range(TILES):
                if t >= 8:
                    pe.wait_ge(s.vkept, t // 4 - 1)
                mm = pe.matmul(c.ps[:, 6 + (t // 4) % 2, (t % 4) * P:(t % 4 + 1) * P], CT[:, t * P:(t + 1) * P], WV[:, :],
                               start=True, stop=True)
                if t % 4 == 3:
                    mm.then_inc(s.vdone, 1)

        @block.scalar
        def _(act):
            for k in range(8):
                i, b = k // 4, k % 4
                act.wait_ge(s.proj, k + 1)
                act.activation(PART[:, i, 0, CH * b:CH * (b + 1)], c.ps[:, 4 + k % 2, :], ACT.Copy).then_inc(s.first, 1)
                act.wait_ge(s.rest, k + 1)
                act.activation(PART[:, i, 1, CH * b:CH * (b + 1)], REST[:, k % 2, :], ACT.Copy).then_inc(s.second, 1)

        @block.vector
        def _(dve):
            dve.memset(m.va[:, :, :, :], 1.0).then_inc(s.zeroed, 1)
            dve.wait_ge(s.zeroed, 1)
            for b in range(CHUNKS):
                dve.wait_ge(s.latent, b + 1)
                dve.tensor_copy(CT[:, CH * b:CH * (b + 1)], c.ps[0:LATENT, b, :]).then_inc(s.ckept, 1)

            def third(k):
                i, b = k // 4, k % 4
                dve.wait_ge(s.second, k + 1)
                dve.tensor_tensor(PART[:, i, 2, CH * b:CH * (b + 1)], REST[:, k % 2, :],
                                  PART[:, i, 1, CH * b:CH * (b + 1)], ALU.subtract).then_inc(s.third, 1)

            for k in range(8):
                i, b = k // 4, k % 4
                dve.wait_ge(s.first, k + 1)
                if k >= 2:
                    dve.wait_ge(s.third, k - 1)
                dve.tensor_tensor(REST[:, k % 2, :], c.ps[:, 4 + k % 2, :], PART[:, i, 0, CH * b:CH * (b + 1)],
                                  ALU.subtract).then_inc(s.rest, 1)
                if k >= 1:
                    third(k - 1)
            third(7)
            for b in range(CHUNKS):
                dve.wait_ge(s.vdone, b + 1)
                dve.tensor_copy(m.va[:, 4 * b:4 * b + 4, :, 0:AD],
                                c.ps[:, 6 + b % 2, :].rearrange("p (t h e) -> p t h e", t=4, e=AD)).then_inc(s.vkept, 1)


CROWS = 32 + VW
CAUSAL_COUNTERS = ("vs_ready p1_scored p1_maxed m_neg m_a m_b m_c m_d m_turned m_kept s_done exped attended "
                   "ctx_left ctx_turned ctx_sum ctx_done")


def causal_phase(nc, c, m, q_stack, k_stack, mask_qk, mask_kq, ahead):
    with ExitStack() as ctx:
        def sb(name, shape, dt=F32):
            return ctx.enter_context(nc.sbuf_tensor("ac_" + name, shape, dt))

        QS = sb("QS", [P, 2, T], BF16)
        KS = sb("KS", [P, 2, T], BF16)
        VS = sb("VS", [P, 2, TILES, 2 * VW])
        MQK = sb("MQK", [P, P], BF16)
        MKQ = sb("MKQ", [P, P], BF16)
        PM = sb("PM", [P, CHUNKS, 4, 2])
        NM = sb("NM", [P, 4, 2])
        NR = sb("NR", [P, 4, 2])
        M3 = sb("M3", [P, 4, P], BF16)
        PT = sb("PT", [P, 4, 2, CH])
        ZERO = sb("ZERO", [P, CH])
        PICK = sb("PICK", [P, CROWS])
        CX = sb("CX", [P, CH])
        LI = sb("LI", [P, 4, 2])
        s = Counters(nc, ctx, "ac_", CAUSAL_COUNTERS)
        start_counters(nc, s)
        d = Counters(nc, ctx, "acd_", "stack0 stack1 masks zero")
        stack = (d.stack0, d.stack1)
        m_bank = c.ps[:, 7, :].bitcast(BF16)
        o_bank = c.ps[:, 7, CH // 2:CH // 2 + 4 * CROWS]
        m3 = M3[:, :, :].rearrange("p t (s r) -> p t s r", s=2)
        block = ctx.enter_context(nc.Block())

        @block.sync
        def _(sp):
            sp.dma_start(MQK[:, :], mask_qk).then_inc(d.masks, 16)
            sp.dma_start(MKQ[:, :], mask_kq).then_inc(d.masks, 16)
            with sp.Fori(0, PAIRS // 2) as it:
                for u in range(2):
                    need(sp, s.ctx_done, it * len(STEPS) + CHUNKS * (u - 1))
                    for dst, src in ((QS, q_stack), (KS, k_stack)):
                        for h in range(2):
                            sp.dma_start(dst[64 * h:64 * h + USED, u, :],
                                         src[bass.ds(it * 4 + 2 * u + h, 1), :, :].rearrange("h r t -> (h r) t"))\
                              .then_inc(stack[u], 16)
            for early in ahead:
                load_early(sp, early)

        @block.gpsimd
        def _(pool):
            pool.memset(ZERO[:, :], 0.0)
            pool.tensor_tensor(PICK[:, :], c.ident[:, 0:CROWS], c.ident[:, 64:64 + CROWS], ALU.add)
            pool.memset(M3[:, :, :], 0.0).then_inc(d.zero, 1)
            with pool.Fori(0, PAIRS // 2) as it:
                for u in range(2):
                    need(pool, s.ctx_done, it * len(STEPS) + CHUNKS * (u - 1))
                    pool.tensor_copy(VS[:, u, :, :], m.va[:, :, :, :].rearrange("p t h e -> p t (h e)")
                                     [:, :, bass.ds((it * 2 + u) * (2 * VW), 2 * VW)]).then_inc(s.vs_ready, 1)

        @block.tensor
        def _(pe):
            pe.wait_ge(d.masks, 32)
            pe.wait_ge(d.zero, 1)

            def p1(it, st, n, h):
                u, b = STEPS[st]
                i, j = n // (b + 1), n % (b + 1)
                last = j == b
                w = (i + 1) * P if last else CH
                q0 = CH * b + P * i
                if n == 0 and h == 0 and st % CHUNKS == 0:
                    pe.wait_ge(stack[u], it * 64 + 64)
                need(pe, s.p1_maxed, 2 * (it * STEP_UNITS + units_before(st) + n) + h - 1)
                mm = pe.matmul(c.ps[:, 4 + h, 0:w], QS[64 * h:64 * h + USED, u, q0:q0 + P],
                               KS[64 * h:64 * h + USED, u, CH * j:CH * j + w], start=True, stop=not last)
                if last:
                    mm = pe.matmul(c.ps[:, 4 + h, w - P:w], c.ident_bf[:, :], MQK[:, :], start=False, stop=True)
                mm.then_inc(s.p1_scored, 1)

            def maxima(it, st):
                need(pe, s.m_d, it * len(STEPS) + st + 1)
                need(pe, s.m_kept, it * len(STEPS) + st)
                for i in range(4):
                    mm = pe.transpose(m_bank[:, i * P:(i + 1) * P], M3[:, i, :], c.ident_bf[:, :])
                mm.then_inc(s.m_turned, 1)

            def s2(it, st, j):
                u, b = STEPS[st]
                n = units_before(st) + j
                q0 = max(0, j - 4 * b) * P
                need(pe, s.exped, it * STEP_UNITS + n - 1)
                if j == 0:
                    need(pe, s.m_kept, it * len(STEPS) + st + 1)
                for h in range(2):
                    mm = pe.matmul(c.ps[:, 2 * (n % 2) + h, q0:CH], KS[64 * h:64 * h + USED, u, P * j:P * (j + 1)],
                                   QS[64 * h:64 * h + USED, u, CH * b + q0:CH * (b + 1)], start=True, stop=j < 4 * b)
                if j >= 4 * b:
                    for h in range(2):
                        mm = pe.matmul(c.ps[:, 2 * (n % 2) + h, q0:q0 + P], c.ident_bf[:, :], MKQ[:, :],
                                       start=False, stop=True)
                mm.then_inc(s.s_done, 1)

            def attend(it, st, j):
                u, b = STEPS[st]
                n = units_before(st) + j
                need(pe, s.exped, it * STEP_UNITS + n + 2)
                if j == 0:
                    need(pe, s.ctx_left, it * len(STEPS) + st)
                    if st % CHUNKS == 0:
                        need(pe, s.vs_ready, it * 2 + u + 1)
                    if b == 0:
                        for h in range(2):
                            pe.matmul(c.ps[64 + 32 * h:64 + 32 * h + VW, 6, :], ZERO[:, 0:VW], ZERO[:, :],
                                      start=True, stop=False, skip_group_check=True)
                for e in range(2):
                    q0 = max(0, j + e - 4 * b) * P
                    for h in range(2):
                        row = 64 * e + 32 * h
                        mm = pe.matmul(c.ps[row:row + VW, 6, q0:CH], VS[:, u, j + e, h * VW:(h + 1) * VW],
                                       PT[:, (n + e) % 4, h, q0:CH], start=(j == 0 and q0 == 0),
                                       stop=j == UNITS[b] - 2, skip_group_check=True)
                mm.then_inc(s.attended, 1)

            def turn_context(it, st):
                k = it * len(STEPS) + st
                need(pe, s.ctx_left, k + 1)
                need(pe, s.ctx_done, k)
                for i in range(4):
                    mm = pe.matmul(o_bank[:, i * CROWS:(i + 1) * CROWS], CX[:, i * P:(i + 1) * P],
                                   PICK[:, :], start=i == 0, stop=True, skip_group_check=True)
                mm.then_inc(s.ctx_turned, 1)

            pe.matmul(c.ps[:, 6, :], ZERO[:, 0:P], ZERO[:, :], start=True, stop=True)

            with pe.Fori(0, PAIRS // 2) as it:
                for n in range(UNITS[0]):
                    for h in range(2):
                        p1(it, 0, n, h)
                maxima(it, 0)
                for st, (u, b) in enumerate(STEPS):
                    after = UNITS[STEPS[st + 1][1]] if st + 1 < len(STEPS) else 0
                    among = max(2, UNITS[b] - 3)
                    for n in range(UNITS[b] + 1):
                        search = [(i, h) for i in range(after) if i * among // after == n for h in range(2)]
                        cuts = [len(search) * i // 3 for i in range(4)]
                        for i, h in search[cuts[0]:cuts[1]]:
                            p1(it, st + 1, i, h)
                        if n < UNITS[b]:
                            s2(it, st, n)
                        for i, h in search[cuts[1]:cuts[2]]:
                            p1(it, st + 1, i, h)
                        if n >= 2 and n % 2 == 0:
                            attend(it, st, n - 2)
                        for i, h in search[cuts[2]:cuts[3]]:
                            p1(it, st + 1, i, h)
                        if n == among:
                            if st >= 1:
                                turn_context(it, st - 1)
                            if after:
                                maxima(it, st + 1)
                turn_context(it, len(STEPS) - 1)

        @block.scalar
        def _(act):
            act.wait_ge(d.zero, 1)

            def leave(it, st):
                k = it * len(STEPS) + st
                need(act, s.attended, it * (STEP_UNITS // 2) + units_before(st + 1) // 2)
                need(act, s.ctx_turned, k)
                act.activation(CX[:, :], c.ps[:, 6, :], ACT.Copy).then_inc(s.ctx_left, 1)

            with act.Fori(0, PAIRS // 2) as it:
                for st, (u, b) in enumerate(STEPS):
                    for j in range(UNITS[b]):
                        n = units_before(st) + j
                        q0 = max(0, j - 4 * b) * P
                        need(act, s.s_done, it * STEP_UNITS + n + 1)
                        need(act, s.attended, it * (STEP_UNITS // 2) + (n // 2 - 1))
                        act.activation(PT[:, n % 4, :, q0:CH], c.ps[:, 2 * (n % 2):2 * (n % 2) + 2, q0:CH], ACT.Exp,
                                       scale=A_SCALE).then_inc(s.exped, 1)
                        if j == 0 and st >= 1:
                            leave(it, st - 1)
                leave(it, len(STEPS) - 1)

        @block.vector
        def _(dve):
            dve.wait_ge(d.zero, 1)

            def p1_max(it, st, n):
                u, b = STEPS[st]
                i, j = n // (b + 1), n % (b + 1)
                w = (i + 1) * P if j == b else CH
                done = 2 * (it * STEP_UNITS + units_before(st) + n)
                for h in range(2):
                    need(dve, s.p1_scored, done + h + 1)
                    dve.tensor_reduce(PM[:, j, i, h:h + 1], c.ps[:, 4 + h, 0:w], AX.X, ALU.max).then_inc(s.p1_maxed, 1)

            def maxima(it, st):
                u, b = STEPS[st]
                k = it * len(STEPS) + st
                need(dve, s.p1_maxed, 2 * (it * STEP_UNITS + units_before(st + 1)))
                dve.tensor_reduce(NM[:, :, :], PM[:, 0:b + 1, :, :].rearrange("p j i s -> p i s j"), AX.X, ALU.max,
                                  negate=True).then_inc(s.m_neg, 1)
                need(dve, s.m_neg, k + 1)
                need(dve, s.m_turned, k)
                dve.tensor_copy(m3[:, :, :, 0], NM[:, :, :]).then_inc(s.m_a, 1)
                need(dve, s.m_a, k + 1)
                dve.tensor_tensor(NR[:, :, :], NM[:, :, :], m3[:, :, :, 0], ALU.subtract).then_inc(s.m_b, 1)
                need(dve, s.m_b, k + 1)
                dve.tensor_copy(m3[:, :, :, 1], NR[:, :, :]).then_inc(s.m_c, 1)
                need(dve, s.m_c, k + 1)
                dve.tensor_tensor(m3[:, :, :, 2], NR[:, :, :], m3[:, :, :, 1], ALU.subtract).then_inc(s.m_d, 1)

            def keep_maxima(it, st):
                u, b = STEPS[st]
                need(dve, s.m_turned, it * len(STEPS) + st + 1)
                for h in range(2):
                    mm = dve.tensor_copy(QS[64 * h:64 * h + 3, u, CH * b:CH * (b + 1)], m_bank[64 * h:64 * h + 3, 0:CH])
                mm.then_inc(s.m_kept, 1)

            def context(it, st):
                u, b = STEPS[st]
                k = it * len(STEPS) + st
                o = o_bank.rearrange("p (i r) -> p i r", r=CROWS)
                need(dve, s.ctx_turned, k + 1)
                dve.reciprocal(LI[:, :, :], o[:, :, AD::32]).then_inc(s.ctx_sum, 1)
                need(dve, s.ctx_sum, k + 1)
                for h in range(2):
                    mm = dve.tensor_tensor(m.ctx[:, 4 * b:4 * b + 4, bass.ds((it * 2 + u) * (2 * AD) + h * AD, AD)],
                                           o[:, :, 32 * h:32 * h + AD], LI[:, :, h:h + 1].to_broadcast([P, 4, AD]), ALU.mult)
                mm.then_inc(s.ctx_done, 1)

            with dve.Fori(0, PAIRS // 2) as it:
                for n in range(UNITS[0]):
                    p1_max(it, 0, n)
                maxima(it, 0)
                keep_maxima(it, 0)
                for st in range(len(STEPS)):
                    if st + 1 < len(STEPS):
                        for n in range(UNITS[STEPS[st + 1][1]]):
                            p1_max(it, st + 1, n)
                        maxima(it, st + 1)
                        keep_maxima(it, st + 1)
                    if st >= 1:
                        context(it, st - 1)
                context(it, len(STEPS) - 1)


POST_COUNTERS = ("ct_turned ct_kept y_done summed scale clipped low bits unit magic rounded w_turned w_kept o_done "
                 "o_kept o_summed " + LN_NAMES)


def quant_phase(nc, c, m, w_o, w8, bias, in_scale, w_scale):
    with ExitStack() as ctx:
        def sb(name, shape, dt=F32):
            return ctx.enter_context(nc.sbuf_tensor("qz_" + name, shape, dt))

        WO = sb("WO", [P, P])
        W8 = sb("W8", [P, P])
        W8T = sb("W8T", [P, P])
        BIAS = sb("BIAS", [P, 1])
        SI = sb("SI", [P, 1])
        SW = sb("SW", [P, 1])
        RSI = sb("RSI", [P, 1])
        SIW = sb("SIW", [P, 1])
        CT = sb("CT", [P, CHUNKS, CH])
        Y = sb("Y", [P, CHUNKS, CH])
        X1 = sb("X1", [P, CHUNKS, CH])
        XQ = sb("XQ", [P, CHUNKS, CH])
        UNIT = sb("UNIT", [P, CH])
        s = Counters(nc, ctx, "qz_", POST_COUNTERS)
        start_counters(nc, s)
        d = Counters(nc, ctx, "qzd_", "w")
        ln = ln_buffers(nc, ctx, c, "qz_ln_")
        one = [c.ps[:, b, :] for b in range(CHUNKS)]
        two = [c.ps[:, CHUNKS + b, :] for b in range(CHUNKS)]
        block = ctx.enter_context(nc.Block())

        def xa(b):
            return c.xa[:, 1 + CH * b:1 + CH * (b + 1)]

        @block.sync
        def _(sp):
            for dst, src in ((WO, w_o), (W8, w8), (BIAS, bias.rearrange("(p a) -> p a", a=1)),
                             (SI, in_scale.rearrange("(a b) -> a b", a=1).broadcast_to([P, 1])),
                             (SW, w_scale.rearrange("(a b) -> a b", a=1).broadcast_to([P, 1]))):
                sp.dma_start(dst[:, :], src).then_inc(d.w, 16)

        @block.tensor
        def _(pe):
            pe.wait_ge(d.w, 80)
            pe.transpose(two[0][:, 0:P], W8[:, :], c.ident[:, :]).then_inc(s.w_turned, 1)
            for b in range(CHUNKS):
                for i in range(4):
                    mm = pe.transpose(one[b][:, i * P:(i + 1) * P], m.ctx[:, 4 * b + i, :], c.ident[:, :])
                mm.then_inc(s.ct_turned, 1)
            need(pe, s.w_kept, 1)
            for b in range(CHUNKS):
                need(pe, s.ct_kept, b + 1)
                pe.matmul(two[b], WO[:, :], CT[:, b, :], start=True, stop=True).then_inc(s.y_done, 1)
            for b in range(CHUNKS):
                need(pe, s.summed, b + 1)
                ln_mean(pe, s, ln[b], b, Y[:, b, :], one[b])
            for b in range(CHUNKS):
                ln_var(pe, s, ln[b], b, two[b])
            for b in range(CHUNKS):
                need(pe, s.rounded, b + 1)
                pe.matmul(one[b], W8T[:, :], XQ[:, b, :], start=True, stop=True).then_inc(s.o_done, 1)
            for b in range(CHUNKS):
                need(pe, s.o_summed, b + 1)
                ln_mean(pe, s, ln[b], CHUNKS + b, Y[:, b, :], two[b])
            for b in range(CHUNKS):
                ln_var(pe, s, ln[b], CHUNKS + b, one[b])

        @block.scalar
        def _(act):
            for b in range(CHUNKS):
                need(act, s.ct_turned, b + 1)
                act.activation(CT[:, b, :], one[b], ACT.Copy).then_inc(s.ct_kept, 1)
            for k, var in enumerate((two, one)):
                for b in range(CHUNKS):
                    ln_square(act, s, ln[b], CHUNKS * k + b)
                for b in range(CHUNKS):
                    ln_root(act, s, ln[b], CHUNKS * k + b, var[b], c.eps5[:, 0:1])

        @block.vector
        def _(dve):
            dve.wait_ge(d.w, 80)
            dve.tensor_tensor(SIW[:, :], SI[:, :], SW[:, :], ALU.mult)
            dve.reciprocal(RSI[:, :], SI[:, :]).then_inc(s.scale, 1)
            need(dve, s.scale, 1)
            need(dve, s.w_turned, 1)
            dve.tensor_copy(W8T[:, :], two[0][:, 0:P]).then_inc(s.w_kept, 1)
            for b in range(CHUNKS):
                need(dve, s.y_done, b + 1)
                dve.tensor_tensor(Y[:, b, :], two[b], xa(b), ALU.add).then_inc(s.summed, 1)
            for b in range(CHUNKS):
                ln_center(dve, s, ln[b], b, Y[:, b, :], one[b])
            for b in range(CHUNKS):
                xq = XQ[:, b, :]
                ln_scale(dve, s, ln[b], b, X1[:, b, :])
                need(dve, s.ln_done, b + 1)
                dve.tensor_scalar(xq, X1[:, b, :], RSI[:, 0:1], 448.0, ALU.mult, ALU.min).then_inc(s.clipped, 1)
                need(dve, s.clipped, b + 1)
                dve.tensor_scalar(xq, xq, -448.0, None, ALU.max).then_inc(s.low, 1)
                need(dve, s.low, b + 1)
                dve.tensor_scalar(UNIT[:, :].bitcast(U32), xq.bitcast(U32), 0x7F800000, None,
                                  ALU.bitwise_and).then_inc(s.bits, 1)
                need(dve, s.bits, b + 1)
                dve.tensor_scalar(UNIT[:, :], UNIT[:, :], 2.0 ** -6, 1.5 * 2.0 ** 20, ALU.max, ALU.mult).then_inc(s.unit, 1)
                need(dve, s.unit, b + 1)
                dve.tensor_tensor(xq, xq, UNIT[:, :], ALU.add).then_inc(s.magic, 1)
                need(dve, s.magic, b + 1)
                dve.tensor_tensor(xq, xq, UNIT[:, :], ALU.subtract).then_inc(s.rounded, 1)
            for b in range(CHUNKS):
                need(dve, s.o_done, b + 1)
                dve.tensor_scalar(Y[:, b, :], one[b], SIW[:, 0:1], BIAS[:, 0:1], ALU.mult, ALU.add).then_inc(s.o_kept, 1)
                need(dve, s.o_kept, b + 1)
                dve.tensor_tensor(Y[:, b, :], Y[:, b, :], X1[:, b, :], ALU.add).then_inc(s.o_summed, 1)
            for b in range(CHUNKS):
                ln_center(dve, s, ln[b], CHUNKS + b, Y[:, b, :], two[b])
            for b in range(CHUNKS):
                ln_scale(dve, s, ln[b], CHUNKS + b, xa(b))


AttentionBuffers = namedtuple("AttentionBuffers", "va ctx")


def attention_and_quant(nc, c, t, ahead=()):
    q_stack = nc.dram_tensor("q_stack", (AHEADS, USED, T), BF16, kind="Internal").ap()
    k_stack = nc.dram_tensor("k_stack", (AHEADS, USED, T), BF16, kind="Internal").ap()
    with ExitStack() as ctx:
        m = AttentionBuffers(va=ctx.enter_context(nc.sbuf_tensor("va", [P, TILES, AHEADS, VW], F32)),
                            ctx=ctx.enter_context(nc.sbuf_tensor("ctx", [P, TILES, P], F32)))
        project_phase(nc, c, m, t["L0_attn_W_DKV"], t["L0_attn_W_UK"], t["L0_attn_W_UV"], t["L0_attn_W_UQ"],
                      t["c_ones_rows"], q_stack, k_stack)
        causal_phase(nc, c, m, q_stack, k_stack, t["c_mask_qk"], t["c_mask_kq"], ahead)
        quant_phase(nc, c, m, t["L0_attn_W_O"], t["L0_ffn_weight_fp8"], t["L0_ffn_bias"], t["L0_ffn_input_scale"],
                    t["L0_ffn_weight_scale"])



DT_RANK = 64
STATES = 16
BC = 2 * STATES
UNITS_SSM = 2 * STATES
SSM_COUNTERS = ("affined proj pkept sig_e sig_d sig_r gate vproj vkept vabs vexp vlog soft dtproj dtkept dlproj "
                "bcproj bckept bc_hi bc_rest bc_mid bc_done dx uskip b_done c_done da_done dbu_done scanned carried "
                "hc_done y_acc y_gated total copied " + LN_NAMES)


def ssm_weights(nc, ctx, loaded, t):
    def sb(name, shape, dt=F32):
        return ctx.enter_context(nc.sbuf_tensor("sm_" + name, shape, dt))

    WP = sb("WP", [P, P])
    WU = sb("WU", [P, 2, P])
    WX = sb("WX", [P, 2, DT_RANK])
    WBC = sb("WBC", [P, 2, 3 * BC])
    WDT = sb("WDT", [DT_RANK, 2, P])
    VEC = sb("VEC", [P, 9])
    BX = sb("BX", [DT_RANK, 2])
    BBC = sb("BBC", [3 * BC, 2])
    AL = sb("AL", [P, 2, STATES])
    SEL = sb("SEL", [3 * BC, BC, P], BF16)
    col = lambda a: a.rearrange("(p a) -> p a", a=1)
    loads = [(WP[:, :], t["W_proj"]), (VEC[:, 0:1], col(t["gamma"])), (VEC[:, 1:2], col(t["beta"])),
             (VEC[:, 2:3], col(t["b_proj"])), (SEL[:, :, :], t["c_select"])]
    for k, (wu, bu) in enumerate((("W_fc", "b_fc"), ("W_bc", "b_bc"))):
        i = str(k + 1)
        loads += [(WU[:, k, :], t[wu]), (VEC[:, 3 + 3 * k:4 + 3 * k], col(t[bu])),
                  (VEC[:, 4 + 3 * k:5 + 3 * k], col(t["b_dt" + i])), (VEC[:, 5 + 3 * k:6 + 3 * k], col(t["D" + i])),
                  (WX[:, k, :], t["W_x" + i][:, 0:DT_RANK]), (WDT[:, k, :], t["W_dt" + i]),
                  (BX[:, k:k + 1], col(t["b_x" + i][0:DT_RANK])), (AL[:, k, :], t["A_log" + i])]
        for r in range(3):
            loads += [(WBC[:, k, BC * r:BC * (r + 1)], t["W_x" + i][:, DT_RANK:DT_RANK + BC]),
                      (BBC[BC * r:BC * (r + 1), k:k + 1], col(t["b_x" + i][DT_RANK:DT_RANK + BC]))]
    return Early((WP, WU, WX, WBC, WDT, VEC, BX, BBC, AL, SEL), loads, loaded)


def ssm_phase(nc, c, x3, w):
    with ExitStack() as ctx:
        def sb(name, shape, dt=F32):
            return ctx.enter_context(nc.sbuf_tensor("sm_" + name, shape, dt))

        WP, WU, WX, WBC, WDT, VEC, BX, BBC, AL, SEL = w.tensors
        XN = sb("XN", [P, CH])
        PJ = sb("PJ", [P, CH])
        SG = sb("SG", [P, CH])
        Z = sb("Z", [P, CH])
        VB = sb("VB", [P, 2, CH])
        VA = sb("VA", [P, 2, CH])
        VL = sb("VL", [P, 2, CH])
        U = sb("U", [P, 2, CH])
        DT = sb("DT", [DT_RANK, 2, CH])
        DL = sb("DL", [P, 2, CH])
        DX = sb("DX", [P, 2, CH])
        BCF = sb("BCF", [3 * BC, 2, CH])
        BCR = sb("BCR", [3 * BC, 2, CH])
        BCM = sb("BCM", [3 * BC, 2, CH], BF16)
        BCS = sb("BCS", [3 * BC, 2, CH], BF16)
        ACC = sb("ACC", [P, CH])
        Y = sb("Y", [P, CH])
        DA = sb("DA", [P, 2, CH])
        DBU = sb("DBU", [P, 2, CH])
        HS = sb("HS", [P, 2, CH])
        HL = sb("HL", [P, UNITS_SSM])
        HC = sb("HC", [P, 2, CH])
        s = Counters(nc, ctx, "sm_", SSM_COUNTERS)
        f = Counters(nc, ctx, "smf_", LN_NAMES)
        start_counters(nc, [*s, *f])
        first = LnBuffers(c.avg, *[sb("first_" + n, [P, CH]) for n in LnBuffers._fields[1:]])
        d = Counters(nc, ctx, "smd_", "alog a")
        B_BANK, C_BANK = (0, 1, 4), (2, 3, 7)
        mean, var = c.ps[:, 5, :], c.ps[:, 6, :]
        pre = (c.ps[:, 4, :], c.ps[:, 7, :])
        block = ctx.enter_context(nc.Block())

        @block.gpsimd
        def _(pool):
            pool.memset(HL[:, :], 0.0).then_inc(d.a, 1)
            with pool.Fori(0, CHUNKS) as b:
                for i in range(UNITS_SSM):
                    need(pool, s.hc_done, b * UNITS_SSM + i + 1)
                    if i == 0:
                        need(pool, s.uskip, b * 2 + 2)
                        need(pool, s.y_gated, b)
                    need(pool, s.y_acc, b * UNITS_SSM + i)
                    pool.tensor_tensor(Y[:, :], (ACC if i == 0 else Y)[:, :], HC[:, i % 2, :], ALU.add).then_inc(s.y_acc, 1)
                need(pool, s.ln_done, b + 1)
                pool.tensor_copy(x3[:, bass.ds(b * CH, CH)], c.xa[:, bass.ds(b * CH + 1, CH)]).then_inc(s.copied, 1)

        @block.tensor
        def _(pe):
            pe.wait_ge(w.loaded, 16 * len(w.loads))

            def spread(b, i):
                k, n, g = i // STATES, i % STATES, b * UNITS_SSM + i
                if i == 2:
                    need(pe, s.vkept, b * 2 + 2)
                need(pe, s.dbu_done, g - 2)
                pe.matmul(c.ps[:, B_BANK[i % 3], :], SEL[:, n, :], BCS[:, k, :], start=True, stop=True).then_inc(s.b_done, 1)
                need(pe, s.hc_done, g - 2)
                pe.matmul(c.ps[:, C_BANK[i % 3], :], SEL[:, STATES + n, :], BCS[:, k, :], start=True, stop=True).then_inc(s.c_done, 1)

            ln_pe(pe, f, first, 0, c.xa[:, 1:1 + CH], mean, var)
            with pe.Fori(0, CHUNKS) as b:
                need(pe, s.affined, b + 1)
                pe.matmul(pre[0], WP[:, :], XN[:, :], start=True, stop=True).then_inc(s.proj, 1)
                need(pe, s.pkept, b + 1)
                for k in range(2):
                    pe.matmul(pre[k], WU[:, k, :], PJ[:, :], start=True, stop=True).then_inc(s.vproj, 1)
                need(pe, s.soft, b * 2 + 1)
                for k, bank in enumerate((mean, var)):
                    pe.matmul(pre[k][0:DT_RANK, :], WX[:, k, :], U[:, k, :], start=True, stop=True).then_inc(s.dtproj, 1)
                    pe.matmul(bank[0:3 * BC, :], WBC[:, k, :], U[:, k, :], start=True, stop=True).then_inc(s.bcproj, 1)
                for k in range(2):
                    need(pe, s.dtkept, b * 2 + k + 1)
                    pe.matmul(pre[k], WDT[:, k, :], DT[:, k, :], start=True, stop=True).then_inc(s.dlproj, 1)
                need(pe, s.bc_done, b + 1)
                for i in range(UNITS_SSM):
                    if i == UNITS_SSM - 6:
                        ln_mean(pe, f, first, b + 1, c.xa[:, bass.ds((b + 1) % CHUNKS * CH + 1, CH)], mean)
                    spread(b, i)
                ln_var(pe, f, first, b + 1, var)
                need(pe, f.ln_sd, b + 2)
                need(pe, s.total, b + 1)
                ln_pe(pe, s, c, b, ACC[:, :], mean, var)

        @block.scalar
        def _(act):
            act.wait_ge(w.loaded, 16 * len(w.loads))
            act.wait_ge(d.a, 1)
            act.activation(AL[:, :, :], AL[:, :, :], ACT.Exp).then_inc(d.alog, 1)
            act.wait_ge(d.alog, 1)
            act.activation(AL[:, :, :], AL[:, :, :], ACT.Copy, scale=-1.0).then_inc(d.alog, 1)
            act.wait_ge(d.alog, 2)

            ln_act(act, f, first, 0, var, c.eps6[:, 0:1])
            with act.Fori(0, CHUNKS) as b:
                need(act, s.proj, b + 1)
                act.activation(PJ[:, :], pre[0], ACT.Identity, bias=VEC[:, 2:3]).then_inc(s.pkept, 1)
                need(act, s.pkept, b + 1)
                act.activation(SG[:, :], PJ[:, :], ACT.Exp, scale=-1.0).then_inc(s.sig_e, 1)
                for i, (ready, bias) in enumerate(((s.vproj, 3), (s.dlproj, 4))):
                    g = b * 2 + i
                    need(act, s.soft, g)
                    for k in range(2):
                        need(act, ready, b * 2 + k + 1)
                        mm = act.activation(VB[:, k, :], pre[k], ACT.Identity, bias=VEC[:, bias + 3 * k:bias + 3 * k + 1])
                    mm.then_inc(s.vkept, 1)
                    need(act, s.vkept, g + 1)
                    act.activation(VA[:, :, :], VB[:, :, :], ACT.Abs).then_inc(s.vabs, 1)
                    need(act, s.vabs, g + 1)
                    act.activation(VL[:, :, :], VA[:, :, :], ACT.Exp, scale=-1.0).then_inc(s.vexp, 1)
                    need(act, s.vexp, g + 1)
                    act.activation(VL[:, :, :], VL[:, :, :], ACT.Ln, bias=1.0).then_inc(s.vlog, 1)
                    if i == 0:
                        for k in range(2):
                            need(act, s.dtproj, b * 2 + k + 1)
                            act.activation(DT[:, k, :], pre[k][0:DT_RANK, :], ACT.Identity, bias=BX[:, k:k + 1]).then_inc(s.dtkept, 1)
                        need(act, s.bc_done, b)
                        for k, bank in enumerate((mean, var)):
                            need(act, s.bcproj, b * 2 + k + 1)
                            mm = act.activation(BCF[:, k, :], bank[0:3 * BC, :], ACT.Identity, bias=BBC[:, k:k + 1])
                        mm.then_inc(s.bckept, 1)
                need(act, s.soft, b * 2 + 2)
                for i in range(UNITS_SSM):
                    k, n, g = i // STATES, i % STATES, b * UNITS_SSM + i
                    need(act, s.scanned, g - 1)
                    act.activation(DA[:, i % 2, :], DL[:, k, :], ACT.Exp, scale=AL[:, k, n:n + 1]).then_inc(s.da_done, 1)
                ln_act(act, f, first, b + 1, var, c.eps6[:, 0:1])
                ln_act(act, s, c, b, var, c.eps5[:, 0:1])

        @block.vector
        def _(dve):
            dve.wait_ge(w.loaded, 16 * len(w.loads))
            dve.wait_ge(d.a, 1)

            def times_b(b, i):
                g = b * UNITS_SSM + i
                need(dve, s.b_done, g + 1)
                need(dve, s.scanned, g - 1)
                dve.tensor_tensor(DBU[:, i % 2, :], c.ps[:, B_BANK[i % 3], :], DX[:, i // STATES, :], ALU.mult).then_inc(s.dbu_done, 1)

            def scan(b, i):
                g = b * UNITS_SSM + i
                need(dve, s.carried, g - 1)
                need(dve, s.hc_done, g - 1)
                need(dve, s.dbu_done, g + 1)
                need(dve, s.da_done, g + 1)
                dve.tensor_tensor_scan(HS[:, i % 2, :], DA[:, i % 2, :], DBU[:, i % 2, :], HL[:, i:i + 1],
                                       ALU.mult, ALU.add).then_inc(s.scanned, 1)

            def times_c(b, i):
                g = b * UNITS_SSM + i
                need(dve, s.scanned, g + 1)
                dve.tensor_copy(HL[:, i:i + 1], HS[:, i % 2, CH - 1:CH]).then_inc(s.carried, 1)
                need(dve, s.c_done, g + 1)
                need(dve, s.y_acc, g - 1)
                dve.tensor_tensor(HC[:, i % 2, :], c.ps[:, C_BANK[i % 3], :], HS[:, i % 2, :], ALU.mult).then_inc(s.hc_done, 1)

            def normalized(k):
                ln_scale(dve, f, first, k, XN[:, :])
                need(dve, f.ln_done, k + 1)
                dve.tensor_scalar(XN[:, :], XN[:, :], VEC[:, 0:1], VEC[:, 1:2], ALU.mult, ALU.add).then_inc(s.affined, 1)

            ln_center(dve, f, first, 0, c.xa[:, 1:1 + CH], mean)
            normalized(0)
            with dve.Fori(0, CHUNKS) as b:
                x = c.xa[:, bass.ds(b * CH + 1, CH)]
                need(dve, s.vlog, b * 2 + 1)
                dve.scalar_tensor_tensor(U[:, :, :], VB[:, :, :], 0.0, VL[:, :, :], ALU.max, ALU.add).then_inc(s.soft, 1)
                need(dve, s.sig_e, b + 1)
                dve.tensor_scalar(SG[:, :], SG[:, :], 1.0, None, ALU.add).then_inc(s.sig_d, 1)
                need(dve, s.sig_d, b + 1)
                dve.reciprocal(SG[:, :], SG[:, :]).then_inc(s.sig_r, 1)
                need(dve, s.sig_r, b + 1)
                dve.tensor_tensor(Z[:, :], SG[:, :], PJ[:, :], ALU.mult).then_inc(s.gate, 1)
                need(dve, s.bckept, b + 1)
                dve.tensor_copy(BCS[:, :, :], BCF[:, :, :]).then_inc(s.bc_hi, 1)
                need(dve, s.bc_hi, b + 1)
                for i in (1, 2):
                    rows = slice(BC * i, BC * (i + 1))
                    mm = dve.tensor_tensor(BCR[rows, :, :], BCF[rows, :, :], BCS[rows, :, :], ALU.subtract)
                mm.then_inc(s.bc_rest, 1)
                need(dve, s.bc_rest, b + 1)
                dve.tensor_copy(BCS[BC:2 * BC, :, :], BCR[BC:2 * BC, :, :])
                dve.tensor_copy(BCM[2 * BC:3 * BC, :, :], BCR[2 * BC:3 * BC, :, :]).then_inc(s.bc_mid, 1)
                need(dve, s.bc_mid, b + 1)
                dve.tensor_tensor(BCS[2 * BC:3 * BC, :, :], BCR[2 * BC:3 * BC, :, :], BCM[2 * BC:3 * BC, :, :],
                                  ALU.subtract).then_inc(s.bc_done, 1)
                need(dve, s.vlog, b * 2 + 2)
                dve.scalar_tensor_tensor(DL[:, :, :], VB[:, :, :], 0.0, VL[:, :, :], ALU.max, ALU.add).then_inc(s.soft, 1)
                need(dve, s.soft, b * 2 + 2)
                dve.tensor_tensor(DX[:, :, :], DL[:, :, :], U[:, :, :], ALU.mult).then_inc(s.dx, 1)
                need(dve, s.dx, b + 1)
                dve.tensor_scalar(ACC[:, :], U[:, 0, :], VEC[:, 5:6], None, ALU.mult).then_inc(s.uskip, 1)
                need(dve, s.uskip, b * 2 + 1)
                dve.scalar_tensor_tensor(ACC[:, :], U[:, 1, :], VEC[:, 8:9], ACC[:, :], ALU.mult, ALU.add).then_inc(s.uskip, 1)
                for i in range(UNITS_SSM + 2):
                    if i < UNITS_SSM:
                        times_b(b, i)
                    if 1 <= i <= UNITS_SSM:
                        scan(b, i - 1)
                    if i >= 2:
                        times_c(b, i - 2)
                    if i == UNITS_SSM - 4:
                        ln_center(dve, f, first, b + 1, c.xa[:, bass.ds((b + 1) % CHUNKS * CH + 1, CH)], mean)
                need(dve, s.y_acc, b * UNITS_SSM + UNITS_SSM)
                dve.tensor_tensor(ACC[:, :], Y[:, :], Z[:, :], ALU.mult).then_inc(s.y_gated, 1)
                need(dve, s.y_gated, b + 1)
                dve.scalar_tensor_tensor(ACC[:, :], x, 2.0, ACC[:, :], ALU.mult, ALU.add).then_inc(s.total, 1)
                need(dve, s.total, b + 1)
                ln_center(dve, s, c, b, ACC[:, :], mean)
                normalized(b + 1)
                ln_scale(dve, s, c, b, x)



LAYERS = 6
HEADS = 16
DH = 64
INNER = HEADS * DH
WIN = 32
KEYS = P + WIN
GROUPS = 4
GH = HEADS // GROUPS
GD = GH * DH
HID = 341
HPART = [(0, 128), (128, 128), (256, HID - 256)]
AHEAD = 4

SHIFT, MEAN, VAR, SPREAD, GATE, VAL, DOWN = 0, 2, 3, 4, (5, 6, 7), (9, 10, 11), 12
PIECES = 13

LOCAL_COUNTERS = ("xs_staged tab_ready qk_done v_done squared v_kept summed roped clamped norm_a "
                  "k_scaled rotated kprev turned qk_kept scored maxed biased exped prev_turned p_turned pt_kept "
                  "attended recipd weighted o_kept projected resid shifted affined gelud gate "
                  "val vprev_kept gated down ffn_done gate_kept ln_mean ln_centered ln_squared ln_var "
                  "ln_eps ln_rstd scaled ln_diag ln_spread ln_done")


def local_tables(nc, ctx, loaded, rope, mask, kfac):
    def sb(name, shape, dt=F32):
        return ctx.enter_context(nc.sbuf_tensor("lo_" + name, shape, dt))

    ROPE = sb("ROPE", [P, TILES, 4 * DH])
    MASK = sb("MASK", [P, TILES + 1, KEYS], BF16)
    KFAC = sb("KFAC", [P, 1])
    return Early((ROPE, MASK, KFAC), [(ROPE[:, :, :], rope), (MASK[:, :, :], mask), (KFAC[:, :], kfac)], loaded)


def local_phase(nc, c, wqkv, q_scale, k_scale, wo, ln_g, ln_b, w1, b1, w2, b2, tables):
    with ExitStack() as ctx:
        def sb(name, shape, dt=F32):
            return ctx.enter_context(nc.sbuf_tensor("lo_" + name, shape, dt))

        W = sb("W", [P, GROUPS, 3 * GD])
        WO = sb("WO", [P, INNER // P, P])
        W1 = sb("W1", [P, 2 * HID])
        W2 = sb("W2", [P, 3, P])
        B1 = sb("B1", [P, 2, 3])
        VEC = sb("VEC", [P, 3])
        QS = sb("QS", [P, 4 * DH])
        TAB = sb("TAB", [P, 4 * DH])
        ROPE, MASK, KFAC = tables.tensors
        XS = sb("XS", [P, 2, P])
        SQ = sb("SQ", [P, 2, 2 * GD])
        SS = sb("SS", [P, 2, 2 * GH])
        SSM = sb("SSM", [P, 2, 2 * GH])
        MHALF = sb("MHALF", [P, 1])
        A = sb("A", [P, GROUPS, 2 * GH])
        TB = sb("TB", [P, 2, 2 * GD])
        RB = sb("RB", [P, 2, 2 * GD])
        QT = sb("QT", [P, 2, 2, P])
        KT = sb("KT", [P, GROUPS, 2, KEYS])
        V = sb("V", [P, GROUPS, GD])
        VP = sb("VP", [WIN, GROUPS, GD])
        NM = sb("NM", [P, 2, GH])
        NB = sb("NB", [P, 2, GH])
        PR = sb("PR", [P, 2, GH, KEYS])
        RS = sb("RS", [P, 2, GH])
        RI = sb("RI", [P, GH])
        PP = sb("PP", [WIN, 2, GH * WIN])
        PTS = sb("PTS", [P, 2, GH * P])
        OTS = sb("OTS", [P, INNER // P, P])
        XS2 = sb("XS2", [P, CH])
        XN = sb("XN", [P, CH])
        VE = sb("VE", [P, 4])
        RV = sb("RV", [P, 4])
        DIAG = sb("DIAG", [P, 4, P])
        ONES = sb("ONES", [P, P])
        GT = sb("GT", [P, 3, CH])
        H = sb("H", [P, 3, CH])

        s = Counters(nc, ctx, "lo_", LOCAL_COUNTERS)
        start_counters(nc, s)
        d = Counters(nc, ctx, "lod_", "w0 w1 w2 w3 wo ffn vec qs")
        slices = (d.w0, d.w1, d.w2, d.w3)
        N_FFN = 6 + 6

        QK_B, T_B, PT_B, O_B = 0, 1, 6, 7

        def s_bank(par):
            return c.ps[:, 2 + 2 * par:4 + 2 * par, 0:2 * KEYS].rearrange("p h (b k) -> p b h k", b=2)

        y_bank = c.ps[:, T_B, 0:P]
        ot_bank = c.ps[:, O_B, 0:GD].rearrange("p (b t) -> p b t", b=2)
        v_bank = c.ps[:, T_B, P:P + GD]
        pt_bank = c.ps[:, PT_B, :]
        f_bank = c.ps[:, PT_B, :]

        def chunks(eng, chunk):
            load = 16 * N_FFN
            chunk(0, 0, None)
            with eng.Fori(1, CHUNKS) as ch:
                chunk(0, ch, (ch - 1, ch - 1, load))
            with eng.Fori(1, LAYERS) as l:
                chunk(l, 0, (l * CHUNKS - 1, CHUNKS - 1, l * load))
                with eng.Fori(1, CHUNKS) as ch:
                    chunk(l, ch, (l * CHUNKS + ch - 1, ch - 1, l * load + load))

        LAST = (LAYERS * CHUNKS - 1, CHUNKS - 1, LAYERS * 16 * N_FFN)

        block = ctx.enter_context(nc.Block())

        @block.sync
        def _(sp):
            def layer(l, first):
                for part, src in enumerate((q_scale, k_scale)):
                    row = src[bass.ds(l, 1), :]
                    if part == 0 and not first:
                        need(sp, s.tab_ready, 16 * l)
                    sp.dma_start(QS[:, part * DH:(part + 1) * DH], row.broadcast_to([P, DH])).then_inc(d.qs, 16)
                    for h in range(2):
                        o = (2 + part) * DH + h * (DH // 2)
                        sp.dma_start(QS[:, o:o + DH // 2],
                                     src[bass.ds(l, 1), (1 - h) * (DH // 2):(2 - h) * (DH // 2)]
                                     .broadcast_to([P, DH // 2])).then_inc(d.qs, 16)
                for g in range(GROUPS):
                    if not first:
                        need(sp, s.v_done, 64 * l - 3 + g)
                    src = wqkv[bass.ds(l, 1), :, :].rearrange("a p (b n) -> p (a b) n", b=3)
                    sp.dma_start(W[:, g, :].rearrange("p (b n) -> p b n", b=3),
                                 src[:, :, GD * g:GD * (g + 1)]).then_inc(slices[g], 16)
                if not first:
                    need(sp, s.projected, 16 * l)
                sp.dma_start(WO[:, :, :], wo[bass.ds(l, 1), :, :].rearrange("a (k p) n -> p (a k) n", p=P)).then_inc(d.wo, 16)
                if not first:
                    need(sp, s.ffn_done, 4 * l)
                sp.dma_start(W1[:, :], w1[bass.ds(l, 1), :, :].rearrange("a p n -> (a p) n")).then_inc(d.ffn, 16)
                sp.dma_start(W2[:, 0:2, :], w2[bass.ds(l, 1), 0:256, :].rearrange("a (k p) n -> p (a k) n", p=P)).then_inc(d.ffn, 16)
                sp.dma_start(W2[0:HID - 256, 2, :], w2[bass.ds(l, 1), 256:HID, :].rearrange("a p n -> (a p) n")).then_inc(d.ffn, 16)
                for i, src in enumerate((ln_g, ln_b, b2)):
                    sp.dma_start(VEC[:, i:i + 1], src[bass.ds(l, 1), :].rearrange("a p -> p a")).then_inc(d.ffn, 16)
                for half in range(2):
                    for j, (h0, w) in enumerate(HPART):
                        sp.dma_start(B1[0:w, half, j:j + 1],
                                     b1[bass.ds(l, 1), half * HID + h0:half * HID + h0 + w].rearrange("a p -> p a")).then_inc(d.ffn, 16)

            layer(0, True)
            with sp.Fori(1, LAYERS) as l:
                layer(l, False)
            for w in slices:
                sp.wait_ge(w, 16 * LAYERS)
                sp.sem_inc(w, 16)

        @block.gpsimd
        def _(pool):
            pool.memset(MHALF[:, :], -0.5)
            pool.memset(ONES[:, :], 1.0)
            pool.memset(VP[:, :, :], 0.0)
            pool.memset(KT[:, :, :, :], 0.0).then_inc(d.vec, 1)
            pool.wait_ge(tables.loaded, 48)
            pool.wait_ge(d.vec, 1)

            def piece(p, ffn):
                k, fch, load = ffn
                if p == SHIFT:
                    need(pool, s.resid, k * 4 + 4)
                    need(pool, s.ln_centered, k)
                    for rows, first in ((slice(0, 64), 1), (slice(64, P), 0)):
                        m = pool.tensor_tensor(XS2[rows, :], c.xb[rows, bass.ds(fch * CH + first, CH)],
                                               ONES[rows, 0:1].to_broadcast([64, CH]), ALU.mult)
                    m.then_inc(s.shifted, 1)
                    need(pool, s.shifted, k + 1)
                if p == VAR:
                    need(pool, s.ln_eps, k + 1)
                    pool.tensor_tensor(RV[:, :], VE[:, :], MHALF[:, 0:1].to_broadcast([P, 4]), ALU.pow).then_inc(s.ln_rstd, 1)
                    need(pool, s.ln_rstd, k + 1)
                    need(pool, s.ln_spread, k)
                    pool.tensor_tensor(DIAG[:, :, :], c.ident[:, :].unsqueeze(1).to_broadcast([P, 4, P]),
                                       RV[:, :].unsqueeze(2).to_broadcast([P, 4, P]), ALU.mult).then_inc(s.ln_diag, 1)
                if p == SPREAD:
                    pool.wait_ge(d.ffn, load)
                    need(pool, s.ln_done, k + 1)
                    pool.tensor_tensor(XN[:, :], XN[:, :], VEC[:, 0:1].to_broadcast([P, CH]), ALU.mult).then_inc(s.scaled, 1)
                    need(pool, s.scaled, k + 1)
                    pool.tensor_tensor(XN[:, :], XN[:, :], VEC[:, 1:2].to_broadcast([P, CH]), ALU.add).then_inc(s.affined, 1)

            def stage(n, t, slot, chunk_count, scaled):
                need(pool, s.v_done, n * 4 - 4)
                need(pool, s.ffn_done, chunk_count - 3)
                need(pool, s.k_scaled, scaled)
                for rows, first in ((slice(0, 64), 1), (slice(64, P), 0)):
                    m = pool.tensor_tensor(XS[rows, slot, :], c.xa[rows, bass.ds(t * P + first, P)],
                                           ONES[rows, 0:1].to_broadcast([64, P]), ALU.mult)
                m.then_inc(s.xs_staged, 1)
                need(pool, s.xs_staged, n + 1)

            def tile(l, ch, j, ffn=None, beyond=False):
                n = (l * CHUNKS + ch) * 4 + j
                t = ch * 4 + j
                if not beyond:
                    pool.wait_ge(d.qs, l * 96 + 96)
                need(pool, s.roped, n * 4)
                pool.tensor_tensor(TAB[:, :], ROPE[:, bass.ds(t, 1), :].rearrange("p a b -> p (a b)"),
                                   QS[:, :], ALU.mult).then_inc(s.tab_ready, 1)
                for g in range(GROUPS):
                    G, par = n * 4 + g, g % 2
                    need(pool, s.scored, G - 3)
                    pool.tensor_tensor(KT[:, g, :, 0:WIN], KT[:, g, :, P:KEYS],
                                       KFAC[:, :].unsqueeze(2).to_broadcast([P, 2, WIN]), ALU.mult).then_inc(s.kprev, 1)
                    need(pool, s.clamped, G + 1)
                    need(pool, s.exped, G - 3)
                    pool.tensor_tensor(A[:, g, :], SSM[:, par, :], MHALF[:, 0:1].to_broadcast([P, 2 * GH]),
                                       ALU.pow).then_inc(s.norm_a, 1)
                    need(pool, s.roped, G + 1)
                    pool.tensor_tensor(TB[:, par, :], TB[:, par, :], RB[:, par, :], ALU.add).then_inc(s.rotated, 1)
                    need(pool, s.norm_a, G + 1)
                    need(pool, s.rotated, G + 1)
                    a_k = A[:, g, GH:2 * GH].unsqueeze(2).to_broadcast([P, GH, DH])
                    k = TB[:, par, GD:2 * GD].rearrange("p (h e) -> p h e", h=GH)
                    pool.tensor_tensor(k, k, a_k, ALU.mult).then_inc(s.k_scaled, 1)
                    if ffn is not None:
                        p = 4 * (j - 1) + g
                        if p == SHIFT:
                            need(pool, s.k_scaled, G + 1)
                        piece(p, ffn)
                    if g == 2 and not beyond:
                        stage(n + 1, (t + 1) % TILES, (j + 1) % 2, l * CHUNKS + ch + (j + 1) // 4, G + 1)

            def chunk(l, ch, ffn):
                for j in range(4):
                    tile(l, ch, j, ffn)

            stage(0, 0, 0, 0, 0)
            chunks(pool, chunk)
            tile(LAYERS, 0, 0, beyond=True)
            need(pool, s.k_scaled, (LAYERS * TILES + 1) * GROUPS)
            for p in range(PIECES):
                piece(p, LAST)

        @block.tensor
        def _(pe):
            pe.wait_ge(tables.loaded, 48)
            pe.wait_ge(d.vec, 1)

            def proj_v(G, slot, g):
                need(pe, s.v_kept, G)
                need(pe, s.qk_kept, G)
                pe.matmul(v_bank, XS[:, slot, :], W[:, g, 2 * GD:3 * GD], start=True, stop=True).then_inc(s.v_done, 1)

            def proj_qk(G, n, slot, g, layer):
                if layer is not None:
                    pe.wait_ge(slices[g], layer * 16 + 16)
                need(pe, s.xs_staged, n + 1)
                need(pe, s.roped, G)
                pe.matmul(c.ps[:, QK_B, :], XS[:, slot, :], W[:, g, 0:2 * GD], start=True, stop=True).then_inc(s.qk_done, 1)

            def turn(G, n, par):
                need(pe, s.k_scaled, G + 1)
                need(pe, s.resid, n)
                need(pe, s.v_kept, G + 1)
                need(pe, s.qk_kept, G)
                for b in range(4):
                    m = pe.transpose(c.ps[:, T_B, b * P:(b + 1) * P], TB[:, par, b * P:(b + 1) * P], c.ident[:, :])
                m.then_inc(s.turned, 1)

            def masks(G, t, par):
                need(pe, s.exped, G - 1)
                for h in range(2):
                    for b in range(2):
                        pe.matmul(s_bank(par)[:, b, h, :], c.ident_bf[:, :],
                                  MASK[:, bass.ds(t, 1), :].rearrange("p a k -> p (a k)"),
                                  start=(b == 0), stop=False, skip_group_check=True)

            def score(G, g, par):
                need(pe, s.qk_kept, G + 1)
                for b in range(2):
                    for h in range(2):
                        m = pe.matmul(s_bank(par)[:, b, h, :], QT[64 * h:64 * h + 64, par, b, :],
                                      KT[64 * h:64 * h + 64, g, b, :], start=False, stop=(b == 1),
                                      skip_group_check=True)
                m.then_inc(s.scored, 1)

            def pturn(G, par, p, ffn):
                need(pe, s.weighted, G + 1)
                need(pe, s.pt_kept, G)
                if ffn is not None:
                    piece_left(p - 1, ffn)
                for h in range(GH):
                    m = pe.transpose(pt_bank[:, h * P:(h + 1) * P], PR[:, par, h, WIN:KEYS], c.ident[:, :])
                m.then_inc(s.p_turned, 1)

            def attend(G, g, par):
                need(pe, s.pt_kept, G + 1)
                need(pe, s.prev_turned, G + 1)
                need(pe, s.v_kept, G + 1)
                need(pe, s.o_kept, G)
                need(pe, s.vprev_kept, G - 3)
                for b in range(2):
                    for h in range(2):
                        i = 2 * b + h
                        pe.matmul(ot_bank[64 * h:64 * h + 64, b, :], V[:, g, i * DH:(i + 1) * DH],
                                  PTS[:, par, i * P:(i + 1) * P], start=(b == 0), stop=False, skip_group_check=True)
                for b in range(2):
                    for h in range(2):
                        i = 2 * b + h
                        m = pe.matmul(ot_bank[64 * h:64 * h + 64, b, 0:WIN], VP[:, g, i * DH:(i + 1) * DH],
                                      PP[:, par, i * WIN:(i + 1) * WIN], start=False, stop=(b == 1),
                                      skip_group_check=True)
                m.then_inc(s.attended, 1)

            def project(n, l):
                need(pe, s.o_kept, 4 * n + 4)
                pe.wait_ge(d.wo, 16 * l + 16)
                for k in range(INNER // P):
                    m = pe.matmul(y_bank, WO[:, k, :], OTS[:, k, :], start=(k == 0), stop=(k == INNER // P - 1))
                m.then_inc(s.projected, 1)

            def piece_left(p, ffn):
                k = ffn[0]
                if p == MEAN:
                    need(pe, s.ln_centered, k + 1)
                if p == VAR:
                    need(pe, s.ln_eps, k + 1)
                if p == SPREAD:
                    need(pe, s.ln_done, k + 1)
                if p in GATE:
                    need(pe, s.gate_kept, k * 3 + (GATE.index(p) + 1))
                if p in VAL:
                    need(pe, s.gated, k * 3 + (VAL.index(p) + 1))
                if p == DOWN:
                    need(pe, s.ffn_done, k + 1)

            def piece(p, ffn):
                k, fch, load = ffn
                piece_left(p - 1, ffn)
                if p == MEAN:
                    need(pe, s.shifted, k + 1)
                    pe.matmul(f_bank, c.avg[:, :], XS2[:, :], start=True, stop=True).then_inc(s.ln_mean, 1)
                if p == VAR:
                    need(pe, s.ln_squared, k + 1)
                    for i in range(4):
                        m = pe.matmul(f_bank[:, i:i + 1], c.ln_sq[:, i * P:(i + 1) * P], c.avg[:, 0:1],
                                      start=i == 0, stop=True, skip_group_check=True)
                    m.then_inc(s.ln_var, 1)
                if p == SPREAD:
                    need(pe, s.ln_diag, k + 1)
                    pe.matmul(f_bank, ONES[:, :], DIAG[:, :, :].rearrange("p a b -> p (a b)"),
                              start=True, stop=True).then_inc(s.ln_spread, 1)
                if p in GATE:
                    h0, w = HPART[GATE.index(p)]
                    if p == GATE[0]:
                        pe.wait_ge(d.ffn, load)
                        need(pe, s.affined, k + 1)
                    pe.matmul(f_bank[0:w, :], W1[:, HID + h0:HID + h0 + w], XN[:, :], start=True, stop=True).then_inc(s.gate, 1)
                if p in VAL:
                    h0, w = HPART[VAL.index(p)]
                    pe.matmul(f_bank[0:w, :], W1[:, h0:h0 + w], XN[:, :], start=True, stop=True).then_inc(s.val, 1)
                if p == DOWN:
                    for j, (h0, w) in enumerate(HPART):
                        m = pe.matmul(f_bank, W2[0:w, j, :], H[0:w, j, :], start=(j == 0), stop=(j == 2))
                    m.then_inc(s.down, 1)

            def step(n, t, g, l, slot, layer=None, p=None, ffn=None, first=False):
                G = n * 4 + g
                proj_qk(G + AHEAD, n + 1, slot, g, layer)
                if not first:
                    pturn(G, g % 2, p, ffn)
                if not first or g >= 2:
                    masks(G + 2, t + (g + 2) // 4, g % 2)
                    score(G + 2, (g + 2) % 4, g % 2)
                if not first:
                    attend(G, g, g % 2)
                if not first or g >= 1:
                    turn(G + 3, n, (g + 3) % 2)
                if ffn is not None and p < PIECES:
                    piece(p, ffn)
                proj_v(G + AHEAD, slot, g)
                if not first and g == GROUPS - 1:
                    project(n, l)

            def chunk(l, ch, ffn):
                for j in range(4):
                    for g in range(GROUPS):
                        step((l * CHUNKS + ch) * 4 + j, ch * 4 + j, g, l, (j + 1) % 2,
                             (l * CHUNKS + ch + 1) // CHUNKS if j == 3 else None, 4 * j + g, ffn)

            for g in range(GROUPS):
                step(-1, -1, g, 0, 0, 0, first=True)
            chunks(pe, chunk)
            for p in range(PIECES):
                piece(p, LAST)

        @block.scalar
        def _(act):
            def square(G, par):
                need(act, s.qk_done, G + 1)
                need(act, s.summed, G - 1)
                act.activation(SQ[:, par, :], c.ps[:, QK_B, :], ACT.Square).then_inc(s.squared, 1)

            def keep(G, g, par):
                need(act, s.turned, G + 1)
                need(act, s.scored, G - 1)
                need(act, s.kprev, G + 1)
                act.activation(QT[:, par, :, :], c.ps[:, T_B, 0:GD].rearrange("p (b t) -> p b t", b=2), ACT.Copy)
                act.activation(KT[:, g, :, WIN:KEYS], c.ps[:, T_B, GD:2 * GD].rearrange("p (b t) -> p b t", b=2),
                               ACT.Copy).then_inc(s.qk_kept, 1)

            def exps(G, g, par):
                need(act, s.biased, G + 1)
                need(act, s.p_turned, G - 1)
                need(act, s.prev_turned, G - 1)
                need(act, s.recipd, G - 1)
                for h in range(GH):
                    m = act.activation(PR[:, par, h, :], s_bank(par)[:, h // 2, h % 2, :], ACT.Exp,
                                       bias=NB[:, par, h:h + 1], scale=A[:, g, h:h + 1],
                                       accum_out=RS[:, par, h:h + 1])
                m.then_inc(s.exped, 1)

            def pt_keep(G, par):
                need(act, s.p_turned, G + 1)
                need(act, s.attended, G - 1)
                act.activation(PTS[:, par, :], pt_bank, ACT.Copy).then_inc(s.pt_kept, 1)

            def piece(p, ffn):
                k, fch, load = ffn
                if p == MEAN:
                    need(act, s.ln_centered, k + 1)
                    need(act, s.ln_var, k)
                    act.activation(c.ln_sq[:, :], c.ln_cen[:, :], ACT.Square).then_inc(s.ln_squared, 1)
                if p in GATE:
                    j = GATE.index(p)
                    w = HPART[j][1]
                    if j == 0:
                        act.wait_ge(d.ffn, load)
                        need(act, s.gated, k * 3)
                    need(act, s.gate, k * 3 + (j + 1))
                    act.activation(GT[0:w, j, :], f_bank[0:w, :], ACT.Identity, bias=B1[0:w, 1, j:j + 1]).then_inc(s.gate_kept, 1)
                if p == GATE[-1]:
                    need(act, s.gate_kept, k * 3 + 3)
                    act.activation(GT[:, 0:2, :], GT[:, 0:2, :], ACT.Gelu)
                    act.activation(GT[0:w, 2, :], GT[0:w, 2, :], ACT.Gelu).then_inc(s.gelud, 1)

            def step(n, g, p=None, ffn=None, first=False):
                G = n * 4 + g
                square(G + AHEAD, g % 2)
                if not first:
                    pt_keep(G, g % 2)
                if not first or g == 3:
                    exps(G + 1, (g + 1) % 4, (g + 1) % 2)
                if not first or g >= 1:
                    keep(G + 3, (g + 3) % 4, (g + 3) % 2)
                if ffn is not None and p < PIECES:
                    piece(p, ffn)

            def chunk(l, ch, ffn):
                for j in range(4):
                    for g in range(GROUPS):
                        step((l * CHUNKS + ch) * 4 + j, g, 4 * j + g, ffn)

            for g in range(GROUPS):
                step(-1, g, first=True)
            chunks(act, chunk)
            for p in range(PIECES):
                piece(p, LAST)

        @block.vector
        def _(dve):
            def rope_qk(G, n, par):
                need(dve, s.squared, G + 1)
                need(dve, s.tab_ready, n + 1)
                need(dve, s.turned, G - 1)
                tab = TAB[:, :].rearrange("p (c q e) -> p c q e", c=2, q=2)
                qk = c.ps[:, QK_B, :].rearrange("p (q h e) -> p q h e", q=2, h=GH)
                dve.tensor_tensor(TB[:, par, :].rearrange("p (q h e) -> p q h e", q=2, h=GH), qk,
                                  tab[:, 0, :, :].unsqueeze(2).to_broadcast([P, 2, GH, DH]), ALU.mult)
                for q in range(2):
                    src = c.ps[:, QK_B, q * GD:(q + 1) * GD].rearrange("p (h a e) -> p h a e", h=GH, a=2)[:, :, ::-1, :]
                    dst = RB[:, par, q * GD:(q + 1) * GD].rearrange("p (h a e) -> p h a e", h=GH, a=2)
                    sin = tab[:, 1, q, :].rearrange("p (a e) -> p a e", a=2).unsqueeze(1).to_broadcast([P, GH, 2, DH // 2])
                    m = dve.tensor_tensor(dst, src, sin, ALU.mult)
                m.then_inc(s.roped, 1)

            def sums(G, par):
                need(dve, s.squared, G + 1)
                dve.tensor_reduce(SS[:, par, :], SQ[:, par, :].rearrange("p (h e) -> p h e", e=DH), AX.X,
                                  ALU.add).then_inc(s.summed, 1)
                need(dve, s.norm_a, G - 1)
                need(dve, s.summed, G + 1)
                dve.tensor_scalar(SSM[:, par, :], SS[:, par, :], 1e-24, None, ALU.max).then_inc(s.clamped, 1)

            def v_keep(G, n, g, first):
                need(dve, s.v_done, G + 1)
                if not first and g == GROUPS - 1:
                    need(dve, s.projected, n + 1)
                if not first:
                    need(dve, s.attended, G - 3)
                    dve.tensor_copy(VP[:, g, :], V[P - WIN:P, g, :]).then_inc(s.vprev_kept, 1)
                    need(dve, s.vprev_kept, G - 3)
                dve.tensor_copy(V[:, g, :], v_bank).then_inc(s.v_kept, 1)

            def prev_turn(G, par):
                need(dve, s.weighted, G + 1)
                need(dve, s.attended, G - 1)
                dve.transpose(PP[:, par, :].rearrange("p (h k) -> p h k", h=GH), PR[0:WIN, par, :, 0:WIN]).then_inc(s.prev_turned, 1)

            def recip(G, par):
                need(dve, s.exped, G + 1)
                dve.reciprocal(RI[:, :], RS[:, par, :]).then_inc(s.recipd, 1)

            def weight(G, par):
                need(dve, s.recipd, G + 1)
                dve.tensor_tensor(PR[:, par, :, :], PR[:, par, :, :],
                                  RI[:, :].unsqueeze(2).to_broadcast([P, GH, KEYS]), ALU.mult).then_inc(s.weighted, 1)

            def o_keep(G, n, g):
                need(dve, s.attended, G + 1)
                need(dve, s.projected, n)
                dve.tensor_copy(OTS[:, 2 * g:2 * g + 2, :], ot_bank).then_inc(s.o_kept, 1)

            def maxes(G, g, par):
                need(dve, s.scored, G + 1)
                dve.tensor_reduce(NM[:, par, :].rearrange("p (b h) -> p b h", b=2), s_bank(par), AX.X, ALU.max,
                                  negate=True).then_inc(s.maxed, 1)
                need(dve, s.maxed, G + 1)
                need(dve, s.norm_a, G + 1)
                need(dve, s.exped, G - 1)
                dve.tensor_tensor(NB[:, par, :], NM[:, par, :], A[:, g, 0:GH], ALU.mult).then_inc(s.biased, 1)

            def residual(n, t):
                need(dve, s.projected, n + 1)
                dve.tensor_tensor(c.xb[:, bass.ds(t * P + 1, P)], y_bank, c.xa[:, bass.ds(t * P + 1, P)],
                                  ALU.add).then_inc(s.resid, 1)

            def piece(p, ffn):
                k, fch, load = ffn
                if p == MEAN:
                    need(dve, s.ln_mean, k + 1)
                    need(dve, s.ln_squared, k)
                    dve.tensor_tensor(c.ln_cen[:, :], XS2[:, :], f_bank, ALU.subtract).then_inc(s.ln_centered, 1)
                if p == VAR:
                    need(dve, s.ln_var, k + 1)
                    need(dve, s.ln_rstd, k)
                    dve.tensor_scalar(VE[:, :], f_bank[:, 0:4], 1e-5, None, ALU.add).then_inc(s.ln_eps, 1)
                if p == SPREAD:
                    need(dve, s.ln_spread, k + 1)
                    need(dve, s.val, k * 3)
                    dve.tensor_tensor(XN[:, :], c.ln_cen[:, :], f_bank, ALU.mult).then_inc(s.ln_done, 1)
                if p in VAL:
                    j = VAL.index(p)
                    w = HPART[j][1]
                    if j == 0:
                        dve.wait_ge(d.ffn, load)
                        need(dve, s.gelud, k + 1)
                        need(dve, s.down, k)
                    need(dve, s.val, k * 3 + (j + 1))
                    dve.scalar_tensor_tensor(H[0:w, j, :], f_bank[0:w, :], B1[0:w, 0, j:j + 1], GT[0:w, j, :],
                                             ALU.add, ALU.mult).then_inc(s.gated, 1)
                if p == DOWN:
                    need(dve, s.down, k + 1)
                    need(dve, s.xs_staged, k * 4 + 5)
                    dve.scalar_tensor_tensor(c.xa[:, bass.ds(fch * CH + 1, CH)], f_bank, VEC[:, 2:3],
                                             c.xb[:, bass.ds(fch * CH + 1, CH)], ALU.add, ALU.add).then_inc(s.ffn_done, 1)

            def step(n, t, g, p=None, ffn=None, first=False):
                G = n * 4 + g
                sums(G + AHEAD, g % 2)
                rope_qk(G + AHEAD, n + 1, g % 2)
                if not first or g >= 2:
                    maxes(G + 2, (g + 2) % 4, g % 2)
                if not first:
                    o_keep(G, n, g)
                if not first or g == GROUPS - 1:
                    recip(G + 1, (g + 1) % 2)
                    weight(G + 1, (g + 1) % 2)
                    prev_turn(G + 1, (g + 1) % 2)
                if ffn is not None and p < PIECES:
                    piece(p, ffn)
                v_keep(G + AHEAD, n, g, first)
                if not first and g == GROUPS - 1:
                    residual(n, t)

            def chunk(l, ch, ffn):
                for j in range(4):
                    for g in range(GROUPS):
                        step((l * CHUNKS + ch) * 4 + j, ch * 4 + j, g, 4 * j + g, ffn)

            for g in range(GROUPS):
                step(-1, -1, g, first=True)
            chunks(dve, chunk)
            for p in range(PIECES):
                piece(p, LAST)


def store_phase(nc, c, x3, out):
    with ExitStack() as ctx:
        s = Counters(nc, ctx, "st_", LN_NAMES + " summed turned kept stored")
        y_tok = ctx.enter_context(nc.sbuf_tensor("y_tok", [P, TILES, P], F32))
        start_counters(nc, [s.ln_mean, s.ln_centered, s.ln_squared, s.ln_var, s.ln_sd, s.ln_rstd, s.ln_done])
        ln = ln_buffers(nc, ctx, c, "st_ln_")
        block = ctx.enter_context(nc.Block())

        def x(b):
            return c.xb[:, 1 + CH * b:1 + CH * (b + 1)]

        def y(b):
            return c.xa[:, 1 + CH * b:1 + CH * (b + 1)]

        @block.tensor
        def _(pe):
            for b in range(CHUNKS):
                pe.wait_ge(s.summed, b + 1)
                ln_mean(pe, s, ln[b], b, x(b), c.ps[:, b, :])
            for b in range(CHUNKS):
                ln_var(pe, s, ln[b], b, c.ps[:, 4 + b, :])
            for b in range(CHUNKS):
                need(pe, s.ln_done, b + 1)
                for t in range(4):
                    m = pe.transpose(c.ps[:, b, t * P:(t + 1) * P],
                                     c.xa[:, 1 + CH * b + P * t:1 + CH * b + P * (t + 1)], c.ident[:, :])
                m.then_inc(s.turned, 1)

        @block.scalar
        def _(act):
            for b in range(CHUNKS):
                ln_square(act, s, ln[b], b)
            for b in range(CHUNKS):
                ln_root(act, s, ln[b], b, c.ps[:, 4 + b, :], c.eps5[:, 0:1])

        @block.vector
        def _(dve):
            for b in range(CHUNKS):
                dve.tensor_tensor(x(b), x3[:, CH * b:CH * (b + 1)], y(b), ALU.add).then_inc(s.summed, 1)
            dve.wait_ge(s.summed, CHUNKS)
            for b in range(CHUNKS):
                ln_center(dve, s, ln[b], b, x(b), c.ps[:, b, :])
            for b in range(CHUNKS + 1):
                if b < CHUNKS:
                    ln_scale(dve, s, ln[b], b, y(b))
                if b >= 1:
                    dve.wait_ge(s.turned, b)
                    dve.tensor_copy(y_tok[:, 4 * b - 4:4 * b, :],
                                    c.ps[:, b - 1, :].rearrange("p (t f) -> p t f", t=4)).then_inc(s.kept, 1)

        @block.sync
        def _(sp):
            for b in range(CHUNKS):
                sp.wait_ge(s.kept, b + 1)
                sp.dma_start(out[0, CH * b:CH * (b + 1), :].rearrange("(t p) f -> p t f", p=P),
                             y_tok[:, 4 * b:4 * b + 4, :]).then_inc(s.stored, 16)
            sp.wait_ge(s.stored, 16 * CHUNKS)


def program(nc, t, out):
    with ExitStack() as ctx:
        c = Common(nc, ctx)
        loaded = Counters(nc, ctx, "early_", "ssm local")
        weights = ssm_weights(nc, ctx, loaded.ssm, {n.removeprefix("L1_attn_"): a for n, a in t.items()})
        tables = local_tables(nc, ctx, loaded.local, t["c_rope"], t["c_mask"], t["c_kfac"])
        load_phase(nc, c, t["L0_attn_x"], t["c_ident"])
        attention_and_quant(nc, c, t, (weights, tables))
        x3 = ctx.enter_context(nc.sbuf_tensor("x3", [P, T], F32))
        ssm_phase(nc, c, x3, weights)
        local_phase(nc, c, *[t["L1_ffn_" + n] for n in ("Wqkv", "q_scale", "k_scale", "Wo", "ln_g", "ln_b", "W1", "b1", "W2", "b2")],
                    tables)
        store_phase(nc, c, x3, out)



def constants():
    import numpy as np
    bf16 = mybir.dt.np(BF16)
    f32 = np.float32
    half = np.arange(0, DH, 2, dtype=f32)
    inv_freq = (f32(1.0) / f32(10000.0) ** (half / f32(DH))).astype(f32)
    freqs = np.arange(T, dtype=f32)[:, None] * inv_freq[None, :]
    cos, sin = np.cos(freqs).astype(f32), np.sin(freqs).astype(f32)
    base = ((half + 0.4 * DH) / (1.4 * DH)).astype(np.float64)
    power = (np.arange(T) % P - P // 2) / (WIN // 2)
    scale = base[None, :] ** power[:, None]
    both = lambda a: np.concatenate([a, a], -1)
    sign = np.concatenate([-np.ones(DH // 2), np.ones(DH // 2)])[None, :]
    parts = [both(cos * scale) * 8.0, both(cos / scale), both(sin * scale) * sign * 8.0, both(sin / scale) * sign]
    rope = np.stack(parts, 1).astype(f32).reshape(TILES, P, 4 * DH).transpose(1, 0, 2)
    q = np.arange(P)[:, None]
    k = np.arange(KEYS)[None, :] - WIN
    seen = (k <= q) & (k >= q - WIN)
    mask = np.repeat(np.where(seen, 0.0, -1e30)[:, None, :], TILES + 1, 1)
    mask[:, [0, TILES], 0:WIN] = -1e30
    return {
        "c_ident": np.eye(P, dtype=f32),
        "c_rope": np.ascontiguousarray(rope),
        "c_mask": mask.astype(bf16),
        "c_select": np.ascontiguousarray(np.broadcast_to(
            (np.arange(3 * BC)[:, None] % BC == np.arange(BC)[None, :])[:, :, None], (3 * BC, BC, P))).astype(bf16),
        "c_ones_rows": (np.arange(P) % MROWS < 3).astype(f32)[:, None],
        "c_mask_qk": np.where(np.arange(P)[None, :] > q, -1e30, 0.0).astype(bf16),
        "c_mask_kq": np.where(q > np.arange(P)[None, :], -1e30, 0.0).astype(bf16),
        "c_kfac": np.tile(both(base ** (P // (WIN // 2))), 2).astype(f32)[:, None],
    }


def kernel(**inputs):
    import numpy as _np
    import concourse.bacc as _bacc
    from concourse import mybir as _mybir
    from concourse.bass_utils import run_bass_kernel_spmd as _run

    nc = _bacc.Bacc("TRN2", target_bir_lowering=False, num_devices=1)
    arrays = {"in_" + n: _np.ascontiguousarray(a) for n, a in inputs.items()}
    arrays.update(constants())
    tensors = {n.removeprefix("in_"): nc.dram_tensor(n, a.shape, _mybir.dt.from_np(a.dtype), kind="ExternalInput").ap()
               for n, a in arrays.items()}
    out = nc.dram_tensor("out_0_dram", (1, T, P), F32, kind="ExternalOutput").ap()
    program(nc, tensors, out)
    r = _run(nc, [arrays], core_ids=[0])
    return r.results[0]["out_0_dram"]
```
